# Optimizing a Trainium2 kernel written in Bass

```python
import numpy as np
import jax
import jax.numpy as jnp

def _softmax(x, axis=-1):
    return jax.nn.softmax(x, axis=axis)
def _gelu(x):
    return jax.nn.gelu(x, approximate=True)
def _silu(x):
    return jax.nn.silu(x)
def _sigmoid(x):
    return jax.nn.sigmoid(x)
def _layernorm(x, axis=-1, eps=1e-5):
    m = jnp.mean(x, axis=axis, keepdims=True)
    v = jnp.var(x, axis=axis, keepdims=True)
    return (x - m) / jnp.sqrt(v + eps)
def _scatter_add(tgt, idx, src, axis=0):
    return tgt.at[idx].add(src)
def _segment_sum(src, seg, n):
    return jax.ops.segment_sum(src, seg, n)

kernel_name = 'mk_conv_seq_d2_conv_nchw256_f684d4'

def setup_inputs(seed: int = 0):
    np.random.seed(seed)
    _w = jnp.asarray
    def _rec_inputs():
        import jax
        import jax.numpy as jnp
        _gk = jax.random.key(seed)
        x = -7.109e-05 + 0.9999 * jax.random.normal(jax.random.fold_in(_gk, 1), (4, 256, 256, 256), jnp.float32)
        return x
    x = _rec_inputs()
    def _L0_conv_setup():
        import jax, jax.numpy as jnp
        import numpy as np
        EPS = 1e-08
        N_ANGLES = 8
        RADIUS_WIDTH = 8
        HIGH_FREQ_RATIO = 0.8
        OVERLAP_RATIO = 1.5
        WEIGHT_RANGE = 0.5
        key = jax.random.key(seed)
        k1, k2, k3, k4 = jax.random.split(key, 4)
        B, C, H, W = (4, 256, 256, 256)
        c_mid = 16
        n_radii = int(max(H // 2, W // 2) // RADIUS_WIDTH) + 1
        x = jax.random.normal(k1, (B, C, H, W), dtype=jnp.float32)
        w_in = jax.random.normal(k2, (c_mid, C), dtype=jnp.float32) * 0.05
        w_out = jax.random.normal(k3, (C, c_mid), dtype=jnp.float32) * 0.05
        weights = jax.random.normal(k4, (c_mid, N_ANGLES, n_radii), dtype=jnp.float32) * 0.5
        return {'x': x, 'w_in': w_in, 'w_out': w_out, 'weights': weights}
    _L0_conv_all = _L0_conv_setup()
    _L0_conv_in = {k: v for k, v in _L0_conv_all.items() if k in ('w_in', 'w_out', 'weights', )}
    del _L0_conv_all

    def _L1_conv_setup():
        import jax, jax.numpy as jnp
        from jax import lax
        import numpy as np
        DIM = 256
        INNER = 128
        DS = 2
        K = 3
        EPS = 1e-05

        def _sss(seq, wd, bd, wv, bv):
            delta = jax.nn.sigmoid(jnp.einsum('nlc,dc->nld', seq, wd) + bd)
            value = jnp.einsum('nlc,dc->nld', seq, wv) + bv
            init = jnp.zeros((seq.shape[0], seq.shape[2]), seq.dtype)

            def step(state, dv):
                d, v = dv
                s = (1.0 - d) * state + d * v
                return (s, s)
            _, ys = lax.scan(step, init, (jnp.moveaxis(delta, 1, 0), jnp.moveaxis(value, 1, 0)))
            return jnp.moveaxis(ys, 0, 1)

        def _bidir(seq, wd, bd, wv, bv):
            fwd = _sss(seq, wd, bd, wv, bv)
            bwd = jnp.flip(_sss(jnp.flip(seq, axis=1), wd, bd, wv, bv), axis=1)
            return 0.5 * (fwd + bwd)
        key = jax.random.key(seed)
        ks = jax.random.split(key, 16)
        s = lambda *sh: 0.05
        inp = {'x': jax.random.normal(ks[0], (4, DIM, 200, 200), jnp.float32), 'gn_w': jnp.ones((DIM,), jnp.float32), 'gn_b': jnp.zeros((DIM,), jnp.float32), 'w_in': jax.random.normal(ks[1], (2 * INNER, DIM), jnp.float32) * 0.05, 'w_dw': jax.random.normal(ks[2], (INNER, 1, K, K), jnp.float32) * 0.1, 'row_wd': jax.random.normal(ks[3], (INNER, INNER), jnp.float32) * 0.05, 'row_bd': jax.random.normal(ks[4], (INNER,), jnp.float32) * 0.05, 'row_wv': jax.random.normal(ks[5], (INNER, INNER), jnp.float32) * 0.05, 'row_bv': jax.random.normal(ks[6], (INNER,), jnp.float32) * 0.05, 'col_wd': jax.random.normal(ks[7], (INNER, INNER), jnp.float32) * 0.05, 'col_bd': jax.random.normal(ks[8], (INNER,), jnp.float32) * 0.05, 'col_wv': jax.random.normal(ks[9], (INNER, INNER), jnp.float32) * 0.05, 'col_bv': jax.random.normal(ks[10], (INNER,), jnp.float32) * 0.05, 'w_out': jax.random.normal(ks[11], (DIM, INNER), jnp.float32) * 0.05}
        return inp
    _L1_conv_all = _L1_conv_setup()
    _L1_conv_in = {k: v for k, v in _L1_conv_all.items() if k in ('gn_w', 'gn_b', 'w_in', 'w_dw', 'row_wd', 'row_bd', 'row_wv', 'row_bv', 'col_wd', 'col_bd', 'col_wv', 'col_bv', 'w_out', )}
    del _L1_conv_all

    return {
        "x": x,
        "L0_conv_w_in": _L0_conv_in["w_in"],
        "L0_conv_w_out": _L0_conv_in["w_out"],
        "L0_conv_weights": _L0_conv_in["weights"],
        "L1_conv_gn_w": _L1_conv_in["gn_w"],
        "L1_conv_gn_b": _L1_conv_in["gn_b"],
        "L1_conv_w_in": _L1_conv_in["w_in"],
        "L1_conv_w_dw": _L1_conv_in["w_dw"],
        "L1_conv_row_wd": _L1_conv_in["row_wd"],
        "L1_conv_row_bd": _L1_conv_in["row_bd"],
        "L1_conv_row_wv": _L1_conv_in["row_wv"],
        "L1_conv_row_bv": _L1_conv_in["row_bv"],
        "L1_conv_col_wd": _L1_conv_in["col_wd"],
        "L1_conv_col_bd": _L1_conv_in["col_bd"],
        "L1_conv_col_wv": _L1_conv_in["col_wv"],
        "L1_conv_col_bv": _L1_conv_in["col_bv"],
        "L1_conv_w_out": _L1_conv_in["w_out"],
    }

def reference(x, L0_conv_w_in, L0_conv_w_out, L0_conv_weights, L1_conv_gn_w, L1_conv_gn_b, L1_conv_w_in, L1_conv_w_dw, L1_conv_row_wd, L1_conv_row_bd, L1_conv_row_wv, L1_conv_row_bv, L1_conv_col_wd, L1_conv_col_bd, L1_conv_col_wv, L1_conv_col_bv, L1_conv_w_out):
    import jax
    import jax.numpy as jnp
    def _L0_conv_ref(x, w_in, w_out, weights):
        import jax, jax.numpy as jnp
        import numpy as np
        EPS = 1e-08
        N_ANGLES = 8
        RADIUS_WIDTH = 8
        HIGH_FREQ_RATIO = 0.8
        OVERLAP_RATIO = 1.5
        WEIGHT_RANGE = 0.5
        B, C, H, W = x.shape
        xp = jnp.einsum('bchw,mc->bmhw', x, w_in)
        fs = jnp.fft.fftshift(jnp.fft.fft2(xp, norm='ortho'), axes=(-2, -1))
        mag = jnp.abs(fs) + EPS
        cy, cx = (H // 2, W // 2)
        yy = jnp.arange(H, dtype=jnp.float32)[:, None]
        xx = jnp.arange(W, dtype=jnp.float32)[None, :]
        r = jnp.sqrt((yy - cy) ** 2 + (xx - cx) ** 2)
        theta = (jnp.arctan2(yy - cy, xx - cx) + np.pi) % np.pi
        max_r = max(cy, cx)
        n_radii = int(max_r // RADIUS_WIDTH) + 1
        ridx = jnp.clip(jnp.floor(r / RADIUS_WIDTH).astype(jnp.int32), 0, n_radii - 1)
        delta = np.pi / N_ANGLES
        half_width = OVERLAP_RATIO * delta / 2.0
        centers = (jnp.arange(N_ANGLES, dtype=jnp.float32) * delta + delta / 2.0)[:, None, None]
        dist = jnp.abs(theta[None] - centers)
        aw = jnp.where(dist < half_width, jnp.clip(1.0 - dist / half_width, 0.0, None), 0.0)
        aw = aw / (aw.sum(axis=0, keepdims=True) + EPS)
        w_map = weights[:, :, ridx]
        gain = jnp.einsum('ahw,cahw->chw', aw, w_map)
        gain = 1.0 + WEIGHT_RANGE * jnp.tanh(gain)
        hf = r > HIGH_FREQ_RATIO * max_r
        gain = jnp.where(hf[None], gain, 1.0)
        enh = mag * gain[None] * jnp.exp(1j * jnp.angle(fs))
        x_enh = jnp.fft.ifft2(jnp.fft.ifftshift(enh, axes=(-2, -1)), norm='ortho').real
        out = jnp.einsum('bmhw,cm->bchw', x_enh, w_out)
        return x + out

    def _L1_conv_ref(x, gn_w, gn_b, w_in, w_dw, row_wd, row_bd, row_wv, row_bv, col_wd, col_bd, col_wv, col_bv, w_out):
        import jax, jax.numpy as jnp
        from jax import lax
        import numpy as np
        DIM = 256
        INNER = 128
        DS = 2
        K = 3
        EPS = 1e-05

        def _sss(seq, wd, bd, wv, bv):
            delta = jax.nn.sigmoid(jnp.einsum('nlc,dc->nld', seq, wd) + bd)
            value = jnp.einsum('nlc,dc->nld', seq, wv) + bv
            init = jnp.zeros((seq.shape[0], seq.shape[2]), seq.dtype)

            def step(state, dv):
                d, v = dv
                s = (1.0 - d) * state + d * v
                return (s, s)
            _, ys = lax.scan(step, init, (jnp.moveaxis(delta, 1, 0), jnp.moveaxis(value, 1, 0)))
            return jnp.moveaxis(ys, 0, 1)

        def _bidir(seq, wd, bd, wv, bv):
            fwd = _sss(seq, wd, bd, wv, bv)
            bwd = jnp.flip(_sss(jnp.flip(seq, axis=1), wd, bd, wv, bv), axis=1)
            return 0.5 * (fwd + bwd)
        B, C, H, W = x.shape
        residual = x
        mu = jnp.mean(x, axis=(1, 2, 3), keepdims=True)
        var = jnp.var(x, axis=(1, 2, 3), keepdims=True)
        y = (x - mu) * lax.rsqrt(var + EPS)
        y = y * gn_w[None, :, None, None] + gn_b[None, :, None, None]
        h, w = (H // DS, W // DS)
        y = y.reshape(B, C, h, DS, w, DS).mean(axis=(3, 5))
        y = jnp.einsum('oc,bchw->bohw', w_in, y)
        y, gate = (y[:, :INNER], y[:, INNER:])
        y = lax.conv_general_dilated(y, w_dw, (1, 1), 'SAME', feature_group_count=INNER, dimension_numbers=('NCHW', 'OIHW', 'NCHW'))
        y = jax.nn.silu(y)
        seq_r = y.transpose(0, 2, 3, 1).reshape(B * h, w, INNER)
        rows = _bidir(seq_r, row_wd, row_bd, row_wv, row_bv)
        rows = rows.reshape(B, h, w, INNER).transpose(0, 3, 1, 2)
        seq_c = y.transpose(0, 3, 2, 1).reshape(B * w, h, INNER)
        cols = _bidir(seq_c, col_wd, col_bd, col_wv, col_bv)
        cols = cols.reshape(B, w, h, INNER).transpose(0, 3, 2, 1)
        y = 0.5 * (rows + cols)
        y = y * jax.nn.sigmoid(gate)
        y = jnp.einsum('oc,bchw->bohw', w_out, y)
        y = jax.image.resize(y, (B, C, H, W), method='bilinear')
        return residual + y

    def _gn(v, G=32, eps=1e-5):
        B_, C_, H_, W_ = v.shape
        g = v.reshape(B_, G, C_ // G, H_, W_)
        m = jnp.mean(g, axis=(2, 3, 4), keepdims=True)
        s = jnp.var(g, axis=(2, 3, 4), keepdims=True)
        return ((g - m) / jnp.sqrt(s + eps)).reshape(v.shape)

    def _ln_c(v, eps=1e-6):
        m = jnp.mean(v, axis=1, keepdims=True)
        s = jnp.var(v, axis=1, keepdims=True)
        return (v - m) / jnp.sqrt(s + eps)

    def _ln_t(v, eps=1e-5):
        m = jnp.mean(v, axis=-1, keepdims=True)
        s = jnp.var(v, axis=-1, keepdims=True)
        return (v - m) / jnp.sqrt(s + eps)

    def _to_tokens(v):
        B_, C_, H_, W_ = v.shape
        return v.reshape(B_, C_, H_ * W_).transpose(0, 2, 1)
    def _from_tokens(t, like):
        B_, C_, H_, W_ = like.shape
        return t.transpose(0, 2, 1).reshape(B_, C_, H_, W_)

    x = _L0_conv_ref(x, L0_conv_w_in, L0_conv_w_out, L0_conv_weights)
    x = _L1_conv_ref(x, L1_conv_gn_w, L1_conv_gn_b, L1_conv_w_in, L1_conv_w_dw, L1_conv_row_wd, L1_conv_row_bd, L1_conv_row_wv, L1_conv_row_bv, L1_conv_col_wd, L1_conv_col_bd, L1_conv_col_wv, L1_conv_col_bv, L1_conv_w_out)
    return x


_drawn_inputs = setup_inputs


def setup_inputs(seed=0):
    import zlib

    import numpy as np

    out = dict(_drawn_inputs(seed))
    spreads = {'L1_conv_gn_w': (1.0, 0.6), 'L1_conv_gn_b': (0.0, 0.8)}
    factors = {'L1_conv_w_in': 8.0,
     'L1_conv_w_dw': 8.0,
     'L1_conv_row_wd': 8.0,
     'L1_conv_row_bd': 38.425,
     'L1_conv_row_wv': 8.0,
     'L1_conv_row_bv': 60.817,
     'L1_conv_col_wd': 8.0,
     'L1_conv_col_bd': 39.047,
     'L1_conv_col_wv': 8.0,
     'L1_conv_col_bv': 57.88,
     'L1_conv_w_out': 5.164,
     'L0_conv_weights': 4.65}
    for name, (base, spread) in spreads.items():
        noise = np.random.default_rng([zlib.crc32(name.encode()), seed]).standard_normal(out[name].shape)
        drawn = base * np.exp(spread * noise) if base else spread * noise
        out[name] = jnp.asarray(drawn.astype(out[name].dtype))
    for name, factor in factors.items():
        out[name] = (out[name] * factor).astype(out[name].dtype)
    return out
```

```python
import numpy as np
import concourse.bass as bass
from concourse import mybir
from contextlib import ExitStack

F32 = mybir.dt.float32
BF16 = mybir.dt.bfloat16
ALU = mybir.AluOpType
ACT = mybir.ActivationFunctionType
AX = mybir.AxisListType

P = 128
SIDE = 256
PIX = SIDE * SIDE
LOW = SIDE // 2
LPIX = LOW * LOW
CM = 16
NA, NR = 8, 5
R0 = 12
NSLOT = 272
GA1, GB1, GA1B, GB1B, ROWB = 256, 257, 258, 259, 260
FEPS = 1e-8
TINY = 2.0 ** -100
DELTA = 2.0 ** -50
GN_EPS = 1e-5
LW = LOW + 2
YROWS = LOW + 3
LINE = LOW + 1
SCAN = 4 * LINE


def fourier_bases():
    n = np.arange(SIDE)
    k = np.arange(LOW)
    ang = 2 * np.pi * ((n[:, None] * k[None, :]) % SIDE) / SIDE
    fwd = np.zeros((SIDE, SIDE))
    fwd[:, :LOW] = np.cos(ang)
    fwd[:, LOW:] = np.sin(ang)
    fwd[:, LOW] = 1 - 2 * (n % 2)
    weight = np.full(SIDE, 2.0)
    weight[0] = weight[LOW] = 1.0
    return (fwd / 16).astype(np.float32), (fwd.T * weight[:, None] / 16).astype(np.float32)


def gain_basis():
    f = np.float32
    d = np.arange(-LOW, LOW).astype(f)
    yy, xx = d[:, None], d[None, :]
    r = np.sqrt(yy * yy + xx * xx).astype(f)
    theta = np.mod((np.arctan2(yy, xx).astype(f) + f(np.pi)).astype(f), f(np.pi)).astype(f)
    ridx = np.clip(np.floor(r / 8).astype(int), 0, 16)
    delta = np.pi / NA
    half = f(1.5 * delta / 2)
    centers = (np.arange(NA).astype(f) * f(delta) + f(delta / 2))[:, None, None]
    dist = np.abs(theta[None] - centers)
    aw = np.where(dist < half, np.clip(1 - dist / half, 0, None), 0).astype(f)
    aw = aw / (aw.sum(0, keepdims=True) + f(1e-8))
    aw = aw * (r > f(0.8 * LOW))[None]
    full = np.zeros((NA, NR, SIDE, SIDE), f)
    for j in range(NR):
        full[:, j] = aw * (ridx == R0 + j)[None]
    full = full.reshape(NA * NR, SIDE, SIDE)

    def at(ky, kx):
        return full[:, ky + LOW, kx + LOW]

    t = np.zeros((NA * NR, NSLOT, P), f)
    k = np.arange(P)
    for l in range(P):
        t[:, l] = at(k, np.full(P, l))
        t[:, P + l] = at(k, np.full(P, -l))
        t[:, P + l, 0] = full[:, 0, l + LOW]
        t[:, ROWB, l] = full[:, 0, LOW - l]
    for slot, sign in ((GA1, 1), (GB1, 1), (GA1B, -1), (GB1B, -1)):
        t[:, slot] = at(sign * k, np.full(P, -LOW))
    t[:, GB1, 0] = t[:, GB1B, 0] = full[:, 0, 0]
    return t


def columns():
    c = np.zeros((P, 16), np.float32)
    c[1:, 0] = 1
    c[:, 1] = -c[:, 0]
    c[:, 2] = np.where(c[:, 0] > 0, 0.5, 1.0)
    c[:, 3] = c[:, 2] / 2
    part = np.arange(P) // CM
    for j, rows in enumerate(((0, 1, 2), (3, 4), (5,))):
        c[:, 4 + j] = np.isin(part, rows)
    c[:, 8:10] = 1
    c[0, 8:12] = 1
    return c


def build(nc, B, x, out, t):
    ctx = ExitStack()
    with ctx:
        def sb(name, shape, dt=F32):
            return ctx.enter_context(nc.sbuf_tensor(name, shape, dt))

        def sem(name):
            return ctx.enter_context(nc.semaphore(name))

        def scratch(name, shape, dt=F32):
            return nc.dram_tensor(name, shape, dt, kind="Internal").ap()

        proj_d = scratch("proj_d", [B, 2 * CM, PIX])
        xe_d = scratch("xe_d", [B, CM, PIX])
        xs_d = scratch("xs_d", [B, 3, CM, PIX], BF16)
        gate_d = scratch("gate_d", [B, P, LPIX])
        pe_d = scratch("pe_d", [B, CM, LPIX])
        rowb_d = scratch("rowb_d", [P, CM])

        Y = sb("Y", [P, YROWS, LW])
        S = sb("S", [P, LPIX])
        X = sb("X", [P, 4, 2, 1024])
        Xf = X[:, :, :, :].rearrange("p s h n -> p (s h n)")
        gains = sb("gains", [P, CM, NSLOT])
        corner = sb("corner", [P, CM, 4])
        fwd = sb("fwd", [P, 2, SIDE])
        inv = sb("inv", [P, 2, SIDE])
        wproj = sb("wproj", [P, 2, 2 * CM])
        wpool = sb("wpool", [P, 2, SIDE])
        cmix = sb("cmix", [CM, SIDE])
        wscan = sb("wscan", [P, 4, P])
        wup = sb("wup", [P, SIDE])
        wstack = sb("wstack", [6 * CM, SIDE], BF16)
        gram = sb("gram", [P, P])
        ones = sb("ones", [P, P])
        taps = sb("taps", [P, 4, P])
        cols = sb("cols", [P, 16])
        vec = sb("vec", [P, 32])
        sums = sb("sums", [P, 224])
        stat = sb("stat", [P, 16])
        bank = ctx.enter_context(nc.psum_tensor("bank", [P, 8, 512], F32))

        kappa, negk, half_h, quart_h = (cols[:, i:i + 1] for i in range(4))
        gnw, gnb = vec[:, 0:2], vec[:, 2:4]
        bd, bv, nbd = [vec[:, 4:5], vec[:, 6:7]], [vec[:, 5:6], vec[:, 7:8]], [vec[:, 8:9], vec[:, 9:10]]
        dw = vec[:, 10:19]
        cw, cb = vec[:, 19:21], vec[:, 21:23]
        wsum = vec[:, 23:24]
        sum_x, sum_xx, cross, sum_xe = sums[:, 0:64], sums[:, 64:128], sums[:, 128:136], sums[:, 136:144]
        rs, cshift = stat[:, 8:9], stat[:, 9:11]
        TE_TAPS = [0, 1, 2, 3]
        VE_TAPS = [4, 5, 6, 7, 8]

        def sv(a, n):
            return S[:, a:a + n]

        vert = [sv(q * 1024, 1024) for q in range(2)]
        pooled = [sv(2048 + q * 1024, 1024).rearrange("p (h n) -> p h n", h=2) for q in range(2)]
        pstage = [sv(4096 + q * 512, 512) for q in range(2)]
        gstage = [sv(5120 + q * 512, 512) for q in range(2)]
        junk = sv(6144, 1024).bitcast(BF16)
        img = [sv(m * 512, 512).rearrange("p (t n) -> p t n", t=2) for m in range(8)]
        freq = S[:, 4096:8192].rearrange("p (m n) -> p m n", m=8)
        half1 = [sv(8192 + q * 512, 512).rearrange("p (t n) -> p t n", t=2) for q in range(2)]
        half2 = [sv(9216 + q * 512, 512).rearrange("p (t n) -> p t n", t=2) for q in range(2)]
        xe_s = [sv(10240 + q * 512, 512) for q in range(2)]
        parts = [sv(11264 + q * 768, 768).bitcast(BF16).rearrange("p (i n) -> p i n", i=3) for q in range(2)]
        rest = [sv(12800 + q * 512, 512) for q in range(2)]
        small = [sv(13824 + 16 * i, 16) for i in range(8)]
        tmp = [Xf[:, i * 512:(i + 1) * 512] for i in range(8)]
        xe_t = [sv(q * 1024, 1024) for q in range(2)]
        xq_t = [sv(2048 + q * 1024, 1024) for q in range(2)]
        mix = sv(4096, 1024)
        vsum = sv(5120, 512)
        pe_t = sv(6144, 2048)
        lx = [[Xf[:, q * 4096 + a:q * 4096 + a + n] for a, n in
               ((0, 512), (512, 512), (1024, SCAN + 1), (1544, SCAN + 1), (2064, SCAN + 1), (2584, SCAN + 1), (3104, 512), (3616, 480))]
              for q in range(2)]
        conv, sig, keep, take, fsc, bsc, lowload, _ = zip(*lx)

        def lines(a, first):
            if first:
                return a[:, 1:SCAN + 1].rearrange("p (r w) -> p r w", w=LINE)[:, :, 0:LOW]
            return a[:, 0:SCAN + 1:LINE]

        VW = 8 * LW
        vup = [sv(q * VW, VW).rearrange("p (i a w) -> p i a w", i=4, a=2) for q in range(2)]
        up = [sv(2 * VW + q * 2048, 2048) for q in range(2)]
        stack = [S[0:6 * CM, 2 * VW + 4096 + q * 1024:2 * VW + 4096 + (q + 1) * 1024].bitcast(BF16) for q in range(2)]

        names = """consts_in basis_in0 basis_in1 gain_ps gain_t rowb_out rowb_in ve_setup te_setup mv_setup
        x_in0 x_in1 x_in2 x_in3 x_out0 x_out1 x_out2 x_out3
        proj_ps lowp_ps pool_done square_done proj_st y_ev g_st proj_out0 proj_out1 gate_out0 gate_out1 ve_pool
        img_in0 img_in1 s1_ps s2_ps s3_ps s4_ps h1_st f_st h2_st xe_st parts_done xe_out0 xe_out1
        uv_ready sq_ready m_ready root_ready ew_done ve_ew pl_parts
        st_in0 st_in1 gram_ps st_done ve_stat pe_out tot_in tot_ps var_root norm_set
        pads_done pe_in0 pe_in1 corr_ps corr_add norm_done conv_ps conv_done sig_done s_ready z_ps gates_done
        scans_done merged ve_l1 pl_l1 gate_in0 gate_in1 gcorr_ps gcorr_add gsig_done gated edge_done
        up_rows up_ready up_ps added stack_in0 stack_in1 ve_up
        end_project end_fourier end_stats end_layer end_out held stores_set"""
        s = {n: sem(n) for n in names.split()}
        RING2 = "lowp_ps proj_ps proj_st y_ev g_st s1_ps s2_ps s3_ps s4_ps h1_st f_st h2_st xe_st parts_done st_done corr_add " \
                "conv_ps conv_done gates_done scans_done merged gcorr_add gcorr_ps corr_ps gsig_done gated up_ps up_ready pool_done square_done".split()

        def ready(n):
            return n + 3

        def freed(n):
            return n + 1

        class Steps:
            def __init__(self, eng, name, base):
                self.eng, self.name, self.base, self.n = eng, name, base, 0

            def done(self, ins):
                ins.then_inc(s[self.name], 1)
                self.n += 1

            def wait(self):
                self.eng.wait_ge(s[self.name], self.base + self.n)

        def credit(eng, *which):
            for n in which:
                assert n in RING2
                eng.sem_inc(s[n], 2)

        for_stores = ["x_out0", "x_out1", "x_out2", "x_out3", "proj_out0", "proj_out1", "gate_out0", "gate_out1", "xe_out0", "xe_out1"]

        def hold(eng):
            eng.sem_inc(s["held"], 1)

        def leave(eng, phase, b):
            eng.drain().then_inc(s[phase], 1)
            eng.wait_ge(s[phase], 4 * b + 4)
            hold(eng)

        block = ctx.enter_context(nc.Block())
        EW = 19

        @block.sync
        def _(sp):
            for n in for_stores:
                sp.sem_inc(s[n], 16)
            sp.sem_inc(s["stores_set"], 1)
            pairs = [(fwd[:, :, :], t["fwd"].rearrange("(t p) n -> p t n", p=P)),
                     (inv[:, :, :], t["inv"].rearrange("(t p) n -> p t n", p=P)),
                     (wproj[:, :, :], t["wproj"].rearrange("(t p) n -> p t n", p=P)),
                     (wpool[:, :, :], t["w_in1"].rearrange("(t p) n -> p t n", p=P)),
                     (wscan[:, :, :], t["wscan"].rearrange("(t p) n -> p t n", p=P)),
                     (wup[:, :], t["w_out1"]), (cols[:, :], t["cols"]), (vec[:, 0:19], t["vec"]),
                     (S[:, 0:256].rearrange("p (t n) -> p t n", t=2), t["wtile"].rearrange("(t p) n -> p t n", p=P)),
                     (S[0:6 * CM, 256:512], t["wrep"]), (S[:, 512:640], t["block"]), (S[:, 640:768], t["ident"]),
                     (S[0:NA * NR, 768:784], t["wgain"])]
            for dst, src in pairs:
                sp.dma_start(dst, src).then_inc(s["consts_in"], 16)
            with sp.Fori(0, (NSLOT // 16 - 1) // 2) as i:
                for q in range(2):
                    sp.wait_ge(s["gain_ps"], 2 * i + q + 1)
                    sp.dma_start(Y[0:NA * NR, q * 16:q * 16 + 16, 0:P], t["basis"][:, bass.ds(32 * i + 16 * q, 16), :])\
                      .then_inc(s[f"basis_in{q}"], 16)
            sp.wait_ge(s["gain_ps"], NSLOT // 16)
            sp.dma_start(Y[0:NA * NR, 0:16, 0:P], t["basis"][:, NSLOT - 16:NSLOT, :]).then_inc(s["basis_in0"], 16)
            sp.wait_ge(s["gain_t"], NSLOT // 16 + 1)
            sp.dma_start(rowb_d, gains[:, :, ROWB], allow_slow_non_contiguous=True).then_inc(s["rowb_out"], 16)
            sp.wait_ge(s["rowb_out"], 16)
            sp.dma_start(S[0:1, 1024:1024 + P * CM].rearrange("o (m l) -> o m l", l=P), rowb_d.rearrange("(o l) m -> o m l", o=1),
                         allow_slow_non_contiguous=True).then_inc(s["rowb_in"], 16)

            with sp.Fori(0, B) as b:
                for c in range(4):
                    sp.wait_ge(s[f"x_out{c}"], 256 * b + 16)
                hold(sp)
                def load_chunk(i, c):
                    n = b * 64 + i * 4 + c
                    sp.wait_ge(s["proj_ps"], b * 32 + i * 2 + c // 2 + 1)
                    hold(sp)
                    sp.wait_ge(s["pool_done"], n + 1)
                    sp.wait_ge(s["square_done"], n + 1)
                    hold(sp)
                    sp.dma_start(X[:, c, :, :], x[b, :, bass.ds(i * 4096 + c * 1024, 1024)].rearrange("(h p) n -> p h n", p=P))\
                      .then_inc(s[f"x_in{c}"], 16)

                def store_gate(i, q):
                    sp.wait_ge(s["g_st"], ready(b * 32 + 2 * i + q))
                    hold(sp)
                    sp.dma_start(gate_d[b, :, bass.ds(i * 1024 + q * 512, 512)], gstage[q]).then_inc(s[f"gate_out{q}"], 16)
                for c in range(4):
                    load_chunk(0, c)
                with sp.Fori(1, 16) as i:
                    for q in range(2):
                        load_chunk(i, 2 * q)
                        load_chunk(i, 2 * q + 1)
                        store_gate(i - 1, q)
                for q in range(2):
                    store_gate(15, q)
                for q in range(2):
                    sp.wait_ge(s[f"gate_out{q}"], 256 * b + 256 + 16)
                hold(sp)
                sp.wait_ge(s["end_project"], 4 * b + 4)
                hold(sp)
                with sp.Fori(0, 2) as gp:
                    n0 = b * 16 + gp * 8
                    for gi in range(2):
                        for j in range(4):
                            m = 4 * gi + j
                            sp.wait_ge(s["s1_ps"], n0 + 2)
                            sp.dma_start(img[m], proj_d[b, bass.ds(gp * 8 + m, 1), :].rearrange("o (t p n) -> p (o t) n", t=2, p=P))\
                              .then_inc(s[f"img_in{gi}"], 16)
                    for m in range(8):
                        sp.wait_ge(s["parts_done"], ready(n0 + m))
                        sp.dma_start(xe_d[b, bass.ds(gp * 8 + m, 1), :].rearrange("o (t p n) -> p (o t) n", t=2, p=P),
                                     xe_s[m % 2].rearrange("p (t n) -> p t n", t=2)).then_inc(s[f"xe_out{m % 2}"], 16)
                        for i in range(3):
                            sp.dma_start(xs_d[b, i, bass.ds(gp * 8 + m, 1), :].rearrange("o (t p n) -> p (o t) n", t=2, p=P),
                                         parts[m % 2][:, i, :].rearrange("p (t n) -> p t n", t=2)).then_inc(s[f"xe_out{m % 2}"], 16)
                for q in range(2):
                    sp.wait_ge(s[f"xe_out{q}"], 512 * b + 512 + 16)
                sp.wait_ge(s["end_fourier"], 4 * b + 4)
                hold(sp)
                with sp.Fori(0, 4) as i:
                    for q in range(2):
                        n = b * 8 + 2 * i + q
                        sp.wait_ge(s["st_done"], freed(n))
                        for g in range(8):
                            px = bass.ds(g * (PIX // 8) + i * 2048 + q * 1024, 1024)
                            sp.dma_start(xe_t[q][g * CM:(g + 1) * CM, :], xe_d[b, :, px]).then_inc(s[f"st_in{q}"], 16)
                            sp.dma_start(xq_t[q][g * CM:(g + 1) * CM, :], proj_d[b, CM:2 * CM, px]).then_inc(s[f"st_in{q}"], 16)
                sp.wait_ge(s["st_done"], ready(b * 8 + 7))
                for g in range(8):
                    sp.dma_start(pe_d[b, :, g * (LPIX // 8):(g + 1) * (LPIX // 8)], pe_t[g * CM:(g + 1) * CM, :]).then_inc(s["pe_out"], 16)
                sp.wait_ge(s["pe_out"], 128 * b + 128)
                sp.wait_ge(s["end_stats"], 4 * b + 4)
                hold(sp)
                with sp.Fori(0, 16) as i:
                    for q in range(2):
                        sp.wait_ge(s["corr_ps"], freed(b * 32 + 2 * i + q))
                        hold(sp)
                        sp.dma_start(lowload[q][0:CM, :], pe_d[b, :, bass.ds(i * 1024 + q * 512, 512)]).then_inc(s[f"pe_in{q}"], 16)
                sp.wait_ge(s["corr_ps"], ready(b * 32 + 31))
                hold(sp)
                sp.wait_ge(s["merged"], ready(b * 64 + 63))
                hold(sp)
                with sp.Fori(0, 16) as i:
                    for q in range(2):
                        n = b * 32 + 2 * i + q
                        sp.wait_ge(s["gcorr_add"], freed(n))
                        sp.dma_start(lowload[q][0:CM, :], pe_d[b, :, bass.ds(i * 1024 + q * 512, 512)]).then_inc(s[f"gate_in{q}"], 16)
                        sp.dma_start(conv[q], gate_d[b, :, bass.ds(i * 1024 + q * 512, 512)]).then_inc(s[f"gate_in{q}"], 16)
                sp.wait_ge(s["end_layer"], 4 * b + 4)
                hold(sp)
                with sp.Fori(0, 16) as i:
                    for q in range(2):
                        n = b * 32 + 2 * i + q
                        sp.wait_ge(s["up_ps"], freed(n))
                        px = bass.ds(i * 4096 + q * 2048, 2048)
                        sp.dma_start(stack[q][0:48, :], xs_d[b, 0:3, :, px].rearrange("i m n -> (i m) n")).then_inc(s[f"stack_in{q}"], 16)
                        sp.dma_start(stack[q][48:80, :], xs_d[b, 0:2, :, px].rearrange("i m n -> (i m) n")).then_inc(s[f"stack_in{q}"], 16)
                        sp.dma_start(stack[q][80:96, :], xs_d[b, 0, :, px]).then_inc(s[f"stack_in{q}"], 16)
                        for e in range(2):
                            c = 2 * q + e
                            sp.wait_ge(s[f"x_out{c}"], 256 * b + 16 * i + 16)
                            hold(sp)
                            sp.dma_start(X[:, c, :, :], x[b, :, bass.ds(i * 4096 + c * 1024, 1024)].rearrange("(h p) n -> p h n", p=P))\
                              .then_inc(s[f"x_in{c}"], 16)
                sp.wait_ge(s["end_out"], 4 * b + 4)
                hold(sp)

        @block.tensor
        def _(pe):
            mm = nc.tensor.matmul
            credit(pe, "proj_ps", "lowp_ps", "s1_ps", "s2_ps", "s3_ps", "s4_ps", "corr_ps", "conv_ps", "gcorr_ps", "up_ps")
            pe.sem_inc(s["gain_ps"], 2)
            pe.wait_ge(s["consts_in"], 16 * 13)

            def gain_chunk(q, n, loads):
                pe.wait_ge(s[f"basis_in{q}"], loads)
                pe.wait_ge(s["gain_t"], n + 1)
                for k in range(16):
                    last = mm(bank[:, q, k * CM:(k + 1) * CM], Y[0:NA * NR, q * 16 + k, 0:P], S[0:NA * NR, 768:784], start=True, stop=True)
                last.then_inc(s["gain_ps"], 1)
            with pe.Fori(0, (NSLOT // 16 - 1) // 2) as i:
                for q in range(2):
                    gain_chunk(q, 2 * i + q, 16 * i + 16)
            gain_chunk(0, NSLOT // 16 - 1, 16 * ((NSLOT // 16 - 1) // 2) + 16)
            pe.wait_ge(s["ve_setup"], 3)
            for o in range(2):
                for v, col in ((gnw, 0), (gnb, 2)):
                    for h in range(2):
                        mm(bank[:, 2, col + o:col + o + 1], S[:, 2304 + 1024 + h * SIDE + o * P:2304 + 1024 + h * SIDE + (o + 1) * P],
                           v[:, h:h + 1], start=h == 0, stop=h == 1)
            for h in range(2):
                mm(bank[:, 3, 0:1], S[:, h * P:(h + 1) * P], ones[:, 0:1], start=h == 0, stop=h == 1)
            for h in range(2):
                mm(bank[:, 4, 0:P], S[:, h * P:(h + 1) * P], S[:, h * P:(h + 1) * P], start=h == 0, stop=h == 1)
            for h in range(2):
                last = mm(bank[0:CM, 5, 0:SIDE], wproj[:, h, CM:2 * CM], wpool[:, h, :], start=h == 0, stop=h == 1)
            last.then_inc(s["te_setup"], 1)
            pe.wait_ge(s["mv_setup"], 1)

            with pe.Fori(0, B) as b:
                with pe.Fori(0, 16) as i:
                    for q in range(2):
                        n = b * 32 + 2 * i + q
                        pe.wait_ge(s["proj_st"], freed(n))
                        for e in range(2):
                            pe.wait_ge(s[f"x_in{2 * q + e}"], 512 * b + 16 * i + 16)
                        for h in range(2):
                            for k in range(4):
                                last = mm(bank[32 * k:32 * k + 32, q, :], wproj[:, h, :], X[:, 2 * q + k // 2, h, (k % 2) * 512:(k % 2) * 512 + 512],
                                          start=h == 0, stop=h == 1)
                        last.then_inc(s["proj_ps"], 1)
                        pe.wait_ge(s["pool_done"], 2 + 2 + b * 64 + i * 4 + 2 * q + 2)
                        pe.wait_ge(s["y_ev"], freed(n))
                        pe.wait_ge(s["g_st"], freed(n))
                        for o in range(2):
                            for h in range(2):
                                last = mm(bank[:, 2 + 2 * o + q, :], wpool[:, h, o * P:(o + 1) * P], pooled[q][:, h, :], start=h == 0, stop=h == 1)
                        last.then_inc(s["lowp_ps"], 1)
                leave(pe, "end_project", b)
                with pe.Fori(0, 2) as gp:
                    n0 = b * 16 + gp * 8
                    for gi in range(2):
                        def forward2(m):
                            pe.wait_ge(s["h1_st"], ready(n0 + m))
                            pe.wait_ge(s["f_st"], freed(n0 + m))
                            for tk in range(2):
                                for tx in range(2):
                                    last = mm(bank[:, 2 + m % 2, tk * SIDE:(tk + 1) * SIDE], half1[m % 2][:, tx, tk * P:(tk + 1) * P], fwd[:, tx, :],
                                              start=tx == 0, stop=tx == 1)
                            last.then_inc(s["s2_ps"], 1)
                        pe.wait_ge(s[f"img_in{gi}"], 128 * b + 64 * gp + 64)
                        for j in range(4):
                            m = 4 * gi + j
                            pe.wait_ge(s["h1_st"], freed(n0 + m))
                            for tx in range(2):
                                for ty in range(2):
                                    last = mm(bank[:, m % 2, tx * SIDE:(tx + 1) * SIDE], img[m][:, ty, tx * P:(tx + 1) * P], fwd[:, ty, :],
                                              start=ty == 0, stop=ty == 1)
                            last.then_inc(s["s1_ps"], 1)
                            if j:
                                forward2(m - 1)
                        forward2(4 * gi + 3)
                    for gi in range(2):
                        def inverse2(m):
                            pe.wait_ge(s["h2_st"], ready(n0 + m))
                            pe.wait_ge(s["xe_st"], freed(n0 + m))
                            for ty in range(2):
                                for tl in range(2):
                                    last = mm(bank[:, 6 + m % 2, ty * SIDE:(ty + 1) * SIDE], half2[m % 2][:, tl, ty * P:(ty + 1) * P], inv[:, tl, :],
                                              start=tl == 0, stop=tl == 1)
                            last.then_inc(s["s4_ps"], 1)
                        pe.wait_ge(s["ew_done"], b * 4 + gp * 2 + gi + 2)
                        for j in range(4):
                            m = 4 * gi + j
                            pe.wait_ge(s["h2_st"], freed(n0 + m))
                            for tl in range(2):
                                for tk in range(2):
                                    a = tk * SIDE + tl * P
                                    last = mm(bank[:, 4 + m % 2, tl * SIDE:(tl + 1) * SIDE], freq[:, m, a:a + P], inv[:, tk, :],
                                              start=tk == 0, stop=tk == 1)
                            last.then_inc(s["s3_ps"], 1)
                            if j:
                                inverse2(m - 1)
                        inverse2(4 * gi + 3)
                leave(pe, "end_fourier", b)
                with pe.Fori(0, 4) as i:
                    for q in range(2):
                        n = b * 8 + 2 * i + q
                        pe.wait_ge(s[f"st_in{q}"], 1024 * b + 256 * i + 256)
                        pe.wait_ge(s["st_done"], freed(n))
                        for k in range(2):
                            last = mm(bank[:, 2 * q + k, :], gram[:, :], xe_t[q][:, k * 512:(k + 1) * 512], start=True, stop=True)
                        last.then_inc(s["gram_ps"], 1)
                pe.wait_ge(s["tot_in"], b + 1)
                mm(bank[:, 4, 0:2], ones[:, :], stat[:, 0:2], start=True, stop=True).then_inc(s["tot_ps"], 1)
                leave(pe, "end_stats", b)
                with pe.Fori(0, 16) as i:
                    for q in range(2):
                        n = b * 32 + 2 * i + q
                        pe.wait_ge(s[f"pe_in{q}"], 256 * b + 16 * i + 16)
                        pe.wait_ge(s["corr_add"], freed(n))
                        mm(bank[:, 6 + q, :], cmix[:, 0:P], lowload[q][0:CM, :], start=True, stop=True).then_inc(s["corr_ps"], 1)

                def gates_of(w, q, n, rhs):
                    pe.wait_ge(s["gates_done"], freed(n))
                    pe.wait_ge(s["scans_done"], freed(n))
                    mm(bank[:, 2 + q, :], wscan[:, 2 * w, :], rhs, start=True, stop=True)
                    mm(bank[:, 4 + q, :], wscan[:, 2 * w + 1, :], rhs, start=True, stop=True).then_inc(s["z_ps"], 1)
                pe.wait_ge(s["pads_done"], 4 * b + 4)
                hold(pe)
                with pe.Fori(0, 16) as i:
                    for q in range(2):
                        c = b * 32 + 2 * i + q
                        pe.wait_ge(s["norm_done"], c + b + 2)
                        pe.wait_ge(s["conv_done"], freed(c))
                        for k, tap in enumerate(TE_TAPS):
                            rhs = Y[:, bass.ds(8 * i + 4 * q + 1 + tap // 3, 4), tap % 3:tap % 3 + LOW]
                            last = mm(bank[:, q, :], taps[:, k, :], rhs, start=k == 0, stop=k == len(TE_TAPS) - 1)
                        last.then_inc(s["conv_ps"], 1)
                    for q in range(2):
                        pe.wait_ge(s["s_ready"], b * 32 + 2 * i + q + 1)
                        gates_of(0, q, b * 64 + 2 * i + q, S[:, bass.ds(i * 1024 + q * 512, 512)])
                sc = S[:, :].rearrange("p (r w) -> p w r", w=LOW)
                with pe.Fori(0, 16) as i:
                    for q in range(2):
                        pe.wait_ge(s["s_ready"], b * 32 + 32)
                        gates_of(1, q, b * 64 + 32 + 2 * i + q, sc[:, bass.ds(8 * i + 4 * q, 4), :])
                with pe.Fori(0, 16) as i:
                    for q in range(2):
                        n = b * 32 + 2 * i + q
                        pe.wait_ge(s[f"gate_in{q}"], 512 * b + 32 * i + 32)
                        pe.wait_ge(s["gcorr_add"], freed(n))
                        mm(bank[:, 6 + q, :], cmix[:, P:2 * P], lowload[q][0:CM, :], start=True, stop=True).then_inc(s["gcorr_ps"], 1)
                leave(pe, "end_layer", b)
                with pe.Fori(0, 16) as i:
                    for q in range(2):
                        n = b * 32 + 2 * i + q
                        pe.wait_ge(s["up_ready"], ready(n))
                        pe.wait_ge(s[f"stack_in{q}"], 768 * b + 48 * i + 48)
                        for e in range(2):
                            for h in range(2):
                                k = 2 * e + h
                                pe.wait_ge(s["added"], 4 * n + k + 1)
                                for j in range(2):
                                    px = slice(e * 1024 + j * 512, e * 1024 + j * 512 + 512)
                                    mm(bank[:, 2 * k + j, :], wup[:, h * P:(h + 1) * P], up[q][:, px], start=True, stop=False)
                                    last = mm(bank[:, 2 * k + j, :], wstack[:, h * P:(h + 1) * P], stack[q][:, px], start=False, stop=True)
                                if k < 3:
                                    last.then_inc(s["ve_up"], 1)
                                else:
                                    last.then_inc(s["up_ps"], 1)
                leave(pe, "end_out", b)

        @block.scalar
        def _(act):
            A = nc.scalar.activation
            credit(act, "square_done", "square_done", "proj_st", "h1_st", "f_st", "h2_st", "xe_st", "gates_done", "gsig_done")
            act.sem_inc(s["gain_t"], 1)
            act.wait_ge(s["stores_set"], 1)

            def tanh_chunk(q, n, at):
                act.wait_ge(s["gain_ps"], 2 + n + 1)
                A(gains[:, :, at], bank[:, q, 0:16 * CM].rearrange("p (k m) -> p m k", m=CM), ACT.Tanh).then_inc(s["gain_t"], 1)
            with act.Fori(0, (NSLOT // 16 - 1) // 2) as i:
                for q in range(2):
                    tanh_chunk(q, 2 * i + q, bass.ds(32 * i + 16 * q, 16))
            tanh_chunk(0, NSLOT // 16 - 1, slice(NSLOT - 16, NSLOT))
            act.wait_ge(s["mv_setup"], 1)

            with act.Fori(0, B) as b:
                with act.Fori(0, 16) as i:
                    for q in range(2):
                        n = b * 32 + 2 * i + q
                        for e in range(2):
                            c = 2 * q + e
                            act.wait_ge(s[f"x_in{c}"], 512 * b + 16 * i + 16)
                            act.wait_ge(s["square_done"], 4 + n * 2 + e)
                            A(junk, X[:, c, :, :].rearrange("p h n -> p (h n)"), ACT.Square,
                              accum_out=sum_xx[:, bass.ds(4 * i + c, 1)]).then_inc(s["square_done"], 1)
                        act.wait_ge(s["proj_ps"], ready(n))
                        act.wait_ge(s[f"proj_out{q}"], 64 * (b * 16 + i) + 16)
                        A(pstage[q], bank[:, q, :], ACT.Copy).then_inc(s["proj_st"], 1)
                        act.wait_ge(s["proj_st"], ready(n))
                        for k in range(4):
                            act.dma_start(proj_d[b, :, bass.ds(i * 4096 + q * 2048 + k * 512, 512)], pstage[q][32 * k:32 * k + 32, :])\
                               .then_inc(s[f"proj_out{q}"], 16)
                for q in range(2):
                    act.wait_ge(s[f"proj_out{q}"], 64 * 16 * (b + 1) + 16)
                hold(act)
                leave(act, "end_project", b)
                with act.Fori(0, 2) as gp:
                    n0 = b * 16 + gp * 8
                    g0 = b * 4 + gp * 2

                    def copy_forward(m):
                        act.wait_ge(s["s1_ps"], ready(n0 + m))
                        act.wait_ge(s["s2_ps"], freed(n0 + m))
                        A(half1[m % 2], bank[:, m % 2, :].rearrange("p (t n) -> p t n", t=2), ACT.Copy).then_inc(s["h1_st"], 1)
                        act.wait_ge(s["s2_ps"], ready(n0 + m))
                        A(freq[:, m, :], bank[:, 2 + m % 2, :], ACT.Copy).then_inc(s["f_st"], 1)

                    def copy_inverse(m):
                        act.wait_ge(s["s3_ps"], ready(n0 + m))
                        act.wait_ge(s["s4_ps"], freed(n0 + m))
                        A(half2[m % 2], bank[:, 4 + m % 2, :].rearrange("p (t n) -> p t n", t=2), ACT.Copy).then_inc(s["h2_st"], 1)
                        act.wait_ge(s["s4_ps"], ready(n0 + m))
                        act.wait_ge(s[f"xe_out{m % 2}"], 64 * (b * 8 + gp * 4 + m // 2) + 16)
                        A(parts[m % 2][:, 0, :], bank[:, 6 + m % 2, :], ACT.Copy)
                        A(xe_s[m % 2], bank[:, 6 + m % 2, :], ACT.Copy).then_inc(s["xe_st"], 1)

                    def squares(gi):
                        act.wait_ge(s["uv_ready"], g0 + gi + 1)
                        for k in range(4):
                            last = A(tmp[4 + k], tmp[k], ACT.Square)
                        last.then_inc(s["sq_ready"], 1)

                    def roots(gi):
                        act.wait_ge(s["m_ready"], g0 + gi + 1)
                        for v in (tmp[4], tmp[5], small[2]):
                            last = A(v, v, ACT.Sqrt)
                        last.then_inc(s["root_ready"], 1)
                    for m in range(4):
                        copy_forward(m)
                    copy_forward(4)
                    squares(0)
                    copy_forward(5)
                    copy_forward(6)
                    roots(0)
                    copy_forward(7)
                    copy_inverse(0)
                    squares(1)
                    copy_inverse(1)
                    copy_inverse(2)
                    roots(1)
                    copy_inverse(3)
                    for m in range(4, 8):
                        copy_inverse(m)
                leave(act, "end_fourier", b)
                act.wait_ge(s["tot_ps"], b + 1)
                act.wait_ge(s["norm_set"], b + 1)
                A(stat[:, 5:6], stat[:, 4:5], ACT.Sqrt).then_inc(s["var_root"], 1)
                leave(act, "end_stats", b)
                with act.Fori(0, 16) as i:
                    for q in range(2):
                        act.wait_ge(s["corr_add"], ready(b * 32 + 2 * i + q))
                        v = Y[:, bass.ds(8 * i + 4 * q + 2, 4), 1:1 + LOW]
                        A(v, v, ACT.Identity, scale=rs, bias=cshift[:, 0:1]).then_inc(s["norm_done"], 1)
                act.drain().then_inc(s["norm_done"], 1)

                def gates(w, q, n):
                    act.wait_ge(s["z_ps"], n + 1)
                    act.wait_ge(s["scans_done"], freed(n))
                    z = bank[:, 2 + q, :].rearrange("p (r w) -> p r w", w=LOW)
                    A(lines(keep[q], 1), z, ACT.Sigmoid, scale=-1.0, bias=nbd[w])
                    A(lines(take[q], 1), z, ACT.Sigmoid, bias=bd[w]).then_inc(s["gates_done"], 1)
                act.wait_ge(s["pads_done"], 4 * b + 4)
                with act.Fori(0, 16) as i:
                    for q in range(2):
                        act.wait_ge(s["conv_done"], ready(b * 32 + 2 * i + q))
                        A(sig[q], conv[q], ACT.Sigmoid).then_inc(s["sig_done"], 1)
                    for q in range(2):
                        gates(0, q, b * 64 + 2 * i + q)
                with act.Fori(0, 16) as i:
                    for q in range(2):
                        gates(1, q, b * 64 + 32 + 2 * i + q)
                with act.Fori(0, 16) as i:
                    for q in range(2):
                        n = b * 32 + 2 * i + q
                        act.wait_ge(s["gcorr_add"], ready(n))
                        act.wait_ge(s["gated"], freed(n))
                        A(sig[q], bsc[q][:, 0:512], ACT.Sigmoid, scale=rs, bias=cshift[:, 1:2]).then_inc(s["gsig_done"], 1)
                leave(act, "end_layer", b)
                with act.Fori(0, 16) as i:
                    for c in range(4):
                        act.wait_ge(s["added"], 4 + b * 128 + i * 8 + 2 * c + 2)
                        act.dma_start(out[b, :, bass.ds(i * 4096 + c * 1024, 1024)].rearrange("(h p) n -> p h n", p=P), X[:, c, :, :])\
                           .then_inc(s[f"x_out{c}"], 16)
                leave(act, "end_out", b)
            for c in range(4):
                act.wait_ge(s[f"x_out{c}"], 256 * B + 16)

        @block.gpsimd
        def _(pool):
            g = nc.gpsimd
            credit(pool, "parts_done", "merged", "gated")
            pool.wait_ge(s["mv_setup"], 1)
            pool.wait_ge(s["stores_set"], 1)
            with pool.Fori(0, B) as b:
                leave(pool, "end_project", b)
                with pool.Fori(0, 2) as gp:
                    step = Steps(pool, "pl_parts", (b * 2 + gp) * 8)
                    for m in range(8):
                        q = m % 2
                        pool.wait_ge(s["xe_st"], ready(b * 16 + gp * 8 + m))
                        g.tensor_tensor(rest[q], xe_s[q], parts[q][:, 0, :], ALU.subtract)
                        step.done(g.tensor_tensor(parts[q][:, 1, :], xe_s[q], parts[q][:, 0, :], ALU.subtract))
                        step.wait()
                        g.tensor_tensor(parts[q][:, 2, :], rest[q], parts[q][:, 1, :], ALU.subtract).then_inc(s["parts_done"], 1)
                leave(pool, "end_fourier", b)
                leave(pool, "end_stats", b)
                pool.memset(Y[:, 2:2 + LOW, 0:1], 0.0)
                pool.memset(Y[:, 2:2 + LOW, LW - 1:LW], 0.0)
                pool.memset(Y[:, 1, :], 0.0)
                pool.memset(Y[:, YROWS - 1, :], 0.0)
                for q in range(2):
                    pool.memset(lines(keep[q], 0), 0.0).then_inc(s["pads_done"], 1)
                    pool.memset(lines(take[q], 0), 0.0).then_inc(s["pads_done"], 1)
                with pool.Fori(0, 16) as i:
                    for q in range(2):
                        pool.wait_ge(s["scans_done"], ready(b * 64 + 2 * i + q))
                        g.tensor_tensor(Y[:, bass.ds(8 * i + 4 * q + 1, 4), 1:1 + LOW], lines(fsc[q], 1), lines(bsc[q], 1), ALU.add)\
                         .then_inc(s["merged"], 1)
                yc = Y[:, 1:1 + LOW, :].rearrange("p r w -> p w r")
                with pool.Fori(0, 16) as i:
                    for q in range(2):
                        n = 2 * i + q
                        pool.wait_ge(s["scans_done"], ready(b * 64 + 32 + n))
                        g.tensor_tensor(lines(fsc[q], 1), lines(fsc[q], 1), lines(bsc[q], 1), ALU.add).then_inc(s["pl_l1"], 1)
                        pool.wait_ge(s["pl_l1"], b * 32 + n + 1)
                        v = yc[:, bass.ds(8 * i + 4 * q + 1, 4), :]
                        g.tensor_tensor(v, v, lines(fsc[q], 1), ALU.add).then_inc(s["merged"], 1)
                with pool.Fori(0, 16) as i:
                    for q in range(2):
                        pool.wait_ge(s["gsig_done"], ready(b * 32 + 2 * i + q))
                        v = Y[:, bass.ds(8 * i + 4 * q + 1, 4), 1:1 + LOW]
                        g.tensor_tensor(v, v, sig[q].rearrange("p (r w) -> p r w", w=LOW), ALU.mult).then_inc(s["gated"], 1)
                leave(pool, "end_layer", b)
                leave(pool, "end_out", b)

        @block.vector
        def _(dve):
            v = nc.vector
            stt = v.scalar_tensor_tensor
            ts = v.tensor_scalar
            tt = v.tensor_tensor
            credit(dve, "pool_done", "pool_done", "y_ev", "g_st", "st_done", "corr_add", "conv_done", "scans_done", "gcorr_add", "up_ready")
            dve.sem_inc(s["added"], 4)
            dve.sem_inc(s["ew_done"], 1)
            dve.wait_ge(s["stores_set"], 1)
            st = Steps(dve, "ve_setup", 0)
            dve.wait_ge(s["consts_in"], 16 * 13)
            st.done(v.memset(ones[:, :], 1.0))
            st.done(v.tensor_copy(S[:, 3328:3840].rearrange("p (t n) -> p t n", t=2), wpool[:, :, :]))
            st.wait()
            for h in range(2):
                ins = ts(wpool[:, h, :], wpool[:, h, :], gnw[:, h:h + 1], 0.25, ALU.mult, ALU.mult)
            st.done(ins)
            for w in range(2):
                v.tensor_scalar(nbd[w], bd[w], -1.0, None, ALU.mult)
            for k, tap in enumerate(TE_TAPS):
                ts(taps[:, k, :], S[:, 640:768], dw[:, tap:tap + 1], None, ALU.mult)
            ts(wup[:, :], wup[:, :], 1.0 / 64, None, ALU.mult)
            R = 6 * CM
            w32, p16, acc = S[0:R, 256:512], [S[0:R, 3840 + 128 * j:3968 + 128 * j].bitcast(BF16) for j in range(3)], S[0:R, 4224:4480]
            r1 = S[0:R, 4480:4736]
            st.done(v.tensor_copy(p16[0], w32)); st.wait()
            st.done(tt(r1, w32, p16[0], ALU.subtract)); st.wait()
            st.done(v.tensor_copy(p16[1], r1)); st.wait()
            st.done(tt(r1, r1, p16[1], ALU.subtract)); st.wait()
            st.done(v.tensor_copy(p16[2], r1)); st.wait()
            st.done(ts(acc, p16[0], cols[0:R, 4:5], None, ALU.mult)); st.wait()
            st.done(stt(acc, p16[1], cols[0:R, 5:6], acc, ALU.mult, ALU.add)); st.wait()
            st.done(stt(wstack[:, :], p16[2], cols[0:R, 6:7], acc, ALU.mult, ALU.add))
            dve.wait_ge(s["gain_t"], NSLOT // 16 + 1)
            dve.wait_ge(s["rowb_in"], 16)
            rowb = S[0:1, 1024:1024 + P * CM].rearrange("o (m l) -> o m l", l=P)
            st.done(tt(gains[0:1, :, P:2 * P], gains[0:1, :, P:2 * P], rowb, ALU.add)); st.wait()
            st.done(ts(gains[0:1, :, P:2 * P], gains[0:1, :, P:2 * P], 0.5, None, ALU.mult)); st.wait()
            for j, slot in enumerate((0, None, P, None)):
                if slot is None:
                    st.done(tt(corner[:, :, j], gains[:, :, GA1 + j // 2], gains[:, :, GA1B + j // 2], ALU.add)); st.wait()
                    st.done(ts(corner[:, :, j], corner[:, :, j], 0.25, 1.0, ALU.mult, ALU.add))
                elif slot == 0:
                    st.done(ts(corner[:, :, j], gains[:, :, 0], 0.5, 1.0, ALU.mult, ALU.add))
                else:
                    st.done(ts(corner[:, :, j], gains[:, :, P], 0.5, 1.0, ALU.mult, ALU.add))
            st.wait()
            st.done(ts(gains[:, :, 0:2 * P], gains[:, :, 0:2 * P], quart_h, half_h, ALU.mult, ALU.add))
            dve.wait_ge(s["te_setup"], 1)
            v.tensor_copy(vec[:, 19:23], bank[:, 2, 0:4])
            v.tensor_copy(wsum, bank[:, 3, 0:1])
            tt(gram[:, :], S[:, 512:640], bank[:, 4, 0:P], ALU.mult)
            v.tensor_copy(cmix[:, :], bank[0:CM, 5, 0:SIDE])
            dve.drain().then_inc(s["mv_setup"], 1)

            with dve.Fori(0, B) as b:
                with dve.Fori(0, 16) as i:
                    step = Steps(dve, "ve_pool", (b * 16 + i) * 4)
                    for q in range(2):
                        n = b * 32 + 2 * i + q
                        for e in range(2):
                            c = 2 * q + e
                            dve.wait_ge(s[f"x_in{c}"], 512 * b + 16 * i + 16)
                            xr = X[:, c, :, :].rearrange("p h (r a w) -> p (h r) a w", a=2, w=SIDE)
                            vr = vert[e].rearrange("p (r w) -> p r w", w=SIDE)
                            step.done(tt(vr, xr[:, :, 0, :], xr[:, :, 1, :], ALU.add))
                            if e == 0:
                                dve.wait_ge(s["lowp_ps"], freed(n))
                            step.wait()
                            vp = vert[e].rearrange("p (h n a) -> p h n a", h=2, a=2)
                            stt(pooled[q][:, :, e * 256:(e + 1) * 256], vp[:, :, :, 0], 1.0, vp[:, :, :, 1], ALU.mult, ALU.add,
                                accum_out=sum_x[:, bass.ds(4 * i + c, 1)]).then_inc(s["pool_done"], 1)
                        dve.wait_ge(s["lowp_ps"], ready(n))
                        v.tensor_copy(Y[:, bass.ds(8 * i + 4 * q + 2, 4), 1:1 + LOW],
                                      bank[:, 2 + q, :].rearrange("p (r w) -> p r w", w=LOW)).then_inc(s["y_ev"], 1)
                        dve.wait_ge(s[f"gate_out{q}"], 16 * (b * 16 + i) + 16)
                        v.tensor_copy(gstage[q], bank[:, 4 + q, :]).then_inc(s["g_st"], 1)
                leave(dve, "end_project", b)
                with dve.Fori(0, 2) as gp:
                    for gi in range(2):
                        grp = b * 4 + gp * 2 + gi
                        step = Steps(dve, "ve_ew", grp * EW)
                        dve.wait_ge(s["ew_done"], grp + 1)
                        dve.wait_ge(s["f_st"], ready(b * 16 + gp * 8 + 4 * gi + 3))
                        fm = freq[:, 4 * gi:4 * gi + 4, :]
                        cc, cs, sc, ss = (fm[:, :, k * P:(k + 1) * P] for k in range(4))
                        edge = fm.rearrange("p m (k l) -> p m k l", l=P)[:, :, :, 0]
                        u, w_, p_, q_ = (tmp[k].rearrange("p (m l) -> p m l", m=4) for k in range(4))
                        z4, sq4, m4, sw4 = (small[k].rearrange("p (m k) -> p m k", m=4) for k in range(4))
                        step.done(v.tensor_copy(z4, edge))
                        stt(u, ss, negk, cc, ALU.mult, ALU.add)
                        stt(w_, cc, kappa, ss, ALU.mult, ALU.add)
                        stt(p_, sc, kappa, cs, ALU.mult, ALU.add)
                        stt(q_, cs, negk, sc, ALU.mult, ALU.add).then_inc(s["uv_ready"], 1)
                        step.wait()
                        step.done(tt(sq4, z4, z4, ALU.mult))
                        step.wait()
                        v.tensor_copy(sw4[:, :, 0:2], sq4[:, :, 2:4])
                        step.done(v.tensor_copy(sw4[:, :, 2:4], sq4[:, :, 0:2]))
                        step.done(ts(small[2], small[1], TINY, None, ALU.max))
                        step.wait()
                        step.done(stt(small[2], small[3], kappa, small[2], ALU.mult, ALU.add))
                        step.wait()
                        step.done(ts(small[4], small[2], TINY, DELTA, ALU.is_le, ALU.mult))
                        dve.wait_ge(s["sq_ready"], grp + 1)
                        step.done(stt(tmp[4], tmp[4], TINY, tmp[6], ALU.max, ALU.add))
                        step.done(stt(tmp[5], tmp[5], TINY, tmp[7], ALU.max, ALU.add))
                        step.wait()
                        step.done(ts(tmp[6], tmp[4], TINY, DELTA, ALU.is_le, ALU.mult))
                        ts(tmp[7], tmp[5], TINY, DELTA, ALU.is_le, ALU.mult).then_inc(s["m_ready"], 1)
                        dve.wait_ge(s["m_ready"], grp + 1)
                        zmask = cols[:, 8:12]
                        for k in range(4):
                            ins = tt(small[5][:, 4 * k:4 * k + 4], small[4][:, 4 * k:4 * k + 4], zmask, ALU.mult)
                        step.done(ins)
                        step.done(tt(tmp[0], tmp[0], tmp[6], ALU.add))
                        step.done(stt(tmp[1], tmp[7], kappa, tmp[1], ALU.mult, ALU.add))
                        step.done(tt(tmp[3][0:1, :], tmp[3][0:1, :], tmp[7][0:1, :], ALU.add))
                        step.wait()
                        step.done(tt(small[0], small[0], small[5], ALU.add))
                        dve.wait_ge(s["root_ready"], grp + 1)
                        v.reciprocal(tmp[4], tmp[4])
                        v.reciprocal(tmp[5], tmp[5])
                        step.done(v.reciprocal(small[2], small[2]))
                        step.wait()
                        ts(tmp[4], tmp[4], FEPS, 1.0, ALU.mult, ALU.add)
                        ts(tmp[5], tmp[5], FEPS, 1.0, ALU.mult, ALU.add)
                        step.done(ts(small[2], small[2], FEPS, 1.0, ALU.mult, ALU.add))
                        step.wait()
                        ch = bass.ds(8 * gp + 4 * gi, 4)
                        gp4, gm4 = (tmp[4 + k].rearrange("p (m l) -> p m l", m=4) for k in range(2))
                        tt(gp4, gp4, gains[:, ch, 0:P], ALU.mult)
                        tt(gm4, gm4, gains[:, ch, P:2 * P], ALU.mult)
                        step.done(tt(m4, m4, corner[:, ch, :], ALU.mult))
                        step.wait()
                        tt(tmp[0], tmp[0], tmp[4], ALU.mult)
                        tt(tmp[2], tmp[2], tmp[4], ALU.mult)
                        tt(tmp[1], tmp[1], tmp[5], ALU.mult)
                        tt(tmp[3], tmp[3], tmp[5], ALU.mult)
                        step.done(tt(small[0], small[0], small[2], ALU.mult))
                        step.wait()
                        stt(cc, w_, kappa, u, ALU.mult, ALU.add)
                        stt(ss, u, negk, w_, ALU.mult, ALU.add)
                        stt(cs, q_, negk, p_, ALU.mult, ALU.add)
                        step.done(stt(sc, p_, kappa, q_, ALU.mult, ALU.add))
                        step.wait()
                        v.tensor_copy(edge, z4).then_inc(s["ew_done"], 1)
                        assert step.n == EW
                leave(dve, "end_fourier", b)
                with dve.Fori(0, 4) as i:
                    step = Steps(dve, "ve_stat", (b * 4 + i) * 6)
                    for q in range(2):
                        n = b * 8 + 2 * i + q
                        dve.wait_ge(s[f"st_in{q}"], 1024 * b + 256 * i + 256)
                        xr = xe_t[q].rearrange("p (r a w) -> p r a w", a=2, w=SIDE)
                        step.done(tt(vsum.rearrange("p (r w) -> p r w", w=SIDE), xr[:, :, 0, :], xr[:, :, 1, :], ALU.add))
                        step.wait()
                        vp = vsum.rearrange("p (n a) -> p n a", a=2)
                        step.done(stt(pe_t[:, bass.ds(i * 512 + q * 256, 256)], vp[:, :, 0], 1.0, vp[:, :, 1], ALU.mult, ALU.add,
                                      accum_out=sum_xe[:, bass.ds(2 * i + q, 1)]))
                        dve.wait_ge(s["gram_ps"], n + 1)
                        step.done(stt(mix, xq_t[q], 2.0, bank[:, 2 * q:2 * q + 2, :].rearrange("p k n -> p (k n)"), ALU.mult, ALU.add))
                        step.wait()
                        stt(mix, mix, 1.0, xe_t[q], ALU.mult, ALU.mult, accum_out=cross[:, bass.ds(2 * i + q, 1)]).then_inc(s["st_done"], 1)
                dve.wait_ge(s["st_done"], ready(b * 8 + 7))
                v.reduce_sum(stat[:, 0:1], sum_x, AX.X)
                v.reduce_sum(stat[:, 1:2], sum_xx, AX.X)
                v.reduce_sum(stat[:, 2:3], cross, AX.X)
                v.reduce_sum(stat[:, 3:4], sum_xe, AX.X)
                dve.drain()
                tt(stat[:, 1:2], stat[:, 1:2], stat[:, 2:3], ALU.add)
                stt(stat[:, 0:1], stat[:, 3:4], wsum, stat[:, 0:1], ALU.mult, ALU.add)
                dve.drain().then_inc(s["tot_in"], 1)
                dve.wait_ge(s["tot_ps"], b + 1)
                total = 1.0 / (SIDE * PIX)
                ts(stat[:, 2:4], bank[:, 4, 0:2], total, None, ALU.mult)
                dve.drain()
                tt(stat[:, 6:7], stat[:, 2:3], stat[:, 2:3], ALU.mult)
                dve.drain()
                tt(stat[:, 4:5], stat[:, 3:4], stat[:, 6:7], ALU.subtract)
                dve.drain()
                ts(stat[:, 4:5], stat[:, 4:5], 0.0, GN_EPS, ALU.max, ALU.add)
                dve.drain().then_inc(s["norm_set"], 1)
                dve.wait_ge(s["var_root"], b + 1)
                v.reciprocal(stat[:, 5:6], stat[:, 5:6])
                dve.drain()
                tt(stat[:, 6:7], stat[:, 5:6], stat[:, 5:6], ALU.mult)
                dve.drain()
                tt(stat[:, 6:7], stat[:, 6:7], stat[:, 4:5], ALU.mult)
                dve.drain()
                ts(stat[:, 6:7], stat[:, 6:7], -0.5, 1.5, ALU.mult, ALU.add)
                dve.drain()
                tt(rs, stat[:, 5:6], stat[:, 6:7], ALU.mult)
                dve.drain()
                stt(stat[:, 7:8], stat[:, 2:3], -1.0, rs, ALU.mult, ALU.mult)
                dve.drain()
                stt(cshift, cw, stat[:, 7:8], cb, ALU.mult, ALU.add)
                leave(dve, "end_stats", b)
                with dve.Fori(0, 16) as i:
                    for q in range(2):
                        n = b * 32 + 2 * i + q
                        dve.wait_ge(s["corr_ps"], ready(n))
                        yv = Y[:, bass.ds(8 * i + 4 * q + 2, 4), 1:1 + LOW]
                        tt(yv, yv, bank[:, 6 + q, :].rearrange("p (r w) -> p r w", w=LOW), ALU.add).then_inc(s["corr_add"], 1)

                def scans(w, q, n, step):
                    dve.wait_ge(s["gates_done"], ready(n))
                    dve.wait_ge(s["merged"], freed(n))
                    tk = lines(take[q], 1)
                    step.done(stt(tk, bank[:, 4 + q, :].rearrange("p (r w) -> p r w", w=LOW), bv[w], tk, ALU.add, ALU.mult))
                    step.wait()
                    v.tensor_tensor_scan(out=fsc[q][:, 0:SCAN], data0=keep[q][:, 0:SCAN], data1=take[q][:, 0:SCAN],
                                         initial=0.0, op0=ALU.mult, op1=ALU.add)
                    v.tensor_tensor_scan(out=bsc[q][:, 1:SCAN + 1][:, ::-1], data0=keep[q][:, 1:SCAN + 1][:, ::-1],
                                         data1=take[q][:, 1:SCAN + 1][:, ::-1], initial=0.0, op0=ALU.mult, op1=ALU.add)\
                     .then_inc(s["scans_done"], 1)
                NV = 2 * (len(VE_TAPS) - 1) + 2
                dve.wait_ge(s["pads_done"], 4 * b + 4)
                hold(dve)
                with dve.Fori(0, 16) as i:
                    step = Steps(dve, "ve_l1", b * (16 * NV + 32) + i * NV)
                    for q in range(2):
                        dve.wait_ge(s["norm_done"], b * 33 + 2 * i + q + 2)
                        dve.wait_ge(s["conv_ps"], ready(b * 32 + 2 * i + q))
                    for k, tap in enumerate(VE_TAPS):
                        for q in range(2):
                            if k:
                                dve.wait_ge(s["ve_l1"], step.base + 2 * (k - 1) + q + 1)
                            src = Y[:, bass.ds(8 * i + 4 * q + 1 + tap // 3, 4), tap % 3:tap % 3 + LOW]
                            acc = (conv[q] if k else bank[:, q, :]).rearrange("p (r w) -> p r w", w=LOW)
                            ins = stt(conv[q].rearrange("p (r w) -> p r w", w=LOW), src, dw[:, tap:tap + 1], acc, ALU.mult, ALU.add)
                            if k < len(VE_TAPS) - 1:
                                step.done(ins)
                            else:
                                ins.then_inc(s["conv_done"], 1)
                    for q in range(2):
                        n = b * 32 + 2 * i + q
                        dve.wait_ge(s["sig_done"], n + 1)
                        tt(S[:, bass.ds(i * 1024 + q * 512, 512)], conv[q], sig[q], ALU.mult).then_inc(s["s_ready"], 1)
                    for q in range(2):
                        scans(0, q, b * 64 + 2 * i + q, step)
                with dve.Fori(0, 16) as i:
                    step = Steps(dve, "ve_l1", b * (16 * NV + 32) + 16 * NV + 2 * i)
                    for q in range(2):
                        scans(1, q, b * 64 + 32 + 2 * i + q, step)
                with dve.Fori(0, 16) as i:
                    for q in range(2):
                        n = b * 32 + 2 * i + q
                        dve.wait_ge(s["gcorr_ps"], ready(n))
                        dve.wait_ge(s["gsig_done"], freed(n))
                        tt(bsc[q][:, 0:512], conv[q], bank[:, 6 + q, :], ALU.add).then_inc(s["gcorr_add"], 1)
                dve.wait_ge(s["gated"], ready(b * 32 + 31))
                v.tensor_copy(Y[:, 1:1 + LOW, 0:1], Y[:, 1:1 + LOW, 1:2])
                v.tensor_copy(Y[:, 1:1 + LOW, LW - 1:LW], Y[:, 1:1 + LOW, LW - 2:LW - 1]).then_inc(s["edge_done"], 1)
                dve.wait_ge(s["edge_done"], b + 1)
                v.tensor_copy(Y[:, 0, :], Y[:, 1, :])
                v.tensor_copy(Y[:, LOW + 1, :], Y[:, LOW, :])
                leave(dve, "end_layer", b)
                with dve.Fori(0, 16) as i:
                    for q in range(2):
                        n = b * 32 + 2 * i + q
                        r0 = 8 * i + 4 * q + 1
                        mid, above, below = (Y[:, bass.ds(r0 + d, 4), :] for d in (0, -1, 1))
                        stt(vup[q][:, :, 0, :], mid, 3.0, above, ALU.mult, ALU.add)
                        stt(vup[q][:, :, 1, :], mid, 3.0, below, ALU.mult, ALU.add).then_inc(s["up_rows"], 1)
                        dve.wait_ge(s["up_rows"], n + 1)
                        dve.wait_ge(s["up_ps"], freed(n))
                        vv = vup[q].rearrange("p i a w -> p (i a) w")
                        uu = up[q].rearrange("p (r w a) -> p r w a", w=LOW, a=2)
                        stt(uu[:, :, :, 0], vv[:, :, 1:1 + LOW], 3.0, vv[:, :, 0:LOW], ALU.mult, ALU.add)
                        stt(uu[:, :, :, 1], vv[:, :, 1:1 + LOW], 3.0, vv[:, :, 2:2 + LOW], ALU.mult, ALU.add).then_inc(s["up_ready"], 1)
                    for q in range(2):
                        n = b * 32 + 2 * i + q
                        for k in range(4):
                            e, h = k // 2, k % 2
                            if k < 3:
                                dve.wait_ge(s["ve_up"], 3 * n + k + 1)
                            else:
                                dve.wait_ge(s["up_ps"], ready(n))
                            if h == 0:
                                dve.wait_ge(s[f"x_in{2 * q + e}"], 512 * b + 256 + 16 * i + 16)
                            xv = X[:, 2 * q + e, h, :]
                            tt(xv, xv, bank[:, 2 * k:2 * k + 2, :].rearrange("p k n -> p (k n)"), ALU.add).then_inc(s["added"], 1)
                leave(dve, "end_out", b)


def kernel(**inputs):
    import numpy as _np
    import concourse.bacc as _bacc
    from concourse import mybir as _mybir
    from concourse.bass_utils import run_bass_kernel_spmd as _run

    a = {k: _np.asarray(v) for k, v in inputs.items()}
    x = a["x"]
    B = x.shape[0]
    w_in0, w_out0, wts = a["L0_conv_w_in"], a["L0_conv_w_out"], a["L0_conv_weights"]
    fwd, inv = fourier_bases()
    block = (_np.arange(P)[:, None] // CM == _np.arange(P)[None, :] // CM).astype(_np.float32)
    arrays = {
        "x": x.reshape(B, 256, PIX),
        "fwd": fwd, "inv": inv, "basis": gain_basis(), "cols": columns(), "block": block, "ident": _np.eye(P, dtype=_np.float32),
        "wproj": _np.concatenate([w_in0.T, w_out0], axis=1),
        "wtile": _np.tile(w_out0, (1, 8)),
        "wrep": _np.tile(w_out0.T, (6, 1)),
        "wgain": wts[:, :, R0:R0 + NR].reshape(CM, NA * NR).T,
        "w_in1": a["L1_conv_w_in"].T,
        "wscan": _np.concatenate([a["L1_conv_row_wd"].T, a["L1_conv_row_wv"].T, a["L1_conv_col_wd"].T, a["L1_conv_col_wv"].T], axis=0),
        "w_out1": a["L1_conv_w_out"].T,
        "vec": _np.concatenate([a["L1_conv_gn_w"].reshape(2, P).T, a["L1_conv_gn_b"].reshape(2, P).T]
                               + [a[f"L1_conv_{n}"][:, None] for n in ("row_bd", "row_bv", "col_bd", "col_bv")]
                               + [a["L1_conv_row_bd"][:, None], a["L1_conv_col_bd"][:, None]]
                               + [a["L1_conv_w_dw"].reshape(P, 9)], axis=1),
    }
    nc = _bacc.Bacc("TRN2", target_bir_lowering=False, num_devices=1)
    feed, t = {}, {}
    for name, arr in arrays.items():
        arr = _np.ascontiguousarray(arr)
        feed[f"in_{name}"] = arr
        t[name] = nc.dram_tensor(f"in_{name}", arr.shape, _mybir.dt.from_np(arr.dtype), kind="ExternalInput").ap()
    out = nc.dram_tensor("out", [B, 256, PIX], F32, kind="ExternalOutput").ap()
    build(nc, B, t["x"], out, t)
    r = _run(nc, [feed], core_ids=[0])
    return r.results[0]["out"].reshape(B, 256, SIDE, SIDE)
```

```python
import numpy as np
import concourse.bass as bass
from concourse import mybir
from contextlib import ExitStack

F32 = mybir.dt.float32
BF16 = mybir.dt.bfloat16
U16 = mybir.dt.uint16
ALU = mybir.AluOpType
ACT = mybir.ActivationFunctionType
AX = mybir.AxisListType

P = 128
SIDE = 256
PIX = SIDE * SIDE
LOW = SIDE // 2
LPIX = LOW * LOW
CM = 16
NA, NR = 8, 5
R0 = 12
GK = 3 * NA * NR
NSLOT = 272
GA1, GB1, GA1B, GB1B, ROWB = 256, 257, 258, 259, 260
FEPS = 1e-8
TINY = 2.0 ** -100
DELTA = 2.0 ** -50
GN_EPS = 1e-5
LW = LOW + 2
YROWS = LOW + 3
LINE = LOW + 1
SCAN = 4 * LINE


def fourier_bases():
    n = np.arange(SIDE)
    k = np.arange(LOW)
    ang = 2 * np.pi * ((n[:, None] * k[None, :]) % SIDE) / SIDE
    fwd = np.zeros((SIDE, SIDE))
    fwd[:, :LOW] = np.cos(ang)
    fwd[:, LOW:] = np.sin(ang)
    fwd[:, LOW] = 1 - 2 * (n % 2)
    weight = np.full(SIDE, 2.0)
    weight[0] = weight[LOW] = 1.0
    return (fwd / 16).astype(np.float32), (fwd.T * weight[:, None] / 16).astype(np.float32)


def gain_basis():
    f = np.float32
    d = np.arange(-LOW, LOW).astype(f)
    yy, xx = d[:, None], d[None, :]
    r = np.sqrt(yy * yy + xx * xx).astype(f)
    theta = np.mod((np.arctan2(yy, xx).astype(f) + f(np.pi)).astype(f), f(np.pi)).astype(f)
    ridx = np.clip(np.floor(r / 8).astype(int), 0, 16)
    delta = np.pi / NA
    half = f(1.5 * delta / 2)
    centers = (np.arange(NA).astype(f) * f(delta) + f(delta / 2))[:, None, None]
    dist = np.abs(theta[None] - centers)
    aw = np.where(dist < half, np.clip(1 - dist / half, 0, None), 0).astype(f)
    aw = aw / (aw.sum(0, keepdims=True) + f(1e-8))
    aw = aw * (r > f(0.8 * LOW))[None]
    full = np.zeros((NA, NR, SIDE, SIDE), f)
    for j in range(NR):
        full[:, j] = aw * (ridx == R0 + j)[None]
    full = full.reshape(NA * NR, SIDE, SIDE)

    def at(ky, kx):
        return full[:, ky + LOW, kx + LOW]

    t = np.zeros((NA * NR, NSLOT, P), f)
    k = np.arange(P)
    for l in range(P):
        t[:, l] = at(k, np.full(P, l))
        t[:, P + l] = at(k, np.full(P, -l))
        t[:, P + l, 0] = full[:, 0, l + LOW]
        t[:, ROWB, l] = full[:, 0, LOW - l]
    for slot, sign in ((GA1, 1), (GB1, 1), (GA1B, -1), (GB1B, -1)):
        t[:, slot] = at(sign * k, np.full(P, -LOW))
    t[:, GB1, 0] = t[:, GB1B, 0] = full[:, 0, 0]
    parts = []
    for _ in range(3):
        bits = t.view(np.uint32) & np.uint32(0xffff0000)
        parts.append((bits >> 16).astype(np.uint16))
        t = (t - bits.view(f)).astype(f)
    return np.concatenate(parts)


def columns():
    c = np.zeros((P, 16), np.float32)
    c[1:, 0] = 1
    c[:, 1] = -c[:, 0]
    c[:, 2] = np.where(c[:, 0] > 0, 0.5, 1.0)
    c[:, 3] = c[:, 2] / 2
    part = np.arange(P) // CM
    for j, rows in enumerate(((0, 1, 2), (3, 4), (5,))):
        c[:, 4 + j] = np.isin(part, rows)
    c[:, 8:10] = 1
    c[0, 8:12] = 1
    return c


def build(nc, B, x, out, t):
    ctx = ExitStack()
    with ctx:
        def sb(name, shape, dt=F32):
            return ctx.enter_context(nc.sbuf_tensor(name, shape, dt))

        def sem(name):
            return ctx.enter_context(nc.semaphore(name))

        def scratch(name, shape, dt=F32):
            return nc.dram_tensor(name, shape, dt, kind="Internal").ap()

        proj_d = scratch("proj_d", [B, 2 * CM, PIX])
        xe_d = scratch("xe_d", [B, CM, PIX])
        xs_d = scratch("xs_d", [B, 3, CM, PIX], BF16)
        gate_d = scratch("gate_d", [B, P, LPIX])
        pe_d = scratch("pe_d", [B, CM, LPIX])
        rowb_d = scratch("rowb_d", [P, CM])

        Y = sb("Y", [P, YROWS, LW])
        S = sb("S", [P, LPIX])
        X = sb("X", [P, 4, 2, 1024])
        Xf = X[:, :, :, :].rearrange("p s h n -> p (s h n)")
        gains = sb("gains", [P, CM, NSLOT])
        corner = sb("corner", [P, CM, 4])
        fwd = sb("fwd", [P, 2, SIDE])
        inv = sb("inv", [P, 2, SIDE])
        wproj = sb("wproj", [P, 2, 2 * CM])
        wpool = sb("wpool", [P, 2, SIDE])
        cmix = sb("cmix", [CM, SIDE])
        wscan = sb("wscan", [P, 4, P])
        wup = sb("wup", [P, SIDE])
        wstack = sb("wstack", [6 * CM, SIDE], BF16)
        gram = sb("gram", [P, P])
        ones = sb("ones", [P, P])
        taps = sb("taps", [P, 4, P])
        cols = sb("cols", [P, 16])
        vec = sb("vec", [P, 32])
        sums = sb("sums", [P, 224])
        stat = sb("stat", [P, 16])
        bank = ctx.enter_context(nc.psum_tensor("bank", [P, 8, 512], F32))

        kappa, negk, half_h, quart_h = (cols[:, i:i + 1] for i in range(4))
        gnw, gnb = vec[:, 0:2], vec[:, 2:4]
        bd, bv, nbd = [vec[:, 4:5], vec[:, 6:7]], [vec[:, 5:6], vec[:, 7:8]], [vec[:, 8:9], vec[:, 9:10]]
        dw = vec[:, 10:19]
        cw, cb = vec[:, 19:21], vec[:, 21:23]
        wsum = vec[:, 23:24]
        sum_x, sum_xx, cross, sum_xe = sums[:, 0:64], sums[:, 64:128], sums[:, 128:136], sums[:, 136:144]
        rs, cshift = stat[:, 8:9], stat[:, 9:11]
        TE_TAPS = [0, 1, 2, 3]
        VE_TAPS = [4, 5, 6, 7, 8]

        def sv(a, n):
            return S[:, a:a + n]

        basis = [sv(5120 + q * 1024, 1024)[0:GK, :].bitcast(U16).rearrange("p (k n) -> p k n", k=16) for q in range(2)]
        basis16 = [sv(5120 + q * 1024, 1024)[0:GK, :].bitcast(BF16).rearrange("p (k n) -> p k n", k=16) for q in range(2)]
        wgain = [sv(784 + 8 * j, 8)[0:GK, :].bitcast(BF16) for j in range(3)]
        vert = [sv(q * 1024, 1024) for q in range(2)]
        pooled = [sv(2048 + q * 1024, 1024).rearrange("p (h n) -> p h n", h=2) for q in range(2)]
        pstage = [sv(4096 + q * 512, 512) for q in range(2)]
        gstage = [sv(5120 + q * 512, 512) for q in range(2)]
        junk = sv(6144, 1024).bitcast(BF16)
        img = [sv(m * 512, 512).rearrange("p (t n) -> p t n", t=2) for m in range(8)]
        freq = S[:, 4096:8192].rearrange("p (m n) -> p m n", m=8)
        half1 = [sv(8192 + q * 512, 512).rearrange("p (t n) -> p t n", t=2) for q in range(2)]
        half2 = [sv(9216 + q * 512, 512).rearrange("p (t n) -> p t n", t=2) for q in range(2)]
        xe_s = [sv(10240 + q * 512, 512) for q in range(2)]
        parts = [sv(11264 + q * 768, 768).bitcast(BF16).rearrange("p (i n) -> p i n", i=3) for q in range(2)]
        rest = [sv(12800 + q * 512, 512) for q in range(2)]
        small = [sv(13824 + 16 * i, 16) for i in range(8)]
        tmp = [Xf[:, i * 512:(i + 1) * 512] for i in range(8)]
        xe_t = [sv(q * 1024, 1024) for q in range(2)]
        xq_t = [sv(2048 + q * 1024, 1024) for q in range(2)]
        mix = sv(4096, 1024)
        vsum = sv(5120, 512)
        pe_t = sv(6144, 2048)
        lx = [[Xf[:, q * 4096 + a:q * 4096 + a + n] for a, n in
               ((0, 512), (512, 512), (1024, SCAN + 1), (1544, SCAN + 1), (2064, SCAN + 1), (2584, SCAN + 1))]
              for q in range(2)]
        conv, sig, keep, take, fsc, bsc = zip(*lx)

        gload = [Xf[:, q * 2048:(q + 1) * 2048] for q in range(2)]
        gsum = [Xf[:, 4096 + q * 512:4608 + q * 512] for q in range(2)]
        gsig = [Xf[:, 5120 + q * 512:5632 + q * 512] for q in range(2)]

        def lines(a, first):
            if first:
                return a[:, 1:SCAN + 1].rearrange("p (r w) -> p r w", w=LINE)[:, :, 0:LOW]
            return a[:, 0:SCAN + 1:LINE]

        VW = 8 * LW
        vup = [sv(q * VW, VW).rearrange("p (i a w) -> p i a w", i=4, a=2) for q in range(2)]
        up = [sv(2 * VW + q * 2048, 2048) for q in range(2)]
        stack = [S[0:6 * CM, 2 * VW + 4096 + q * 1024:2 * VW + 4096 + (q + 1) * 1024].bitcast(BF16) for q in range(2)]

        names = """consts_in basis_in0 basis_in1 gain_ps gain_t rowb_out rowb_in ve_setup te_setup mv_setup
        x_in0 x_in1 x_in2 x_in3 x_out0 x_out1 x_out2 x_out3
        proj_ps lowp_ps pool_done square_done proj_st y_ev g_st proj_out0 proj_out1 gate_out0 gate_out1 ve_pool
        img_in0 img_in1 s1_ps s2_ps s3_ps s4_ps h1_st f_st h2_st xe_st parts_done xe_out0 xe_out1
        uv_ready sq_ready m_ready root_ready ew_done ve_ew pl_parts
        st_in0 st_in1 gram_ps st_done ve_stat pe_out tot_in tot_ps var_root norm_set
        pads_done pe_in corr_ps corr_add norm_done conv_ps conv_done sig_done s_ready z_ps gates_done
        scans_done merged take_done ve_l1 pl_l1 gate_in0 gate_in1 gcorr_ps gcorr_add gsig_done gated edge_done
        up_rows up_ready up_ps added stack_in0 stack_in1 ve_up
        end_project end_fourier end_stats end_layer end_out held stores_set"""
        s = {n: sem(n) for n in names.split()}
        RING2 = "lowp_ps proj_ps proj_st y_ev g_st s1_ps s2_ps s3_ps s4_ps h1_st f_st h2_st xe_st parts_done st_done corr_add " \
                "conv_ps conv_done gates_done scans_done merged gcorr_add gcorr_ps corr_ps gsig_done gated s_ready up_ps up_ready pool_done square_done".split()

        def ready(n):
            return n + 3

        def freed(n):
            return n + 1

        class Steps:
            def __init__(self, eng, name, base):
                self.eng, self.name, self.base, self.n = eng, name, base, 0

            def done(self, ins):
                ins.then_inc(s[self.name], 1)
                self.n += 1

            def wait(self):
                self.eng.wait_ge(s[self.name], self.base + self.n)

        def credit(eng, *which):
            for n in which:
                assert n in RING2
                eng.sem_inc(s[n], 2)

        for_stores = ["x_out0", "x_out1", "x_out2", "x_out3", "proj_out0", "proj_out1", "gate_out0", "gate_out1", "xe_out0", "xe_out1"]

        def hold(eng):
            eng.sem_inc(s["held"], 1)

        def leave(eng, phase, b):
            eng.drain().then_inc(s[phase], 1)
            eng.wait_ge(s[phase], 4 * b + 4)
            hold(eng)

        block = ctx.enter_context(nc.Block())
        EW = 18

        FOURIER_ORDER = [("forward", 0), ("forward", 1), ("inverse", 0), ("forward", 2), ("inverse", 1), ("forward", 3), ("inverse", 2), ("inverse", 3)]

        @block.sync
        def _(sp):
            for n in for_stores:
                sp.sem_inc(s[n], 16)
            sp.sem_inc(s["stores_set"], 1)
            pairs = [(fwd[:, :, :], t["fwd"].rearrange("(t p) n -> p t n", p=P)),
                     (inv[:, :, :], t["inv"].rearrange("(t p) n -> p t n", p=P)),
                     (wproj[:, :, :], t["wproj"].rearrange("(t p) n -> p t n", p=P)),
                     (wpool[:, :, :], t["w_in1"].rearrange("(t p) n -> p t n", p=P)),
                     (wscan[:, :, :], t["wscan"].rearrange("(t p) n -> p t n", p=P)),
                     (wup[:, :], t["w_out1"]), (cols[:, :], t["cols"]), (vec[:, 0:19], t["vec"]),
                     (S[:, 0:256].rearrange("p (t n) -> p t n", t=2), t["wtile"].rearrange("(t p) n -> p t n", p=P)),
                     (S[0:6 * CM, 256:512], t["wrep"]), (S[:, 512:640], t["block"]), (S[:, 640:768], t["ident"]),
                     (S[0:GK, 768:784], t["wgain"])]
            for dst, src in pairs:
                sp.dma_start(dst, src).then_inc(s["consts_in"], 16)
            with sp.Fori(0, (NSLOT // 16 - 1) // 2) as i:
                for q in range(2):
                    sp.wait_ge(s["gain_ps"], 2 * i + q + 1)
                    sp.dma_start(basis[q], t["basis"][:, bass.ds(32 * i + 16 * q, 16), :])\
                      .then_inc(s[f"basis_in{q}"], 16)
            sp.wait_ge(s["gain_ps"], NSLOT // 16)
            sp.dma_start(basis[0], t["basis"][:, NSLOT - 16:NSLOT, :]).then_inc(s["basis_in0"], 16)
            sp.wait_ge(s["gain_t"], NSLOT // 16 + 1)
            sp.dma_start(rowb_d, gains[:, :, ROWB], allow_slow_non_contiguous=True).then_inc(s["rowb_out"], 16)
            sp.wait_ge(s["rowb_out"], 16)
            sp.dma_start(S[0:1, 1024:1024 + P * CM].rearrange("o (m l) -> o m l", l=P), rowb_d.rearrange("(o l) m -> o m l", o=1),
                         allow_slow_non_contiguous=True).then_inc(s["rowb_in"], 16)

            with sp.Fori(0, B) as b:
                for c in range(4):
                    sp.wait_ge(s[f"x_out{c}"], 256 * b + 16)
                hold(sp)
                def load_chunk(i, c):
                    n = b * 64 + i * 4 + c
                    sp.wait_ge(s["proj_ps"], b * 32 + i * 2 + c // 2 + 1)
                    hold(sp)
                    sp.wait_ge(s["pool_done"], n + 1)
                    sp.wait_ge(s["square_done"], n + 1)
                    hold(sp)
                    sp.dma_start(X[:, c, :, :], x[b, :, bass.ds(i * 4096 + c * 1024, 1024)].rearrange("(h p) n -> p h n", p=P))\
                      .then_inc(s[f"x_in{c}"], 16)

                def store_gate(i, q):
                    sp.wait_ge(s["g_st"], ready(b * 32 + 2 * i + q))
                    hold(sp)
                    sp.dma_start(gate_d[b, :, bass.ds(i * 1024 + q * 512, 512)], gstage[q]).then_inc(s[f"gate_out{q}"], 16)
                for c in range(4):
                    load_chunk(0, c)
                with sp.Fori(1, 16) as i:
                    for q in range(2):
                        load_chunk(i, 2 * q)
                        load_chunk(i, 2 * q + 1)
                        store_gate(i - 1, q)
                for q in range(2):
                    store_gate(15, q)
                for q in range(2):
                    sp.wait_ge(s[f"gate_out{q}"], 256 * b + 256 + 16)
                hold(sp)
                sp.wait_ge(s["end_project"], 4 * b + 4)
                hold(sp)
                n0 = b * 16
                for gr in range(4):
                    if gr >= 2:
                        sp.wait_ge(s["s1_ps"], 2 + n0 + 4 * (gr - 1))
                        hold(sp)
                    for j in range(4):
                        c = 4 * gr + j
                        sp.dma_start(img[c % 8], proj_d[b, c, :].rearrange("(t p n) -> p t n", t=2, p=P)).then_inc(s[f"img_in{gr % 2}"], 16)
                for c in range(CM):
                    sp.wait_ge(s["parts_done"], ready(n0 + c))
                    hold(sp)
                    sp.dma_start(xe_d[b, c, :].rearrange("(t p n) -> p t n", t=2, p=P),
                                 xe_s[c % 2].rearrange("p (t n) -> p t n", t=2)).then_inc(s[f"xe_out{c % 2}"], 16)
                    for i in range(3):
                        sp.dma_start(xs_d[b, i, c, :].rearrange("(t p n) -> p t n", t=2, p=P),
                                     parts[c % 2][:, i, :].rearrange("p (t n) -> p t n", t=2)).then_inc(s[f"xe_out{c % 2}"], 16)
                for q in range(2):
                    sp.wait_ge(s[f"xe_out{q}"], 512 * b + 512 + 16)
                sp.wait_ge(s["end_fourier"], 4 * b + 4)
                hold(sp)
                with sp.Fori(0, 4) as i:
                    for q in range(2):
                        n = b * 8 + 2 * i + q
                        sp.wait_ge(s["st_done"], freed(n))
                        px = bass.ds(i * 2048 + q * 1024, 1024)
                        for dst, src in ((xe_t[q], xe_d[b]), (xq_t[q], proj_d[b, CM:2 * CM])):
                            sp.dma_start(dst, src.rearrange("m (g n) -> g m n", g=8)[:, :, px]).then_inc(s[f"st_in{q}"], 16)
                sp.wait_ge(s["st_done"], ready(b * 8 + 7))
                sp.dma_start(pe_d[b].rearrange("m (g n) -> g m n", g=8), pe_t).then_inc(s["pe_out"], 16)
                sp.wait_ge(s["pe_out"], 16 * b + 16)
                sp.wait_ge(s["end_stats"], 4 * b + 4)
                hold(sp)
                sp.dma_start(S[0:CM, :], pe_d[b]).then_inc(s["pe_in"], 16)
                sp.wait_ge(s["z_ps"], b * 64 + 64)
                hold(sp)
                sp.dma_start(S[0:CM, :], pe_d[b]).then_inc(s["pe_in"], 16)
                sp.wait_ge(s["merged"], ready(b * 64 + 63))
                hold(sp)

                def load_gate(i, q):
                    sp.dma_start(gload[q], gate_d[b, :, bass.ds(i * 4096 + q * 2048, 2048)]).then_inc(s[f"gate_in{q}"], 16)
                load_gate(0, 0)
                load_gate(0, 1)
                with sp.Fori(1, 4) as i:
                    for q in range(2):
                        sp.wait_ge(s["gcorr_add"], ready(b * 32 + 8 * i + 4 * q - 5))
                        hold(sp)
                        load_gate(i, q)
                sp.wait_ge(s["end_layer"], 4 * b + 4)
                hold(sp)
                with sp.Fori(0, 16) as i:
                    for q in range(2):
                        n = b * 32 + 2 * i + q
                        sp.wait_ge(s["up_ps"], freed(n))
                        px = bass.ds(i * 4096 + q * 2048, 2048)
                        sp.dma_start(stack[q][0:48, :], xs_d[b, 0:3, :, px].rearrange("i m n -> (i m) n")).then_inc(s[f"stack_in{q}"], 16)
                        sp.dma_start(stack[q][48:80, :], xs_d[b, 0:2, :, px].rearrange("i m n -> (i m) n")).then_inc(s[f"stack_in{q}"], 16)
                        sp.dma_start(stack[q][80:96, :], xs_d[b, 0, :, px]).then_inc(s[f"stack_in{q}"], 16)
                        for e in range(2):
                            c = 2 * q + e
                            sp.wait_ge(s[f"x_out{c}"], 256 * b + 16 * i + 16)
                            hold(sp)
                            sp.dma_start(X[:, c, :, :], x[b, :, bass.ds(i * 4096 + c * 1024, 1024)].rearrange("(h p) n -> p h n", p=P))\
                              .then_inc(s[f"x_in{c}"], 16)
                sp.wait_ge(s["end_out"], 4 * b + 4)
                hold(sp)

        @block.tensor
        def _(pe):
            mm = nc.tensor.matmul
            credit(pe, "proj_ps", "lowp_ps", "s1_ps", "s2_ps", "s3_ps", "s4_ps", "corr_ps", "conv_ps", "gcorr_ps", "up_ps")
            pe.sem_inc(s["gain_ps"], 2)
            pe.wait_ge(s["consts_in"], 16 * 13)
            pe.wait_ge(s["ve_setup"], 5)

            def gain_chunk(q, n, loads):
                pe.wait_ge(s[f"basis_in{q}"], loads)
                pe.wait_ge(s["gain_t"], n + 1)
                for k in range(16):
                    for j in range(3):
                        last = mm(bank[:, q, k * CM:(k + 1) * CM], basis16[q][:, k, :], wgain[j], start=j == 0, stop=j == 2)
                last.then_inc(s["gain_ps"], 1)
            with pe.Fori(0, (NSLOT // 16 - 1) // 2) as i:
                for q in range(2):
                    gain_chunk(q, 2 * i + q, 16 * i + 16)
            gain_chunk(0, NSLOT // 16 - 1, 16 * ((NSLOT // 16 - 1) // 2) + 16)
            pe.wait_ge(s["ve_setup"], 8)
            for o in range(2):
                for v, col in ((gnw, 0), (gnb, 2)):
                    for h in range(2):
                        mm(bank[:, 2, col + o:col + o + 1], S[:, 2304 + 1024 + h * SIDE + o * P:2304 + 1024 + h * SIDE + (o + 1) * P],
                           v[:, h:h + 1], start=h == 0, stop=h == 1)
            for h in range(2):
                mm(bank[:, 3, 0:1], S[:, h * P:(h + 1) * P], ones[:, 0:1], start=h == 0, stop=h == 1)
            for h in range(2):
                mm(bank[:, 4, 0:P], S[:, h * P:(h + 1) * P], S[:, h * P:(h + 1) * P], start=h == 0, stop=h == 1)
            for h in range(2):
                last = mm(bank[0:CM, 5, 0:SIDE], wproj[:, h, CM:2 * CM], wpool[:, h, :], start=h == 0, stop=h == 1)
            last.then_inc(s["te_setup"], 1)
            pe.wait_ge(s["mv_setup"], 1)

            with pe.Fori(0, B) as b:
                def project(i, q):
                    n = b * 32 + 2 * i + q
                    pe.wait_ge(s["proj_st"], freed(n))
                    for e in range(2):
                        pe.wait_ge(s[f"x_in{2 * q + e}"], 512 * b + 16 * i + 16)
                    for h in range(2):
                        for k in range(4):
                            last = mm(bank[32 * k:32 * k + 32, q, :], wproj[:, h, :], X[:, 2 * q + k // 2, h, (k % 2) * 512:(k % 2) * 512 + 512],
                                      start=h == 0, stop=h == 1)
                    last.then_inc(s["proj_ps"], 1)

                def project_low(i, q):
                    n = b * 32 + 2 * i + q
                    pe.wait_ge(s["pool_done"], 4 + 2 * n + 2)
                    pe.wait_ge(s["y_ev"], freed(n))
                    pe.wait_ge(s["g_st"], freed(n))
                    for o in range(2):
                        for h in range(2):
                            last = mm(bank[:, 2 + 2 * o + q, :], wpool[:, h, o * P:(o + 1) * P], pooled[q][:, h, :], start=h == 0, stop=h == 1)
                    last.then_inc(s["lowp_ps"], 1)
                project(0, 0)
                with pe.Fori(0, 15) as i:
                    project(i, 1)
                    project_low(i, 0)
                    project(i + 1, 0)
                    project_low(i, 1)
                project(15, 1)
                project_low(15, 0)
                project_low(15, 1)
                leave(pe, "end_project", b)
                n0 = b * 16

                def forward1(c):
                    pe.wait_ge(s["h1_st"], freed(n0 + c))
                    for tx in range(2):
                        for ty in range(2):
                            last = mm(bank[:, c % 2, tx * SIDE:(tx + 1) * SIDE], img[c % 8][:, ty, tx * P:(tx + 1) * P], fwd[:, ty, :],
                                      start=ty == 0, stop=ty == 1)
                    last.then_inc(s["s1_ps"], 1)

                def forward2(c):
                    pe.wait_ge(s["h1_st"], ready(n0 + c))
                    pe.wait_ge(s["f_st"], freed(n0 + c))
                    for tk in range(2):
                        for tx in range(2):
                            last = mm(bank[:, 2 + c % 2, tk * SIDE:(tk + 1) * SIDE], half1[c % 2][:, tx, tk * P:(tk + 1) * P], fwd[:, tx, :],
                                      start=tx == 0, stop=tx == 1)
                    last.then_inc(s["s2_ps"], 1)

                def inverse1(c):
                    pe.wait_ge(s["h2_st"], freed(n0 + c))
                    for tl in range(2):
                        for tk in range(2):
                            a = tk * SIDE + tl * P
                            last = mm(bank[:, 4 + c % 2, tl * SIDE:(tl + 1) * SIDE], freq[:, c % 8, a:a + P], inv[:, tk, :],
                                      start=tk == 0, stop=tk == 1)
                    last.then_inc(s["s3_ps"], 1)

                def inverse2(c):
                    pe.wait_ge(s["h2_st"], ready(n0 + c))
                    pe.wait_ge(s["xe_st"], freed(n0 + c))
                    for ty in range(2):
                        for tl in range(2):
                            last = mm(bank[:, 6 + c % 2, ty * SIDE:(ty + 1) * SIDE], half2[c % 2][:, tl, ty * P:(ty + 1) * P], inv[:, tl, :],
                                      start=tl == 0, stop=tl == 1)
                    last.then_inc(s["s4_ps"], 1)

                def group(gr, first, second):
                    for j in range(4):
                        first(4 * gr + j)
                        if j:
                            second(4 * gr + j - 1)
                    second(4 * gr + 3)
                for way, gr in FOURIER_ORDER:
                    if way == "forward":
                        pe.wait_ge(s[f"img_in{gr % 2}"], 128 * b + 64 * (gr // 2) + 64)
                        group(gr, forward1, forward2)
                    else:
                        pe.wait_ge(s["ew_done"], b * 4 + gr + 2)
                        group(gr, inverse1, inverse2)
                leave(pe, "end_fourier", b)
                with pe.Fori(0, 4) as i:
                    for q in range(2):
                        n = b * 8 + 2 * i + q
                        pe.wait_ge(s[f"st_in{q}"], 128 * b + 32 * i + 32)
                        pe.wait_ge(s["st_done"], freed(n))
                        for k in range(2):
                            last = mm(bank[:, 2 * q + k, :], gram[:, :], xe_t[q][:, k * 512:(k + 1) * 512], start=True, stop=True)
                        last.then_inc(s["gram_ps"], 1)
                pe.wait_ge(s["tot_in"], b + 1)
                mm(bank[:, 4, 0:2], ones[:, :], stat[:, 0:2], start=True, stop=True).then_inc(s["tot_ps"], 1)
                leave(pe, "end_stats", b)
                pe.wait_ge(s["pe_in"], 32 * b + 16)
                hold(pe)
                with pe.Fori(0, 16) as i:
                    for q in range(2):
                        n = b * 32 + 2 * i + q
                        pe.wait_ge(s["corr_add"], freed(n))
                        mm(bank[:, 6 + q, :], cmix[:, 0:P], S[0:CM, bass.ds(i * 1024 + q * 512, 512)], start=True, stop=True).then_inc(s["corr_ps"], 1)

                def gates_of(w, q, n, rhs):
                    pe.wait_ge(s["gates_done"], freed(n))
                    pe.wait_ge(s["scans_done"], freed(n))
                    mm(bank[:, 2 + q, :], wscan[:, 2 * w, :], rhs, start=True, stop=True)
                    mm(bank[:, 4 + q, :], wscan[:, 2 * w + 1, :], rhs, start=True, stop=True).then_inc(s["z_ps"], 1)
                pe.wait_ge(s["pads_done"], 4 * b + 4)
                hold(pe)
                def conv_taps(i):
                    for q in range(2):
                        c = b * 32 + 2 * i + q
                        pe.wait_ge(s["norm_done"], c + b + 2)
                        pe.wait_ge(s["conv_done"], freed(c))
                        for k, tap in enumerate(TE_TAPS):
                            rhs = Y[:, bass.ds(8 * i + 4 * q + 1 + tap // 3, 4), tap % 3:tap % 3 + LOW]
                            last = mm(bank[:, q, :], taps[:, k, :], rhs, start=k == 0, stop=k == len(TE_TAPS) - 1)
                        last.then_inc(s["conv_ps"], 1)

                def row_gates(i):
                    for q in range(2):
                        pe.wait_ge(s["s_ready"], ready(b * 32 + 2 * i + q))
                        gates_of(0, q, b * 64 + 2 * i + q, S[:, bass.ds(i * 1024 + q * 512, 512)])
                conv_taps(0)
                with pe.Fori(1, 16) as i:
                    conv_taps(i)
                    row_gates(i - 1)
                row_gates(15)
                sc = S[:, :].rearrange("p (r w) -> p w r", w=LOW)
                with pe.Fori(0, 16) as i:
                    for q in range(2):
                        pe.wait_ge(s["s_ready"], ready(b * 32 + 31))
                        gates_of(1, q, b * 64 + 32 + 2 * i + q, sc[:, bass.ds(8 * i + 4 * q, 4), :])
                pe.wait_ge(s["pe_in"], 32 * b + 32)
                hold(pe)
                with pe.Fori(0, 16) as i:
                    for q in range(2):
                        n = b * 32 + 2 * i + q
                        pe.wait_ge(s["gcorr_add"], freed(n))
                        mm(bank[:, 6 + q, :], cmix[:, P:2 * P], S[0:CM, bass.ds(i * 1024 + q * 512, 512)], start=True, stop=True).then_inc(s["gcorr_ps"], 1)
                leave(pe, "end_layer", b)
                with pe.Fori(0, 16) as i:
                    for q in range(2):
                        n = b * 32 + 2 * i + q
                        pe.wait_ge(s["up_ready"], ready(n))
                        pe.wait_ge(s[f"stack_in{q}"], 768 * b + 48 * i + 48)
                        for e in range(2):
                            for h in range(2):
                                k = 2 * e + h
                                pe.wait_ge(s["added"], 4 * n + k + 1)
                                for j in range(2):
                                    px = slice(e * 1024 + j * 512, e * 1024 + j * 512 + 512)
                                    mm(bank[:, 2 * k + j, :], wup[:, h * P:(h + 1) * P], up[q][:, px], start=True, stop=False)
                                    last = mm(bank[:, 2 * k + j, :], wstack[:, h * P:(h + 1) * P], stack[q][:, px], start=False, stop=True)
                                if k < 3:
                                    last.then_inc(s["ve_up"], 1)
                                else:
                                    last.then_inc(s["up_ps"], 1)
                leave(pe, "end_out", b)

        @block.scalar
        def _(act):
            A = nc.scalar.activation
            credit(act, "square_done", "square_done", "proj_st", "h1_st", "f_st", "h2_st", "xe_st", "gates_done", "gsig_done")
            act.sem_inc(s["gain_t"], 1)
            act.wait_ge(s["stores_set"], 1)

            def tanh_chunk(q, n, at):
                act.wait_ge(s["gain_ps"], 2 + n + 1)
                A(gains[:, :, at], bank[:, q, 0:16 * CM].rearrange("p (k m) -> p m k", m=CM), ACT.Tanh).then_inc(s["gain_t"], 1)
            with act.Fori(0, (NSLOT // 16 - 1) // 2) as i:
                for q in range(2):
                    tanh_chunk(q, 2 * i + q, bass.ds(32 * i + 16 * q, 16))
            tanh_chunk(0, NSLOT // 16 - 1, slice(NSLOT - 16, NSLOT))
            act.wait_ge(s["mv_setup"], 1)

            with act.Fori(0, B) as b:
                with act.Fori(0, 16) as i:
                    for q in range(2):
                        n = b * 32 + 2 * i + q
                        for e in range(2):
                            c = 2 * q + e
                            act.wait_ge(s[f"x_in{c}"], 512 * b + 16 * i + 16)
                            act.wait_ge(s["square_done"], 4 + n * 2 + e)
                            A(junk, X[:, c, :, :].rearrange("p h n -> p (h n)"), ACT.Square,
                              accum_out=sum_xx[:, bass.ds(4 * i + c, 1)]).then_inc(s["square_done"], 1)
                        act.wait_ge(s["proj_ps"], ready(n))
                        act.wait_ge(s[f"proj_out{q}"], 16 * (b * 16 + i) + 16)
                        A(pstage[q], bank[:, q, :], ACT.Copy).then_inc(s["proj_st"], 1)
                        act.wait_ge(s["proj_st"], ready(n))
                        act.dma_start(proj_d[b, :, bass.ds(i * 4096 + q * 2048, 2048)].rearrange("m (k n) -> k m n", k=4), pstage[q])\
                           .then_inc(s[f"proj_out{q}"], 16)
                for q in range(2):
                    act.wait_ge(s[f"proj_out{q}"], 256 * (b + 1) + 16)
                hold(act)
                leave(act, "end_project", b)
                n0, g0 = b * 16, b * 4

                def copy_forward(c):
                    act.wait_ge(s["s1_ps"], ready(n0 + c))
                    act.wait_ge(s["s2_ps"], freed(n0 + c))
                    A(half1[c % 2], bank[:, c % 2, :].rearrange("p (t n) -> p t n", t=2), ACT.Copy).then_inc(s["h1_st"], 1)
                    act.wait_ge(s["s2_ps"], ready(n0 + c))
                    A(freq[:, c % 8, :], bank[:, 2 + c % 2, :], ACT.Copy).then_inc(s["f_st"], 1)

                def copy_inverse(c):
                    act.wait_ge(s["s3_ps"], ready(n0 + c))
                    act.wait_ge(s["s4_ps"], freed(n0 + c))
                    A(half2[c % 2], bank[:, 4 + c % 2, :].rearrange("p (t n) -> p t n", t=2), ACT.Copy).then_inc(s["h2_st"], 1)
                    act.wait_ge(s["s4_ps"], ready(n0 + c))
                    act.wait_ge(s[f"xe_out{c % 2}"], 64 * (b * 8 + c // 2) + 16)
                    A(parts[c % 2][:, 0, :], bank[:, 6 + c % 2, :], ACT.Copy)
                    A(xe_s[c % 2], bank[:, 6 + c % 2, :], ACT.Copy).then_inc(s["xe_st"], 1)

                def squares(gr):
                    act.wait_ge(s["uv_ready"], g0 + gr + 1)
                    for k in range(4):
                        last = A(tmp[4 + k], tmp[k], ACT.Square)
                    last.then_inc(s["sq_ready"], 1)

                def roots(gr):
                    act.wait_ge(s["m_ready"], g0 + gr + 1)
                    for v in (tmp[4], tmp[5], small[2]):
                        last = A(v, v, ACT.Abs_reciprocal_sqrt)
                    last.then_inc(s["root_ready"], 1)
                applied = 0
                for at, (way, gr) in enumerate(FOURIER_ORDER):
                    between = applied < 4 and at in (1, 2, 4, 6)
                    for j in range(4):
                        (copy_forward if way == "forward" else copy_inverse)(4 * gr + j)
                        if between and j == 0:
                            squares(applied)
                        if between and j == 2:
                            roots(applied)
                            applied += 1
                leave(act, "end_fourier", b)
                act.wait_ge(s["tot_ps"], b + 1)
                act.wait_ge(s["norm_set"], b + 1)
                A(stat[:, 5:6], stat[:, 4:5], ACT.Sqrt).then_inc(s["var_root"], 1)
                leave(act, "end_stats", b)
                with act.Fori(0, 16) as i:
                    for q in range(2):
                        act.wait_ge(s["corr_add"], ready(b * 32 + 2 * i + q))
                        v = Y[:, bass.ds(8 * i + 4 * q + 2, 4), 1:1 + LOW]
                        A(v, v, ACT.Identity, scale=rs, bias=cshift[:, 0:1]).then_inc(s["norm_done"], 1)
                act.drain().then_inc(s["norm_done"], 1)

                def gates(w, q, n):
                    act.wait_ge(s["z_ps"], n + 1)
                    act.wait_ge(s["scans_done"], freed(n))
                    z = bank[:, 2 + q, :].rearrange("p (r w) -> p r w", w=LOW)
                    A(lines(keep[q], 1), z, ACT.Sigmoid, scale=-1.0, bias=nbd[w])
                    A(lines(take[q], 1), z, ACT.Sigmoid, bias=bd[w]).then_inc(s["gates_done"], 1)
                act.wait_ge(s["pads_done"], 4 * b + 4)
                def conv_sigmoid(i):
                    for q in range(2):
                        n = b * 32 + 2 * i + q
                        act.wait_ge(s["conv_done"], ready(n))
                        act.wait_ge(s["s_ready"], freed(n))
                        A(sig[q], conv[q], ACT.Sigmoid).then_inc(s["sig_done"], 1)

                def row_gates(i):
                    for q in range(2):
                        gates(0, q, b * 64 + 2 * i + q)
                conv_sigmoid(0)
                with act.Fori(1, 16) as i:
                    conv_sigmoid(i)
                    row_gates(i - 1)
                row_gates(15)
                with act.Fori(0, 16) as i:
                    for q in range(2):
                        gates(1, q, b * 64 + 32 + 2 * i + q)
                with act.Fori(0, 16) as i:
                    for q in range(2):
                        n = b * 32 + 2 * i + q
                        act.wait_ge(s["gcorr_add"], ready(n))
                        act.wait_ge(s["gated"], freed(n))
                        A(gsig[q], gsum[q], ACT.Sigmoid, scale=rs, bias=cshift[:, 1:2]).then_inc(s["gsig_done"], 1)
                leave(act, "end_layer", b)
                with act.Fori(0, 16) as i:
                    for c in range(4):
                        act.wait_ge(s["added"], 4 + b * 128 + i * 8 + 2 * c + 2)
                        act.dma_start(out[b, :, bass.ds(i * 4096 + c * 1024, 1024)].rearrange("(h p) n -> p h n", p=P), X[:, c, :, :])\
                           .then_inc(s[f"x_out{c}"], 16)
                leave(act, "end_out", b)
            for c in range(4):
                act.wait_ge(s[f"x_out{c}"], 256 * B + 16)

        @block.gpsimd
        def _(pool):
            g = nc.gpsimd
            credit(pool, "parts_done", "merged", "gated", "s_ready")
            pool.wait_ge(s["mv_setup"], 1)
            pool.wait_ge(s["stores_set"], 1)
            with pool.Fori(0, B) as b:
                leave(pool, "end_project", b)
                for c in range(CM):
                    q = c % 2
                    pool.wait_ge(s["xe_st"], ready(b * 16 + c))
                    g.tensor_tensor(rest[q], xe_s[q], parts[q][:, 0, :], ALU.subtract)
                    g.tensor_tensor(parts[q][:, 1, :], xe_s[q], parts[q][:, 0, :], ALU.subtract).then_inc(s["pl_parts"], 1)
                    pool.wait_ge(s["pl_parts"], b * 16 + c + 1)
                    g.tensor_tensor(parts[q][:, 2, :], rest[q], parts[q][:, 1, :], ALU.subtract).then_inc(s["parts_done"], 1)
                leave(pool, "end_fourier", b)
                leave(pool, "end_stats", b)
                pool.memset(Y[:, 2:2 + LOW, 0:1], 0.0)
                pool.memset(Y[:, 2:2 + LOW, LW - 1:LW], 0.0)
                pool.memset(Y[:, 1, :], 0.0)
                pool.memset(Y[:, YROWS - 1, :], 0.0)
                for q in range(2):
                    pool.memset(lines(keep[q], 0), 0.0).then_inc(s["pads_done"], 1)
                    pool.memset(lines(take[q], 0), 0.0).then_inc(s["pads_done"], 1)
                def silu(i):
                    for q in range(2):
                        pool.wait_ge(s["sig_done"], b * 32 + 2 * i + q + 1)
                        g.tensor_tensor(S[:, bass.ds(i * 1024 + q * 512, 512)], conv[q], sig[q], ALU.mult).then_inc(s["s_ready"], 1)

                def merge(i):
                    for q in range(2):
                        pool.wait_ge(s["scans_done"], ready(b * 64 + 2 * i + q))
                        g.tensor_tensor(Y[:, bass.ds(8 * i + 4 * q + 1, 4), 1:1 + LOW], lines(fsc[q], 1), lines(bsc[q], 1), ALU.add)\
                         .then_inc(s["merged"], 1)
                silu(0)
                with pool.Fori(1, 16) as i:
                    silu(i)
                    merge(i - 1)
                merge(15)
                yc = Y[:, 1:1 + LOW, :].rearrange("p r w -> p w r")
                with pool.Fori(0, 16) as i:
                    for q in range(2):
                        n = 2 * i + q
                        pool.wait_ge(s["scans_done"], ready(b * 64 + 32 + n))
                        g.tensor_tensor(lines(fsc[q], 1), lines(fsc[q], 1), lines(bsc[q], 1), ALU.add).then_inc(s["pl_l1"], 1)
                        pool.wait_ge(s["pl_l1"], b * 32 + n + 1)
                        v = yc[:, bass.ds(8 * i + 4 * q + 1, 4), :]
                        g.tensor_tensor(v, v, lines(fsc[q], 1), ALU.add).then_inc(s["merged"], 1)
                with pool.Fori(0, 16) as i:
                    for q in range(2):
                        pool.wait_ge(s["gsig_done"], ready(b * 32 + 2 * i + q))
                        v = Y[:, bass.ds(8 * i + 4 * q + 1, 4), 1:1 + LOW]
                        g.tensor_tensor(v, v, gsig[q].rearrange("p (r w) -> p r w", w=LOW), ALU.mult).then_inc(s["gated"], 1)
                leave(pool, "end_layer", b)
                leave(pool, "end_out", b)

        @block.vector
        def _(dve):
            v = nc.vector
            stt = v.scalar_tensor_tensor
            ts = v.tensor_scalar
            tt = v.tensor_tensor
            credit(dve, "pool_done", "pool_done", "y_ev", "g_st", "st_done", "corr_add", "conv_done", "scans_done", "gcorr_add", "up_ready")
            dve.sem_inc(s["added"], 4)
            dve.sem_inc(s["ew_done"], 1)
            dve.wait_ge(s["stores_set"], 1)
            st = Steps(dve, "ve_setup", 0)
            dve.wait_ge(s["consts_in"], 16 * 13)
            w32, r1 = S[0:GK, 768:784], S[0:GK, 816:832]
            st.done(v.tensor_copy(wgain[0], w32)); st.wait()
            st.done(tt(r1, w32, wgain[0], ALU.subtract)); st.wait()
            st.done(v.tensor_copy(wgain[1], r1)); st.wait()
            st.done(tt(r1, r1, wgain[1], ALU.subtract)); st.wait()
            st.done(v.tensor_copy(wgain[2], r1))
            st.done(v.memset(ones[:, :], 1.0))
            st.done(v.tensor_copy(S[:, 3328:3840].rearrange("p (t n) -> p t n", t=2), wpool[:, :, :]))
            st.wait()
            for h in range(2):
                ins = ts(wpool[:, h, :], wpool[:, h, :], gnw[:, h:h + 1], 0.25, ALU.mult, ALU.mult)
            st.done(ins)
            for w in range(2):
                v.tensor_scalar(nbd[w], bd[w], -1.0, None, ALU.mult)
            for k, tap in enumerate(TE_TAPS):
                ts(taps[:, k, :], S[:, 640:768], dw[:, tap:tap + 1], None, ALU.mult)
            ts(wup[:, :], wup[:, :], 1.0 / 64, None, ALU.mult)
            R = 6 * CM
            w32, p16, acc = S[0:R, 256:512], [S[0:R, 3840 + 128 * j:3968 + 128 * j].bitcast(BF16) for j in range(3)], S[0:R, 4224:4480]
            r1 = S[0:R, 4480:4736]
            st.done(v.tensor_copy(p16[0], w32)); st.wait()
            st.done(tt(r1, w32, p16[0], ALU.subtract)); st.wait()
            st.done(v.tensor_copy(p16[1], r1)); st.wait()
            st.done(tt(r1, r1, p16[1], ALU.subtract)); st.wait()
            st.done(v.tensor_copy(p16[2], r1)); st.wait()
            st.done(ts(acc, p16[0], cols[0:R, 4:5], None, ALU.mult)); st.wait()
            st.done(stt(acc, p16[1], cols[0:R, 5:6], acc, ALU.mult, ALU.add)); st.wait()
            st.done(stt(wstack[:, :], p16[2], cols[0:R, 6:7], acc, ALU.mult, ALU.add))
            dve.wait_ge(s["gain_t"], NSLOT // 16 + 1)
            dve.wait_ge(s["rowb_in"], 16)
            rowb = S[0:1, 1024:1024 + P * CM].rearrange("o (m l) -> o m l", l=P)
            st.done(tt(gains[0:1, :, P:2 * P], gains[0:1, :, P:2 * P], rowb, ALU.add)); st.wait()
            st.done(ts(gains[0:1, :, P:2 * P], gains[0:1, :, P:2 * P], 0.5, None, ALU.mult)); st.wait()
            for j, slot in enumerate((0, None, P, None)):
                if slot is None:
                    st.done(tt(corner[:, :, j], gains[:, :, GA1 + j // 2], gains[:, :, GA1B + j // 2], ALU.add)); st.wait()
                    st.done(ts(corner[:, :, j], corner[:, :, j], 0.25, 1.0, ALU.mult, ALU.add))
                elif slot == 0:
                    st.done(ts(corner[:, :, j], gains[:, :, 0], 0.5, 1.0, ALU.mult, ALU.add))
                else:
                    st.done(ts(corner[:, :, j], gains[:, :, P], 0.5, 1.0, ALU.mult, ALU.add))
            st.wait()
            st.done(ts(gains[:, :, 0:2 * P], gains[:, :, 0:2 * P], quart_h, half_h, ALU.mult, ALU.add))
            dve.wait_ge(s["te_setup"], 1)
            v.tensor_copy(vec[:, 19:23], bank[:, 2, 0:4])
            v.tensor_copy(wsum, bank[:, 3, 0:1])
            tt(gram[:, :], S[:, 512:640], bank[:, 4, 0:P], ALU.mult)
            v.tensor_copy(cmix[:, :], bank[0:CM, 5, 0:SIDE])
            dve.drain().then_inc(s["mv_setup"], 1)

            with dve.Fori(0, B) as b:
                def pool(i, q):
                    n = b * 32 + 2 * i + q
                    for e in range(2):
                        c = 2 * q + e
                        dve.wait_ge(s[f"x_in{c}"], 512 * b + 16 * i + 16)
                        xr = X[:, c, :, :].rearrange("p h (r a w) -> p (h r) a w", a=2, w=SIDE)
                        vr = vert[e].rearrange("p (r w) -> p r w", w=SIDE)
                        tt(vr, xr[:, :, 0, :], xr[:, :, 1, :], ALU.add).then_inc(s["ve_pool"], 1)
                        if e == 0:
                            dve.wait_ge(s["lowp_ps"], freed(n))
                        dve.wait_ge(s["ve_pool"], 2 * n + e + 1)
                        vp = vert[e].rearrange("p (h n a) -> p h n a", h=2, a=2)
                        stt(pooled[q][:, :, e * 256:(e + 1) * 256], vp[:, :, :, 0], 1.0, vp[:, :, :, 1], ALU.mult, ALU.add,
                            accum_out=sum_x[:, bass.ds(4 * i + c, 1)]).then_inc(s["pool_done"], 1)

                def copy_low(i, q):
                    n = b * 32 + 2 * i + q
                    dve.wait_ge(s["lowp_ps"], ready(n))
                    v.tensor_copy(Y[:, bass.ds(8 * i + 4 * q + 2, 4), 1:1 + LOW],
                                  bank[:, 2 + q, :].rearrange("p (r w) -> p r w", w=LOW)).then_inc(s["y_ev"], 1)
                    dve.wait_ge(s[f"gate_out{q}"], 16 * (b * 16 + i) + 16)
                    v.tensor_copy(gstage[q], bank[:, 4 + q, :]).then_inc(s["g_st"], 1)
                pool(0, 0)
                with dve.Fori(0, 15) as i:
                    pool(i, 1)
                    copy_low(i, 0)
                    pool(i + 1, 0)
                    copy_low(i, 1)
                pool(15, 1)
                copy_low(15, 0)
                copy_low(15, 1)
                leave(dve, "end_project", b)
                with dve.Fori(0, 2) as gp:
                    for gi in range(2):
                        grp = b * 4 + gp * 2 + gi
                        step = Steps(dve, "ve_ew", grp * EW)
                        dve.wait_ge(s["ew_done"], grp + 1)
                        dve.wait_ge(s["f_st"], ready(b * 16 + gp * 8 + 4 * gi + 3))
                        fm = freq[:, 4 * gi:4 * gi + 4, :]
                        cc, cs, sc, ss = (fm[:, :, k * P:(k + 1) * P] for k in range(4))
                        edge = fm.rearrange("p m (k l) -> p m k l", l=P)[:, :, :, 0]
                        u, w_, p_, q_ = (tmp[k].rearrange("p (m l) -> p m l", m=4) for k in range(4))
                        z4, sq4, m4, sw4 = (small[k].rearrange("p (m k) -> p m k", m=4) for k in range(4))
                        step.done(v.tensor_copy(z4, edge))
                        stt(u, ss, negk, cc, ALU.mult, ALU.add)
                        stt(w_, cc, kappa, ss, ALU.mult, ALU.add)
                        stt(p_, sc, kappa, cs, ALU.mult, ALU.add)
                        stt(q_, cs, negk, sc, ALU.mult, ALU.add).then_inc(s["uv_ready"], 1)
                        step.wait()
                        step.done(tt(sq4, z4, z4, ALU.mult))
                        step.wait()
                        v.tensor_copy(sw4[:, :, 0:2], sq4[:, :, 2:4])
                        step.done(v.tensor_copy(sw4[:, :, 2:4], sq4[:, :, 0:2]))
                        step.done(ts(small[2], small[1], TINY, None, ALU.max))
                        step.wait()
                        step.done(stt(small[2], small[3], kappa, small[2], ALU.mult, ALU.add))
                        step.wait()
                        step.done(ts(small[4], small[2], TINY, DELTA, ALU.is_le, ALU.mult))
                        dve.wait_ge(s["sq_ready"], grp + 1)
                        step.done(stt(tmp[4], tmp[4], TINY, tmp[6], ALU.max, ALU.add))
                        step.done(stt(tmp[5], tmp[5], TINY, tmp[7], ALU.max, ALU.add))
                        step.wait()
                        step.done(ts(tmp[6], tmp[4], TINY, DELTA, ALU.is_le, ALU.mult))
                        ts(tmp[7], tmp[5], TINY, DELTA, ALU.is_le, ALU.mult).then_inc(s["m_ready"], 1)
                        dve.wait_ge(s["m_ready"], grp + 1)
                        zmask = cols[:, 8:12]
                        for k in range(4):
                            ins = tt(small[5][:, 4 * k:4 * k + 4], small[4][:, 4 * k:4 * k + 4], zmask, ALU.mult)
                        step.done(ins)
                        step.done(tt(tmp[0], tmp[0], tmp[6], ALU.add))
                        step.done(stt(tmp[1], tmp[7], kappa, tmp[1], ALU.mult, ALU.add))
                        step.done(tt(tmp[3][0:1, :], tmp[3][0:1, :], tmp[7][0:1, :], ALU.add))
                        step.wait()
                        step.done(tt(small[0], small[0], small[5], ALU.add))
                        dve.wait_ge(s["root_ready"], grp + 1)
                        ts(tmp[4], tmp[4], FEPS, 1.0, ALU.mult, ALU.add)
                        ts(tmp[5], tmp[5], FEPS, 1.0, ALU.mult, ALU.add)
                        step.done(ts(small[2], small[2], FEPS, 1.0, ALU.mult, ALU.add))
                        step.wait()
                        ch = bass.ds(8 * gp + 4 * gi, 4)
                        gp4, gm4 = (tmp[4 + k].rearrange("p (m l) -> p m l", m=4) for k in range(2))
                        tt(gp4, gp4, gains[:, ch, 0:P], ALU.mult)
                        tt(gm4, gm4, gains[:, ch, P:2 * P], ALU.mult)
                        step.done(tt(m4, m4, corner[:, ch, :], ALU.mult))
                        step.wait()
                        tt(tmp[0], tmp[0], tmp[4], ALU.mult)
                        tt(tmp[2], tmp[2], tmp[4], ALU.mult)
                        tt(tmp[1], tmp[1], tmp[5], ALU.mult)
                        tt(tmp[3], tmp[3], tmp[5], ALU.mult)
                        step.done(tt(small[0], small[0], small[2], ALU.mult))
                        step.wait()
                        stt(cc, w_, kappa, u, ALU.mult, ALU.add)
                        stt(ss, u, negk, w_, ALU.mult, ALU.add)
                        stt(cs, q_, negk, p_, ALU.mult, ALU.add)
                        step.done(stt(sc, p_, kappa, q_, ALU.mult, ALU.add))
                        step.wait()
                        v.tensor_copy(edge, z4).then_inc(s["ew_done"], 1)
                        assert step.n == EW
                leave(dve, "end_fourier", b)
                with dve.Fori(0, 4) as i:
                    step = Steps(dve, "ve_stat", (b * 4 + i) * 6)
                    for q in range(2):
                        n = b * 8 + 2 * i + q
                        dve.wait_ge(s[f"st_in{q}"], 128 * b + 32 * i + 32)
                        xr = xe_t[q].rearrange("p (r a w) -> p r a w", a=2, w=SIDE)
                        step.done(tt(vsum.rearrange("p (r w) -> p r w", w=SIDE), xr[:, :, 0, :], xr[:, :, 1, :], ALU.add))
                        step.wait()
                        vp = vsum.rearrange("p (n a) -> p n a", a=2)
                        step.done(stt(pe_t[:, bass.ds(i * 512 + q * 256, 256)], vp[:, :, 0], 1.0, vp[:, :, 1], ALU.mult, ALU.add,
                                      accum_out=sum_xe[:, bass.ds(2 * i + q, 1)]))
                        dve.wait_ge(s["gram_ps"], n + 1)
                        step.done(stt(mix, xq_t[q], 2.0, bank[:, 2 * q:2 * q + 2, :].rearrange("p k n -> p (k n)"), ALU.mult, ALU.add))
                        step.wait()
                        stt(mix, mix, 1.0, xe_t[q], ALU.mult, ALU.mult, accum_out=cross[:, bass.ds(2 * i + q, 1)]).then_inc(s["st_done"], 1)
                dve.wait_ge(s["st_done"], ready(b * 8 + 7))
                v.reduce_sum(stat[:, 0:1], sum_x, AX.X)
                v.reduce_sum(stat[:, 1:2], sum_xx, AX.X)
                v.reduce_sum(stat[:, 2:3], cross, AX.X)
                v.reduce_sum(stat[:, 3:4], sum_xe, AX.X)
                dve.drain()
                tt(stat[:, 1:2], stat[:, 1:2], stat[:, 2:3], ALU.add)
                stt(stat[:, 0:1], stat[:, 3:4], wsum, stat[:, 0:1], ALU.mult, ALU.add)
                dve.drain().then_inc(s["tot_in"], 1)
                dve.wait_ge(s["tot_ps"], b + 1)
                total = 1.0 / (SIDE * PIX)
                ts(stat[:, 2:4], bank[:, 4, 0:2], total, None, ALU.mult)
                dve.drain()
                tt(stat[:, 6:7], stat[:, 2:3], stat[:, 2:3], ALU.mult)
                dve.drain()
                tt(stat[:, 4:5], stat[:, 3:4], stat[:, 6:7], ALU.subtract)
                dve.drain()
                ts(stat[:, 4:5], stat[:, 4:5], 0.0, GN_EPS, ALU.max, ALU.add)
                dve.drain().then_inc(s["norm_set"], 1)
                dve.wait_ge(s["var_root"], b + 1)
                v.reciprocal(stat[:, 5:6], stat[:, 5:6])
                dve.drain()
                tt(stat[:, 6:7], stat[:, 5:6], stat[:, 5:6], ALU.mult)
                dve.drain()
                tt(stat[:, 6:7], stat[:, 6:7], stat[:, 4:5], ALU.mult)
                dve.drain()
                ts(stat[:, 6:7], stat[:, 6:7], -0.5, 1.5, ALU.mult, ALU.add)
                dve.drain()
                tt(rs, stat[:, 5:6], stat[:, 6:7], ALU.mult)
                dve.drain()
                stt(stat[:, 7:8], stat[:, 2:3], -1.0, rs, ALU.mult, ALU.mult)
                dve.drain()
                stt(cshift, cw, stat[:, 7:8], cb, ALU.mult, ALU.add)
                leave(dve, "end_stats", b)
                with dve.Fori(0, 16) as i:
                    for q in range(2):
                        n = b * 32 + 2 * i + q
                        dve.wait_ge(s["corr_ps"], ready(n))
                        yv = Y[:, bass.ds(8 * i + 4 * q + 2, 4), 1:1 + LOW]
                        tt(yv, yv, bank[:, 6 + q, :].rearrange("p (r w) -> p r w", w=LOW), ALU.add).then_inc(s["corr_add"], 1)

                def scans(w, q, n):
                    dve.wait_ge(s["gates_done"], ready(n))
                    dve.wait_ge(s["merged"], freed(n))
                    tk = lines(take[q], 1)
                    stt(tk, bank[:, 4 + q, :].rearrange("p (r w) -> p r w", w=LOW), bv[w], tk, ALU.add, ALU.mult).then_inc(s["take_done"], 1)
                    dve.wait_ge(s["take_done"], n + 1)
                    v.tensor_tensor_scan(out=fsc[q][:, 0:SCAN], data0=keep[q][:, 0:SCAN], data1=take[q][:, 0:SCAN],
                                         initial=0.0, op0=ALU.mult, op1=ALU.add)
                    v.tensor_tensor_scan(out=bsc[q][:, 1:SCAN + 1][:, ::-1], data0=keep[q][:, 1:SCAN + 1][:, ::-1],
                                         data1=take[q][:, 1:SCAN + 1][:, ::-1], initial=0.0, op0=ALU.mult, op1=ALU.add)\
                     .then_inc(s["scans_done"], 1)
                NV = 2 * (len(VE_TAPS) - 1)
                dve.wait_ge(s["pads_done"], 4 * b + 4)
                hold(dve)

                def convolve(i):
                    base = (b * 16 + i) * NV
                    for q in range(2):
                        dve.wait_ge(s["norm_done"], b * 33 + 2 * i + q + 2)
                        dve.wait_ge(s["conv_ps"], ready(b * 32 + 2 * i + q))
                        dve.wait_ge(s["s_ready"], freed(b * 32 + 2 * i + q))
                    for k, tap in enumerate(VE_TAPS):
                        for q in range(2):
                            if k:
                                dve.wait_ge(s["ve_l1"], base + 2 * (k - 1) + q + 1)
                            src = Y[:, bass.ds(8 * i + 4 * q + 1 + tap // 3, 4), tap % 3:tap % 3 + LOW]
                            acc = (conv[q] if k else bank[:, q, :]).rearrange("p (r w) -> p r w", w=LOW)
                            stt(conv[q].rearrange("p (r w) -> p r w", w=LOW), src, dw[:, tap:tap + 1], acc, ALU.mult, ALU.add)\
                                .then_inc(s["ve_l1" if k < len(VE_TAPS) - 1 else "conv_done"], 1)

                def row_scans(i):
                    for q in range(2):
                        scans(0, q, b * 64 + 2 * i + q)
                convolve(0)
                with dve.Fori(1, 16) as i:
                    convolve(i)
                    row_scans(i - 1)
                row_scans(15)
                with dve.Fori(0, 16) as i:
                    for q in range(2):
                        scans(1, q, b * 64 + 32 + 2 * i + q)
                with dve.Fori(0, 4) as i:
                    for q in range(2):
                        dve.wait_ge(s[f"gate_in{q}"], 64 * b + 16 * i + 16)
                        for k in range(4):
                            n = b * 32 + 8 * i + 4 * q + k
                            dve.wait_ge(s["gcorr_ps"], ready(n))
                            dve.wait_ge(s["gsig_done"], freed(n))
                            tt(gsum[k % 2], gload[q][:, k * 512:(k + 1) * 512], bank[:, 6 + k % 2, :], ALU.add).then_inc(s["gcorr_add"], 1)
                dve.wait_ge(s["gated"], ready(b * 32 + 31))
                v.tensor_copy(Y[:, 1:1 + LOW, 0:1], Y[:, 1:1 + LOW, 1:2])
                v.tensor_copy(Y[:, 1:1 + LOW, LW - 1:LW], Y[:, 1:1 + LOW, LW - 2:LW - 1]).then_inc(s["edge_done"], 1)
                dve.wait_ge(s["edge_done"], b + 1)
                v.tensor_copy(Y[:, 0, :], Y[:, 1, :])
                v.tensor_copy(Y[:, LOW + 1, :], Y[:, LOW, :])
                leave(dve, "end_layer", b)
                def interpolate(i, q):
                    n = b * 32 + 2 * i + q
                    r0 = 8 * i + 4 * q + 1
                    mid, above, below = (Y[:, bass.ds(r0 + d, 4), :] for d in (0, -1, 1))
                    stt(vup[q][:, :, 0, :], mid, 3.0, above, ALU.mult, ALU.add)
                    stt(vup[q][:, :, 1, :], mid, 3.0, below, ALU.mult, ALU.add).then_inc(s["up_rows"], 1)
                    dve.wait_ge(s["up_rows"], n + 1)
                    dve.wait_ge(s["up_ps"], freed(n))
                    vv = vup[q].rearrange("p i a w -> p (i a) w")
                    uu = up[q].rearrange("p (r w a) -> p r w a", w=LOW, a=2)
                    stt(uu[:, :, :, 0], vv[:, :, 1:1 + LOW], 3.0, vv[:, :, 0:LOW], ALU.mult, ALU.add)
                    stt(uu[:, :, :, 1], vv[:, :, 1:1 + LOW], 3.0, vv[:, :, 2:2 + LOW], ALU.mult, ALU.add).then_inc(s["up_ready"], 1)

                def add_x(i, q):
                    n = b * 32 + 2 * i + q
                    for k in range(4):
                        e, h = k // 2, k % 2
                        if k < 3:
                            dve.wait_ge(s["ve_up"], 3 * n + k + 1)
                        else:
                            dve.wait_ge(s["up_ps"], ready(n))
                        if h == 0:
                            dve.wait_ge(s[f"x_in{2 * q + e}"], 512 * b + 256 + 16 * i + 16)
                        xv = X[:, 2 * q + e, h, :]
                        tt(xv, xv, bank[:, 2 * k:2 * k + 2, :].rearrange("p k n -> p (k n)"), ALU.add).then_inc(s["added"], 1)
                interpolate(0, 0)
                with dve.Fori(0, 15) as i:
                    interpolate(i, 1)
                    add_x(i, 0)
                    interpolate(i + 1, 0)
                    add_x(i, 1)
                interpolate(15, 1)
                add_x(15, 0)
                add_x(15, 1)
                leave(dve, "end_out", b)


def kernel(**inputs):
    import numpy as _np
    import concourse.bacc as _bacc
    from concourse import mybir as _mybir
    from concourse.bass_utils import run_bass_kernel_spmd as _run

    a = {k: _np.asarray(v) for k, v in inputs.items()}
    x = a["x"]
    B = x.shape[0]
    w_in0, w_out0, wts = a["L0_conv_w_in"], a["L0_conv_w_out"], a["L0_conv_weights"]
    fwd, inv = fourier_bases()
    block = (_np.arange(P)[:, None] // CM == _np.arange(P)[None, :] // CM).astype(_np.float32)
    arrays = {
        "x": x.reshape(B, 256, PIX),
        "fwd": fwd, "inv": inv, "basis": gain_basis(), "cols": columns(), "block": block, "ident": _np.eye(P, dtype=_np.float32),
        "wproj": _np.concatenate([w_in0.T, w_out0], axis=1),
        "wtile": _np.tile(w_out0, (1, 8)),
        "wrep": _np.tile(w_out0.T, (6, 1)),
        "wgain": _np.tile(wts[:, :, R0:R0 + NR].reshape(CM, NA * NR).T, (3, 1)),
        "w_in1": a["L1_conv_w_in"].T,
        "wscan": _np.concatenate([a["L1_conv_row_wd"].T, a["L1_conv_row_wv"].T, a["L1_conv_col_wd"].T, a["L1_conv_col_wv"].T], axis=0),
        "w_out1": a["L1_conv_w_out"].T,
        "vec": _np.concatenate([a["L1_conv_gn_w"].reshape(2, P).T, a["L1_conv_gn_b"].reshape(2, P).T]
                               + [a[f"L1_conv_{n}"][:, None] for n in ("row_bd", "row_bv", "col_bd", "col_bv")]
                               + [a["L1_conv_row_bd"][:, None], a["L1_conv_col_bd"][:, None]]
                               + [a["L1_conv_w_dw"].reshape(P, 9)], axis=1),
    }
    nc = _bacc.Bacc("TRN2", target_bir_lowering=False, num_devices=1)
    feed, t = {}, {}
    for name, arr in arrays.items():
        arr = _np.ascontiguousarray(arr)
        feed[f"in_{name}"] = arr
        t[name] = nc.dram_tensor(f"in_{name}", arr.shape, _mybir.dt.from_np(arr.dtype), kind="ExternalInput").ap()
    out = nc.dram_tensor("out", [B, 256, PIX], F32, kind="ExternalOutput").ap()
    build(nc, B, t["x"], out, t)
    r = _run(nc, [feed], core_ids=[0])
    return r.results[0]["out"].reshape(B, 256, SIDE, SIDE)
```

```python
import numpy as np
import concourse.bass as bass
from concourse import mybir
from contextlib import ExitStack

F32 = mybir.dt.float32
BF16 = mybir.dt.bfloat16
U16 = mybir.dt.uint16
ALU = mybir.AluOpType
ACT = mybir.ActivationFunctionType
AX = mybir.AxisListType

P = 128
SIDE = 256
PIX = SIDE * SIDE
LOW = SIDE // 2
LPIX = LOW * LOW
CM = 16
NA, NR = 8, 5
R0 = 12
GK = 3 * NA * NR
NSLOT = 272
GA1, GB1, GA1B, GB1B, ROWB = 256, 257, 258, 259, 260
FEPS = 1e-8
TINY = 2.0 ** -100
DELTA = 2.0 ** -50
GN_EPS = 1e-5
LW = LOW + 2
YROWS = LOW + 3
LINE = LOW + 1
SCAN = 4 * LINE


def fourier_bases():
    n = np.arange(SIDE)
    k = np.arange(LOW)
    ang = 2 * np.pi * ((n[:, None] * k[None, :]) % SIDE) / SIDE
    fwd = np.zeros((SIDE, SIDE))
    fwd[:, :LOW] = np.cos(ang)
    fwd[:, LOW:] = np.sin(ang)
    fwd[:, LOW] = 1 - 2 * (n % 2)
    weight = np.full(SIDE, 2.0)
    weight[0] = weight[LOW] = 1.0
    return (fwd / 16).astype(np.float32), (fwd.T * weight[:, None] / 16).astype(np.float32)


def gain_basis():
    f = np.float32
    d = np.arange(-LOW, LOW).astype(f)
    yy, xx = d[:, None], d[None, :]
    r = np.sqrt(yy * yy + xx * xx).astype(f)
    theta = np.mod((np.arctan2(yy, xx).astype(f) + f(np.pi)).astype(f), f(np.pi)).astype(f)
    ridx = np.clip(np.floor(r / 8).astype(int), 0, 16)
    delta = np.pi / NA
    half = f(1.5 * delta / 2)
    centers = (np.arange(NA).astype(f) * f(delta) + f(delta / 2))[:, None, None]
    dist = np.abs(theta[None] - centers)
    aw = np.where(dist < half, np.clip(1 - dist / half, 0, None), 0).astype(f)
    aw = aw / (aw.sum(0, keepdims=True) + f(1e-8))
    aw = aw * (r > f(0.8 * LOW))[None]
    full = np.zeros((NA, NR, SIDE, SIDE), f)
    for j in range(NR):
        full[:, j] = aw * (ridx == R0 + j)[None]
    full = full.reshape(NA * NR, SIDE, SIDE)

    def at(ky, kx):
        return full[:, ky + LOW, kx + LOW]

    t = np.zeros((NA * NR, NSLOT, P), f)
    k = np.arange(P)
    for l in range(P):
        t[:, l] = at(k, np.full(P, l))
        t[:, P + l] = at(k, np.full(P, -l))
        t[:, P + l, 0] = full[:, 0, l + LOW]
        t[:, ROWB, l] = full[:, 0, LOW - l]
    for slot, sign in ((GA1, 1), (GB1, 1), (GA1B, -1), (GB1B, -1)):
        t[:, slot] = at(sign * k, np.full(P, -LOW))
    t[:, GB1, 0] = t[:, GB1B, 0] = full[:, 0, 0]
    parts = []
    for _ in range(3):
        bits = t.view(np.uint32) & np.uint32(0xffff0000)
        parts.append((bits >> 16).astype(np.uint16))
        t = (t - bits.view(f)).astype(f)
    return np.concatenate(parts)


def columns():
    c = np.zeros((P, 24), np.float32)
    c[1:, 0] = 1
    c[:, 1] = -c[:, 0]
    c[:, 2] = np.where(c[:, 0] > 0, 0.5, 1.0)
    c[:, 3] = c[:, 2] / 2
    part = np.arange(P) // CM
    for j, rows in enumerate(((0, 1, 2), (3, 4), (5,))):
        c[:, 4 + j] = np.isin(part, rows)
    c[:, 8:10] = 1
    c[0, 8:12] = 1
    for band in range(8):
        c[:, 16 + band] = part == band
    return c


def build(nc, B, x, out, t):
    ctx = ExitStack()
    with ctx:
        def sb(name, shape, dt=F32):
            return ctx.enter_context(nc.sbuf_tensor(name, shape, dt))

        def sem(name):
            return ctx.enter_context(nc.semaphore(name))

        def scratch(name, shape, dt=F32):
            return nc.dram_tensor(name, shape, dt, kind="Internal").ap()

        proj_d = scratch("proj_d", [B, 2 * CM, PIX])
        xe_d = scratch("xe_d", [B, CM, PIX])
        xs_d = scratch("xs_d", [B, 3, CM, PIX], BF16)
        gate_d = scratch("gate_d", [B, P, LPIX])
        pe_d = scratch("pe_d", [B, CM, LPIX])
        rowb_d = scratch("rowb_d", [P, CM])

        Y = sb("Y", [P, YROWS, LW])
        RING = 8 * LW * 2 + 2 * 2048 + 2 * 1024
        SX = sb("SX", [P, RING + 2 * 8192])
        S = SX[:, 0:LPIX]
        Xf = SX[:, RING + 8192:RING + 2 * 8192]
        ring = SX[:, RING:RING + 2 * 8192].rearrange("p (s h n) -> p s h n", s=8, h=2)
        xslot = [ring[:, (c + 4) % 8, :, :] for c in range(8)]
        gains = sb("gains", [P, CM, NSLOT])
        corner = sb("corner", [P, CM, 4])
        fwd = sb("fwd", [P, 2, SIDE])
        inv = sb("inv", [P, 2, SIDE])
        wproj = sb("wproj", [P, 2, 2 * CM])
        wpool = sb("wpool", [P, 2, SIDE])
        cmix = sb("cmix", [P, 8, SIDE])
        wscan = sb("wscan", [P, 4, P])
        wup = sb("wup", [P, SIDE])
        wstack = sb("wstack", [6 * CM, SIDE], BF16)
        gram = sb("gram", [P, P])
        ones = sb("ones", [P, P])
        taps = sb("taps", [P, 4, P])
        cols = sb("cols", [P, 24])
        vec = sb("vec", [P, 32])
        sums = sb("sums", [P, 224])
        stat = sb("stat", [P, 16])
        bank = ctx.enter_context(nc.psum_tensor("bank", [P, 8, 512], F32))

        kappa, negk, half_h, quart_h = (cols[:, i:i + 1] for i in range(4))
        gnw, gnb = vec[:, 0:2], vec[:, 2:4]
        bd, bv, nbd = [vec[:, 4:5], vec[:, 6:7]], [vec[:, 5:6], vec[:, 7:8]], [vec[:, 8:9], vec[:, 9:10]]
        dw = vec[:, 10:19]
        cw, cb = vec[:, 19:21], vec[:, 21:23]
        wsum = vec[:, 23:24]
        sum_x, sum_xx, cross, sum_xe = sums[:, 0:64], sums[:, 64:128], sums[:, 128:136], sums[:, 136:144]
        rs, cshift = stat[:, 8:9], stat[:, 9:11]
        TE_TAPS = [0, 1, 2, 3]
        VE_TAPS = [4, 5, 6, 7, 8]

        def sv(a, n):
            return S[:, a:a + n]

        basis = [sv(5120 + q * 1024, 1024)[0:GK, :].bitcast(U16).rearrange("p (k n) -> p k n", k=16) for q in range(2)]
        basis16 = [sv(5120 + q * 1024, 1024)[0:GK, :].bitcast(BF16).rearrange("p (k n) -> p k n", k=16) for q in range(2)]
        wgain = [sv(784 + 8 * j, 8)[0:GK, :].bitcast(BF16) for j in range(3)]
        vert = [sv(q * 1024, 1024) for q in range(2)]
        pooled = [sv(2048 + q * 1024, 1024).rearrange("p (h n) -> p h n", h=2) for q in range(2)]
        pstage = [sv(4096 + q * 512, 512) for q in range(2)]
        gstage = [sv(5120 + q * 512, 512) for q in range(2)]
        junk = sv(6144, 1024).bitcast(BF16)
        freq = S[:, 0:8192].rearrange("p (m n) -> p m n", m=CM)
        img = [sv(8192 + m * 512, 512).rearrange("p (t n) -> p t n", t=2) for m in range(8)]
        half1 = [sv(12288 + q * 512, 512).rearrange("p (t n) -> p t n", t=2) for q in range(2)]
        half2 = [sv(13312 + q * 512, 512).rearrange("p (t n) -> p t n", t=2) for q in range(2)]
        small = [sv(14336 + 16 * i, 16) for i in range(8)]
        tmp = [Xf[:, i * 512:(i + 1) * 512] for i in range(8)]
        xe_s = [sv(8192 + r * 512, 512) for r in range(4)]
        rest = [Xf[:, 4096 + q * 512:4608 + q * 512] for q in range(2)]
        parts = [Xf[:, 5120 + r * 768:5888 + r * 768].bitcast(BF16).rearrange("p (i n) -> p i n", i=3) for r in range(4)]
        xe_t = [sv(c * 1024, 1024) for c in range(4)]
        xq_t = [sv(4096 + c * 1024, 1024) for c in range(4)]
        pe_t = sv(10240, 2048)
        mix = [sv(12288 + q * 1024, 1024) for q in range(2)]
        vsum = [sv(14464 + q * 512, 512) for q in range(2)]
        lx = [[Xf[:, q * 4096 + a:q * 4096 + a + n] for a, n in
               ((0, 512), (512, 512), (1024, SCAN + 1), (1544, SCAN + 1), (2064, SCAN + 1), (2584, SCAN + 1))]
              for q in range(2)]
        conv, sig, keep, take, fsc, bsc = zip(*lx)

        gload = [sv(12288 + q * 2048, 2048) for q in range(2)]
        gsum = [sv(q * 512, 512) for q in range(2)]
        gsig = [sv(1024 + q * 512, 512) for q in range(2)]

        def lines(a, first):
            if first:
                return a[:, 1:SCAN + 1].rearrange("p (r w) -> p r w", w=LINE)[:, :, 0:LOW]
            return a[:, 0:SCAN + 1:LINE]

        VW = 8 * LW
        vup = [sv(q * VW, VW).rearrange("p (i a w) -> p i a w", i=4, a=2) for q in range(2)]
        up = [sv(2 * VW + q * 2048, 2048) for q in range(2)]
        stack = [S[0:6 * CM, 2 * VW + 4096 + q * 1024:2 * VW + 4096 + (q + 1) * 1024].bitcast(BF16) for q in range(2)]

        names = """consts_in basis_in0 basis_in1 gain_ps gain_t rowb_out rowb_in ve_setup te_setup mv_setup
        x_in0 x_in1 x_in2 x_in3 x_in4 x_in5 x_in6 x_in7 x_out0 x_out1 x_out2 x_out3 x_out4 x_out5 x_out6 x_out7
        proj_ps lowp_ps pool_done square_done proj_st y_ev g_st proj_out0 proj_out1 gate_out0 gate_out1 ve_pool
        img_in0 img_in1 s1_ps s2_ps s3_ps s4_ps h1_st f_st h2_st xe_st parts_done xe_out0 xe_out1 xe_out2 xe_out3
        xs_out0 xs_out1 xs_out2 xs_out3
        uv_ready sq_ready m_ready root_ready ew_done ve_ew pl_parts
        st_in0 st_in1 st_in2 st_in3 gram_ps st_done ve_stat pe_out tot_in tot_ps var_root norm_set
        pads_done pe_in corr_ps corr_add norm_done conv_ps conv_done sig_done s_ready z_ps gates_done
        scans_done merged take_done both_ways ve_l1 pl_l1 gate_in0 gate_in1 gcorr_ps gcorr_add gsig_done gated0 gated1 edge_done
        up_rows up_ready up_ps added stack_in0 stack_in1 ve_up
        end_project end_fourier end_stats end_layer end_out held stores_set"""
        s = {n: sem(n) for n in names.split()}
        RING2 = "lowp_ps proj_ps proj_st y_ev g_st s1_ps s2_ps s3_ps s4_ps h1_st f_st h2_st xe_st parts_done st_done corr_add " \
                "conv_ps conv_done gates_done take_done scans_done merged gcorr_add gcorr_ps corr_ps gsig_done s_ready up_ps up_ready pool_done square_done".split()

        def ready(n):
            return n + 3

        def freed(n):
            return n + 1

        def x_loads(b, i):
            return 256 * b + 16 * i + 16

        class Steps:
            def __init__(self, eng, name, base):
                self.eng, self.name, self.base, self.n = eng, name, base, 0

            def done(self, ins):
                ins.then_inc(s[self.name], 1)
                self.n += 1

            def wait(self):
                self.eng.wait_ge(s[self.name], self.base + self.n)

        def credit(eng, *which):
            for n in which:
                assert n in RING2
                eng.sem_inc(s[n], 2)

        for_stores = [f"x_out{c}" for c in range(8)] + [
            "proj_out0", "proj_out1", "gate_out0", "gate_out1"] + [
            f"{n}{r}" for n in ("xe_out", "xs_out") for r in range(4)]

        def hold(eng):
            eng.sem_inc(s["held"], 1)

        def leave(eng, phase, b):
            eng.drain().then_inc(s[phase], 1)
            eng.wait_ge(s[phase], 4 * b + 4)
            hold(eng)

        block = ctx.enter_context(nc.Block())
        EW = 18

        @block.sync
        def _(sp):
            for n in for_stores:
                sp.sem_inc(s[n], 16)
            sp.sem_inc(s["stores_set"], 1)
            pairs = [(fwd[:, :, :], t["fwd"].rearrange("(t p) n -> p t n", p=P)),
                     (inv[:, :, :], t["inv"].rearrange("(t p) n -> p t n", p=P)),
                     (wproj[:, :, :], t["wproj"].rearrange("(t p) n -> p t n", p=P)),
                     (wpool[:, :, :], t["w_in1"].rearrange("(t p) n -> p t n", p=P)),
                     (wscan[:, :, :], t["wscan"].rearrange("(t p) n -> p t n", p=P)),
                     (wup[:, :], t["w_out1"]), (cols[:, :], t["cols"]), (vec[:, 0:19], t["vec"]),
                     (S[:, 0:256].rearrange("p (t n) -> p t n", t=2), t["wtile"].rearrange("(t p) n -> p t n", p=P)),
                     (S[0:6 * CM, 256:512], t["wrep"]), (S[:, 512:640], t["block"]), (S[:, 640:768], t["ident"]),
                     (S[0:GK, 768:784], t["wgain"])]
            for dst, src in pairs:
                sp.dma_start(dst, src).then_inc(s["consts_in"], 16)
            with sp.Fori(0, (NSLOT // 16 - 1) // 2) as i:
                for q in range(2):
                    sp.wait_ge(s["gain_ps"], 2 * i + q + 1)
                    sp.dma_start(basis[q], t["basis"][:, bass.ds(32 * i + 16 * q, 16), :])\
                      .then_inc(s[f"basis_in{q}"], 16)
            sp.wait_ge(s["gain_ps"], NSLOT // 16)
            sp.dma_start(basis[0], t["basis"][:, NSLOT - 16:NSLOT, :]).then_inc(s["basis_in0"], 16)
            sp.wait_ge(s["gain_t"], NSLOT // 16 + 1)
            sp.dma_start(rowb_d, gains[:, :, ROWB], allow_slow_non_contiguous=True).then_inc(s["rowb_out"], 16)
            sp.wait_ge(s["rowb_out"], 16)
            sp.dma_start(S[0:1, 1024:1024 + P * CM].rearrange("o (m l) -> o m l", l=P), rowb_d.rearrange("(o l) m -> o m l", o=1),
                         allow_slow_non_contiguous=True).then_inc(s["rowb_in"], 16)

            with sp.Fori(0, B) as b:
                def load_chunk(i, c):
                    sp.dma_start(xslot[c], x[b, :, bass.ds(i * 8192 + c * 1024, 1024)].rearrange("(h p) n -> p h n", p=P))\
                      .then_inc(s[f"x_in{c}"], 16)

                def reuse_slot(i, c):
                    sp.wait_ge(s["proj_ps"], ready(b * 32 + i * 4 + c // 2 - 4))
                    hold(sp)
                    last = b * 64 + i * 8 + c - 8
                    sp.wait_ge(s["pool_done"], 4 + last + 1)
                    sp.wait_ge(s["square_done"], 4 + last + 1)
                    hold(sp)

                def store_gate(i, p):
                    sp.wait_ge(s["g_st"], ready(b * 32 + 4 * i + p))
                    hold(sp)
                    sp.dma_start(gate_d[b, :, bass.ds(i * 2048 + p * 512, 512)], gstage[p % 2]).then_inc(s[f"gate_out{p % 2}"], 16)
                for c in range(8):
                    sp.wait_ge(s[f"x_out{c}"], 128 * b + 16)
                    hold(sp)
                    load_chunk(0, c)
                with sp.Fori(1, 8) as i:
                    for p in range(4):
                        for c in (2 * p, 2 * p + 1):
                            reuse_slot(i, c)
                            load_chunk(i, c)
                        store_gate(i - 1, p)
                for p in range(3):
                    store_gate(7, p)
                for q in range(2):
                    sp.wait_ge(s[f"proj_out{q}"], 256 * b + 256 + 16)
                hold(sp)
                sp.wait_ge(s["pool_done"], 4 + b * 64 + 64)
                sp.wait_ge(s["square_done"], 4 + b * 64 + 64)
                hold(sp)

                def load_images(gr):
                    for c in range(4 * gr, 4 * gr + 4):
                        sp.dma_start(img[c % 8], proj_d[b, c, :].rearrange("(t p n) -> p t n", t=2, p=P)).then_inc(s[f"img_in{gr % 2}"], 16)
                load_images(0)
                load_images(1)
                store_gate(7, 3)
                for q in range(2):
                    sp.wait_ge(s[f"gate_out{q}"], 256 * b + 256 + 16)
                n0 = b * 16
                for gr in (2, 3):
                    sp.wait_ge(s["s1_ps"], 2 + n0 + 4 * (gr - 1))
                    hold(sp)
                    load_images(gr)

                def store_parts(c):
                    sp.wait_ge(s["parts_done"], ready(n0 + c))
                    hold(sp)
                    for i in range(3):
                        sp.dma_start(xs_d[b, i, c, :].rearrange("(t p n) -> p t n", t=2, p=P),
                                     parts[c % 4][:, i, :].rearrange("p (t n) -> p t n", t=2)).then_inc(s[f"xs_out{c % 4}"], 16)
                for c in range(CM):
                    sp.wait_ge(s["xe_st"], ready(n0 + c))
                    hold(sp)
                    sp.dma_start(xe_d[b, c, :].rearrange("(t p n) -> p t n", t=2, p=P),
                                 xe_s[c % 4].rearrange("p (t n) -> p t n", t=2)).then_inc(s[f"xe_out{c % 4}"], 16)
                    if c:
                        store_parts(c - 1)
                for q in range(4):
                    sp.wait_ge(s[f"xe_out{q}"], 64 * b + 64 + 16)
                sp.wait_ge(s["end_fourier"], 4 * b + 4)
                hold(sp)
                for i in range(2):
                    for c in range(4):
                        sp.wait_ge(s["st_done"], b * 8 + 4 * i + c + 1)
                        hold(sp)
                        px = slice(i * 4096 + c * 1024, i * 4096 + c * 1024 + 1024)
                        for dst, src in ((xe_t[c], xe_d[b]), (xq_t[c], proj_d[b, CM:2 * CM])):
                            sp.dma_start(dst, src.rearrange("m (g n) -> g m n", g=8)[:, :, px]).then_inc(s[f"st_in{c}"], 16)
                    if i == 0:
                        store_parts(CM - 1)
                sp.wait_ge(s["st_done"], 4 + b * 8 + 8)
                hold(sp)
                sp.dma_start(pe_d[b].rearrange("m (g n) -> g m n", g=8), pe_t).then_inc(s["pe_out"], 16)
                sp.wait_ge(s["pe_out"], 16 * b + 16)
                for q in range(4):
                    sp.wait_ge(s[f"xs_out{q}"], 192 * b + 192 + 16)
                hold(sp)
                sp.wait_ge(s["end_stats"], 4 * b + 4)
                hold(sp)
                sp.wait_ge(s["z_ps"], b * 64 + 64)
                hold(sp)
                sp.dma_start(pe_t, pe_d[b].rearrange("m (g n) -> g m n", g=8)).then_inc(s["pe_in"], 16)

                def load_gate(i, q):
                    sp.dma_start(gload[q], gate_d[b, :, bass.ds(i * 4096 + q * 2048, 2048)]).then_inc(s[f"gate_in{q}"], 16)
                load_gate(0, 0)
                load_gate(0, 1)
                with sp.Fori(1, 4) as i:
                    for q in range(2):
                        sp.wait_ge(s["gcorr_add"], ready(b * 32 + 8 * i + 4 * q - 5))
                        hold(sp)
                        load_gate(i, q)
                sp.wait_ge(s["merged"], ready(b * 64 + 63))
                hold(sp)

                def load_out(i, p):
                    q = p % 2
                    for c in (2 * p, 2 * p + 1):
                        sp.wait_ge(s[f"x_out{c}"], 128 * b + 16 * i + 16)
                        hold(sp)
                        sp.dma_start(xslot[c], x[b, :, bass.ds(i * 8192 + c * 1024, 1024)].rearrange("(h p) n -> p h n", p=P))\
                          .then_inc(s[f"x_in{c}"], 16)
                    sp.wait_ge(s["up_ps"], freed(b * 32 + 4 * i + p))
                    hold(sp)
                    px = bass.ds(i * 8192 + p * 2048, 2048)
                    sp.dma_start(stack[q][0:48, :], xs_d[b, 0:3, :, px].rearrange("i m n -> (i m) n")).then_inc(s[f"stack_in{q}"], 16)
                    sp.dma_start(stack[q][48:80, :], xs_d[b, 0:2, :, px].rearrange("i m n -> (i m) n")).then_inc(s[f"stack_in{q}"], 16)
                    sp.dma_start(stack[q][80:96, :], xs_d[b, 0, :, px]).then_inc(s[f"stack_in{q}"], 16)
                load_out(0, 0)
                load_out(0, 1)
                sp.wait_ge(s["end_layer"], 4 * b + 4)
                hold(sp)
                load_out(0, 2)
                load_out(0, 3)
                with sp.Fori(1, 8) as i:
                    for p in range(4):
                        load_out(i, p)

        @block.tensor
        def _(pe):
            mm = nc.tensor.matmul
            credit(pe, "proj_ps", "lowp_ps", "s1_ps", "s2_ps", "s3_ps", "s4_ps", "corr_ps", "conv_ps", "gcorr_ps", "up_ps")
            pe.sem_inc(s["gain_ps"], 2)
            pe.wait_ge(s["consts_in"], 16 * 13)
            pe.wait_ge(s["ve_setup"], 5)

            def gain_chunk(q, n, loads):
                pe.wait_ge(s[f"basis_in{q}"], loads)
                pe.wait_ge(s["gain_t"], n + 1)
                for k in range(16):
                    for j in range(3):
                        last = mm(bank[:, q, k * CM:(k + 1) * CM], basis16[q][:, k, :], wgain[j], start=j == 0, stop=j == 2)
                last.then_inc(s["gain_ps"], 1)
            with pe.Fori(0, (NSLOT // 16 - 1) // 2) as i:
                for q in range(2):
                    gain_chunk(q, 2 * i + q, 16 * i + 16)
            gain_chunk(0, NSLOT // 16 - 1, 16 * ((NSLOT // 16 - 1) // 2) + 16)
            pe.wait_ge(s["ve_setup"], 8)
            for o in range(2):
                for v, col in ((gnw, 0), (gnb, 2)):
                    for h in range(2):
                        mm(bank[:, 2, col + o:col + o + 1], S[:, 2304 + 1024 + h * SIDE + o * P:2304 + 1024 + h * SIDE + (o + 1) * P],
                           v[:, h:h + 1], start=h == 0, stop=h == 1)
            for h in range(2):
                mm(bank[:, 3, 0:1], S[:, h * P:(h + 1) * P], ones[:, 0:1], start=h == 0, stop=h == 1)
            for h in range(2):
                mm(bank[:, 4, 0:P], S[:, h * P:(h + 1) * P], S[:, h * P:(h + 1) * P], start=h == 0, stop=h == 1)
            for h in range(2):
                last = mm(bank[:, 5, 0:SIDE], S[:, h * P:(h + 1) * P], wpool[:, h, :], start=h == 0, stop=h == 1)
            last.then_inc(s["te_setup"], 1)
            pe.wait_ge(s["mv_setup"], 1)

            with pe.Fori(0, B) as b:
                def project(i, p):
                    n, q = b * 32 + 4 * i + p, p % 2
                    pe.wait_ge(s["proj_st"], freed(n))
                    for c in (2 * p, 2 * p + 1):
                        pe.wait_ge(s[f"x_in{c}"], x_loads(b, i))
                    for h in range(2):
                        for k in range(4):
                            last = mm(bank[32 * k:32 * k + 32, q, :], wproj[:, h, :], xslot[2 * p + k // 2][:, h, (k % 2) * 512:(k % 2) * 512 + 512],
                                      start=h == 0, stop=h == 1)
                    last.then_inc(s["proj_ps"], 1)

                def project_low(i, p):
                    n, q = b * 32 + 4 * i + p, p % 2
                    pe.wait_ge(s["pool_done"], 4 + 2 * n + 2)
                    pe.wait_ge(s["y_ev"], freed(n))
                    pe.wait_ge(s["g_st"], freed(n))
                    for o in range(2):
                        for h in range(2):
                            last = mm(bank[:, 2 + 2 * o + q, :], wpool[:, h, o * P:(o + 1) * P], pooled[q][:, h, :], start=h == 0, stop=h == 1)
                    last.then_inc(s["lowp_ps"], 1)
                project(0, 0)
                with pe.Fori(0, 7) as i:
                    for p in range(4):
                        project(i + (p + 1) // 4, (p + 1) % 4)
                        project_low(i, p)
                for p in range(4):
                    if p < 3:
                        project(7, p + 1)
                    project_low(7, p)
                leave(pe, "end_project", b)
                n0 = b * 16

                def forward1(c):
                    pe.wait_ge(s["h1_st"], freed(n0 + c))
                    for tx in range(2):
                        for ty in range(2):
                            last = mm(bank[:, c % 2, tx * SIDE:(tx + 1) * SIDE], img[c % 8][:, ty, tx * P:(tx + 1) * P], fwd[:, ty, :],
                                      start=ty == 0, stop=ty == 1)
                    last.then_inc(s["s1_ps"], 1)

                def forward2(c):
                    pe.wait_ge(s["h1_st"], ready(n0 + c))
                    pe.wait_ge(s["f_st"], freed(n0 + c))
                    for tk in range(2):
                        for tx in range(2):
                            last = mm(bank[:, 2 + c % 2, tk * SIDE:(tk + 1) * SIDE], half1[c % 2][:, tx, tk * P:(tk + 1) * P], fwd[:, tx, :],
                                      start=tx == 0, stop=tx == 1)
                    last.then_inc(s["s2_ps"], 1)

                def inverse1(c):
                    pe.wait_ge(s["h2_st"], freed(n0 + c))
                    for tl in range(2):
                        for tk in range(2):
                            a = tk * SIDE + tl * P
                            last = mm(bank[:, 4 + c % 2, tl * SIDE:(tl + 1) * SIDE], freq[:, c, a:a + P], inv[:, tk, :],
                                      start=tk == 0, stop=tk == 1)
                    last.then_inc(s["s3_ps"], 1)

                def inverse2(c):
                    pe.wait_ge(s["h2_st"], ready(n0 + c))
                    pe.wait_ge(s["xe_st"], freed(n0 + c))
                    for ty in range(2):
                        for tl in range(2):
                            last = mm(bank[:, 6 + c % 2, ty * SIDE:(ty + 1) * SIDE], half2[c % 2][:, tl, ty * P:(ty + 1) * P], inv[:, tl, :],
                                      start=tl == 0, stop=tl == 1)
                    last.then_inc(s["s4_ps"], 1)

                for c in range(CM):
                    if c % 4 == 0:
                        pe.wait_ge(s[f"img_in{c // 4 % 2}"], 128 * b + 64 * (c // 8) + 64)
                    forward1(c)
                    if c:
                        forward2(c - 1)
                for c in range(CM):
                    before = (lambda: forward2(CM - 1)) if c == 0 else (lambda: inverse2(c - 1))
                    if c % 4 == 0 and c:
                        before()
                    if c % 4 == 0:
                        pe.wait_ge(s["ew_done"], b * 4 + c // 4 + 2)
                    inverse1(c)
                    if c % 4 or c == 0:
                        before()
                inverse2(CM - 1)
                leave(pe, "end_fourier", b)
                with pe.Fori(0, 2) as i:
                    for c in range(4):
                        pe.wait_ge(s[f"st_in{c}"], 64 * b + 32 * i + 32)
                        pe.wait_ge(s["st_done"], b * 8 + 4 * i + c + 1)
                        for k in range(2):
                            last = mm(bank[:, 2 * c + k, :], gram[:, :], xe_t[c][:, k * 512:(k + 1) * 512], start=True, stop=True)
                        last.then_inc(s["gram_ps"], 1)
                pe.wait_ge(s["tot_in"], b + 1)
                mm(bank[:, 4, 0:2], ones[:, :], stat[:, 0:2], start=True, stop=True).then_inc(s["tot_ps"], 1)
                leave(pe, "end_stats", b)
                def correct(n, half, added, product):
                    pe.wait_ge(s[added], freed(b * 32 + n))
                    mm(bank[:, 6 + n % 2, :], cmix[:, n // 4, half * P:(half + 1) * P], pe_t[:, (n % 4) * 512:(n % 4 + 1) * 512],
                       start=True, stop=True).then_inc(s[product], 1)
                for n in range(32):
                    correct(n, 0, "corr_add", "corr_ps")

                def gates_of(w, q, n, rhs):
                    pe.wait_ge(s["gates_done"], freed(n))
                    pe.wait_ge(s["take_done"], freed(n))
                    mm(bank[:, 2 + q, :], wscan[:, 2 * w, :], rhs, start=True, stop=True)
                    mm(bank[:, 4 + q, :], wscan[:, 2 * w + 1, :], rhs, start=True, stop=True).then_inc(s["z_ps"], 1)
                pe.wait_ge(s["pads_done"], 4 * b + 4)
                hold(pe)
                def conv_taps(i, first=False):
                    for q in range(2):
                        c = b * 32 + 2 * i + q
                        pe.wait_ge(s["norm_done"], c + b + 2)
                        if not first:
                            pe.wait_ge(s["ve_l1"], (b * 16 + i - 1) * 2 * (len(VE_TAPS) - 1) + q + 1)
                        for k, tap in enumerate(TE_TAPS):
                            rhs = Y[:, bass.ds(8 * i + 4 * q + 1 + tap // 3, 4), tap % 3:tap % 3 + LOW]
                            last = mm(bank[:, q, :], taps[:, k, :], rhs, start=k == 0, stop=k == len(TE_TAPS) - 1)
                        last.then_inc(s["conv_ps"], 1)

                def row_gates(i):
                    for q in range(2):
                        pe.wait_ge(s["s_ready"], ready(b * 32 + 2 * i + q))
                        gates_of(0, q, b * 64 + 2 * i + q, S[:, bass.ds(i * 1024 + q * 512, 512)])
                conv_taps(0, first=True)
                with pe.Fori(1, 16) as i:
                    conv_taps(i)
                    row_gates(i - 1)
                row_gates(15)
                sc = S[:, :].rearrange("p (r w) -> p w r", w=LOW)
                with pe.Fori(0, 16) as i:
                    for q in range(2):
                        pe.wait_ge(s["s_ready"], ready(b * 32 + 31))
                        gates_of(1, q, b * 64 + 32 + 2 * i + q, sc[:, bass.ds(8 * i + 4 * q, 4), :])
                pe.wait_ge(s["pe_in"], 16 * b + 16)
                for n in range(32):
                    correct(n, 1, "gcorr_add", "gcorr_ps")
                leave(pe, "end_layer", b)
                with pe.Fori(0, 8) as i:
                    for p in range(4):
                        n, q = b * 32 + 4 * i + p, p % 2
                        pe.wait_ge(s["up_ready"], ready(n))
                        pe.wait_ge(s[f"stack_in{q}"], 768 * b + 96 * i + 48 * (p // 2) + 48)
                        for e in range(2):
                            for h in range(2):
                                k = 2 * e + h
                                pe.wait_ge(s["added"], 4 * n + k + 1)
                                for j in range(2):
                                    px = slice(e * 1024 + j * 512, e * 1024 + j * 512 + 512)
                                    mm(bank[:, 2 * k + j, :], wup[:, h * P:(h + 1) * P], up[q][:, px], start=True, stop=False)
                                    last = mm(bank[:, 2 * k + j, :], wstack[:, h * P:(h + 1) * P], stack[q][:, px], start=False, stop=True)
                                if k < 3:
                                    last.then_inc(s["ve_up"], 1)
                                else:
                                    last.then_inc(s["up_ps"], 1)
                leave(pe, "end_out", b)

        @block.scalar
        def _(act):
            A = nc.scalar.activation
            credit(act, "square_done", "square_done", "proj_st", "h1_st", "f_st", "h2_st", "xe_st", "gates_done", "gsig_done")
            act.sem_inc(s["gain_t"], 1)
            act.wait_ge(s["stores_set"], 1)

            def tanh_chunk(q, n, at):
                act.wait_ge(s["gain_ps"], 2 + n + 1)
                A(gains[:, :, at], bank[:, q, 0:16 * CM].rearrange("p (k m) -> p m k", m=CM), ACT.Tanh).then_inc(s["gain_t"], 1)
            with act.Fori(0, (NSLOT // 16 - 1) // 2) as i:
                for q in range(2):
                    tanh_chunk(q, 2 * i + q, bass.ds(32 * i + 16 * q, 16))
            tanh_chunk(0, NSLOT // 16 - 1, slice(NSLOT - 16, NSLOT))
            act.wait_ge(s["mv_setup"], 1)

            with act.Fori(0, B) as b:
                with act.Fori(0, 8) as i:
                    for p in range(4):
                        n, q = b * 32 + 4 * i + p, p % 2
                        for c in (2 * p, 2 * p + 1):
                            act.wait_ge(s[f"x_in{c}"], x_loads(b, i))
                            act.wait_ge(s["square_done"], 4 + b * 64 + 8 * i + c)
                            A(junk, xslot[c].rearrange("p h n -> p (h n)"), ACT.Square,
                              accum_out=sum_xx[:, bass.ds(8 * i + c, 1)]).then_inc(s["square_done"], 1)
                        act.wait_ge(s["proj_ps"], ready(n))
                        act.wait_ge(s[f"proj_out{q}"], 16 * (b * 16 + 2 * i + p // 2) + 16)
                        A(pstage[q], bank[:, q, :], ACT.Copy).then_inc(s["proj_st"], 1)
                        act.wait_ge(s["proj_st"], ready(n))
                        act.dma_start(proj_d[b, :, bass.ds(i * 8192 + p * 2048, 2048)].rearrange("m (k n) -> k m n", k=4), pstage[q])\
                           .then_inc(s[f"proj_out{q}"], 16)
                for q in range(2):
                    act.wait_ge(s[f"proj_out{q}"], 256 * (b + 1) + 16)
                hold(act)
                leave(act, "end_project", b)
                n0, g0 = b * 16, b * 4

                def copy_half1(c):
                    act.wait_ge(s["s1_ps"], ready(n0 + c))
                    act.wait_ge(s["s2_ps"], freed(n0 + c))
                    A(half1[c % 2], bank[:, c % 2, :].rearrange("p (t n) -> p t n", t=2), ACT.Copy).then_inc(s["h1_st"], 1)

                def copy_freq(c):
                    act.wait_ge(s["s2_ps"], ready(n0 + c))
                    A(freq[:, c, :], bank[:, 2 + c % 2, :], ACT.Copy).then_inc(s["f_st"], 1)

                def copy_half2(c):
                    act.wait_ge(s["s3_ps"], ready(n0 + c))
                    act.wait_ge(s["s4_ps"], freed(n0 + c))
                    A(half2[c % 2], bank[:, 4 + c % 2, :].rearrange("p (t n) -> p t n", t=2), ACT.Copy).then_inc(s["h2_st"], 1)

                def copy_xe(c):
                    act.wait_ge(s["s4_ps"], ready(n0 + c))
                    act.wait_ge(s[f"xe_out{c % 4}"], 16 * (b * 4 + c // 4) + 16)
                    act.wait_ge(s[f"xs_out{c % 4}"], 48 * (b * 4 + c // 4) + 16)
                    A(parts[c % 4][:, 0, :], bank[:, 6 + c % 2, :], ACT.Copy)
                    A(xe_s[c % 4], bank[:, 6 + c % 2, :], ACT.Copy).then_inc(s["xe_st"], 1)

                def squares(gr):
                    act.wait_ge(s["uv_ready"], g0 + gr + 1)
                    for k in range(4):
                        last = A(tmp[4 + k], tmp[k], ACT.Square)
                    last.then_inc(s["sq_ready"], 1)

                def roots(gr):
                    act.wait_ge(s["m_ready"], g0 + gr + 1)
                    for v in (tmp[4], tmp[5], small[2]):
                        last = A(v, v, ACT.Abs_reciprocal_sqrt)
                    last.then_inc(s["root_ready"], 1)
                squares_after = {("f", 4): 0, ("f", 10): 1, ("x", 0): 2, ("x", 7): 3}
                roots_after = {("f", 5): 0, ("f", 12): 1, ("x", 1): 2, ("x", 8): 3}

                def behind(kind, c):
                    (copy_freq if kind == "f" else copy_xe)(c)
                    if (kind, c) in squares_after:
                        squares(squares_after[kind, c])
                    if (kind, c) in roots_after:
                        roots(roots_after[kind, c])
                for c in range(CM):
                    copy_half1(c)
                    if c:
                        behind("f", c - 1)
                copy_half2(0)
                behind("f", CM - 1)
                for c in range(1, CM):
                    if c % 4 == 0:
                        behind("x", c - 1)
                    copy_half2(c)
                    if c % 4:
                        behind("x", c - 1)
                behind("x", CM - 1)
                leave(act, "end_fourier", b)
                act.wait_ge(s["tot_ps"], b + 1)
                act.wait_ge(s["norm_set"], b + 1)
                A(stat[:, 5:6], stat[:, 4:5], ACT.Sqrt).then_inc(s["var_root"], 1)
                leave(act, "end_stats", b)
                with act.Fori(0, 16) as i:
                    for q in range(2):
                        act.wait_ge(s["corr_add"], ready(b * 32 + 2 * i + q))
                        v = Y[:, bass.ds(8 * i + 4 * q + 2, 4), 1:1 + LOW]
                        A(v, v, ACT.Identity, scale=rs, bias=cshift[:, 0:1]).then_inc(s["norm_done"], 1)
                act.drain().then_inc(s["norm_done"], 1)

                def gates(w, q, n):
                    act.wait_ge(s["z_ps"], n + 1)
                    act.wait_ge(s["scans_done"], freed(n))
                    z = bank[:, 2 + q, :].rearrange("p (r w) -> p r w", w=LOW)
                    A(lines(keep[q], 1), z, ACT.Sigmoid, scale=-1.0, bias=nbd[w])
                    A(lines(take[q], 1), z, ACT.Sigmoid, bias=bd[w]).then_inc(s["gates_done"], 1)
                act.wait_ge(s["pads_done"], 4 * b + 4)
                def conv_sigmoid(i):
                    for q in range(2):
                        n = b * 32 + 2 * i + q
                        act.wait_ge(s["conv_done"], ready(n))
                        act.wait_ge(s["s_ready"], freed(n))
                        A(sig[q], conv[q], ACT.Sigmoid).then_inc(s["sig_done"], 1)

                def row_gates(i):
                    for q in range(2):
                        gates(0, q, b * 64 + 2 * i + q)
                conv_sigmoid(0)
                with act.Fori(1, 16) as i:
                    row_gates(i - 1)
                    conv_sigmoid(i)
                row_gates(15)
                with act.Fori(0, 16) as i:
                    for q in range(2):
                        gates(1, q, b * 64 + 32 + 2 * i + q)
                def gate_sigmoid(i, q, first=False):
                    act.wait_ge(s["gcorr_add"], ready(b * 32 + 2 * i + q))
                    if not first:
                        act.wait_ge(s[f"gated{q}"], b * 16 + i)
                    A(gsig[q], gsum[q], ACT.Sigmoid, scale=rs, bias=cshift[:, 1:2]).then_inc(s["gsig_done"], 1)
                gate_sigmoid(0, 0, first=True)
                gate_sigmoid(0, 1, first=True)
                with act.Fori(1, 16) as i:
                    gate_sigmoid(i, 0)
                    gate_sigmoid(i, 1)
                leave(act, "end_layer", b)
                with act.Fori(0, 8) as i:
                    for c in range(8):
                        act.wait_ge(s["added"], 4 + b * 128 + i * 16 + 2 * c + 2)
                        act.dma_start(out[b, :, bass.ds(i * 8192 + c * 1024, 1024)].rearrange("(h p) n -> p h n", p=P), xslot[c])\
                           .then_inc(s[f"x_out{c}"], 16)
                leave(act, "end_out", b)
            for c in range(8):
                act.wait_ge(s[f"x_out{c}"], 128 * B + 16)

        @block.gpsimd
        def _(pool):
            g = nc.gpsimd
            credit(pool, "parts_done", "merged", "s_ready")
            pool.wait_ge(s["mv_setup"], 1)
            pool.wait_ge(s["stores_set"], 1)
            with pool.Fori(0, B) as b:
                leave(pool, "end_project", b)
                pool.drain().then_inc(s["end_fourier"], 1)
                for c in range(CM):
                    q, r = c % 2, c % 4
                    pool.wait_ge(s["xe_st"], ready(b * 16 + c))
                    pool.wait_ge(s["parts_done"], freed(b * 16 + c))
                    g.tensor_tensor(rest[q], xe_s[r], parts[r][:, 0, :], ALU.subtract)
                    g.tensor_tensor(parts[r][:, 1, :], xe_s[r], parts[r][:, 0, :], ALU.subtract).then_inc(s["pl_parts"], 1)
                    pool.wait_ge(s["pl_parts"], b * 16 + c + 1)
                    g.tensor_tensor(parts[r][:, 2, :], rest[q], parts[r][:, 1, :], ALU.subtract).then_inc(s["parts_done"], 1)
                for q in range(4):
                    pool.wait_ge(s[f"xs_out{q}"], 192 * b + 192 + 16)
                hold(pool)
                leave(pool, "end_stats", b)
                pool.wait_ge(s["pe_out"], 16 * b + 16)
                hold(pool)
                pool.memset(Y[:, 2:2 + LOW, 0:1], 0.0)
                pool.memset(Y[:, 2:2 + LOW, LW - 1:LW], 0.0)
                pool.memset(Y[:, 1, :], 0.0)
                pool.memset(Y[:, YROWS - 1, :], 0.0)
                for q in range(2):
                    pool.memset(lines(keep[q], 0), 0.0).then_inc(s["pads_done"], 1)
                    pool.memset(lines(take[q], 0), 0.0).then_inc(s["pads_done"], 1)
                def silu(i):
                    for q in range(2):
                        pool.wait_ge(s["sig_done"], b * 32 + 2 * i + q + 1)
                        g.tensor_tensor(S[:, bass.ds(i * 1024 + q * 512, 512)], conv[q], sig[q], ALU.mult).then_inc(s["s_ready"], 1)

                def merge(i):
                    for q in range(2):
                        pool.wait_ge(s["scans_done"], ready(b * 64 + 2 * i + q))
                        g.tensor_tensor(Y[:, bass.ds(8 * i + 4 * q + 1, 4), 1:1 + LOW], lines(fsc[q], 1), lines(bsc[q], 1), ALU.add)\
                         .then_inc(s["merged"], 1)
                silu(0)
                with pool.Fori(1, 16) as i:
                    silu(i)
                    merge(i - 1)
                merge(15)
                yc = Y[:, 1:1 + LOW, :].rearrange("p r w -> p w r")
                with pool.Fori(0, 16) as i:
                    for q in range(2):
                        if q == 0:
                            pool.wait_ge(s["scans_done"], ready(b * 64 + 32 + 2 * i))
                            g.tensor_tensor(lines(fsc[0], 1), lines(fsc[0], 1), lines(bsc[0], 1), ALU.add).then_inc(s["pl_l1"], 1)
                            pool.wait_ge(s["pl_l1"], b * 16 + i + 1)
                        else:
                            pool.wait_ge(s["both_ways"], b * 16 + i + 1)
                        v = yc[:, bass.ds(8 * i + 4 * q + 1, 4), :]
                        g.tensor_tensor(v, v, lines(fsc[q], 1), ALU.add).then_inc(s["merged"], 1)
                with pool.Fori(0, 16) as i:
                    pool.wait_ge(s["gsig_done"], ready(b * 32 + 2 * i))
                    v = Y[:, bass.ds(8 * i + 1, 4), 1:1 + LOW]
                    g.tensor_tensor(v, v, gsig[0].rearrange("p (r w) -> p r w", w=LOW), ALU.mult).then_inc(s["gated0"], 1)
                leave(pool, "end_layer", b)
                leave(pool, "end_out", b)

        @block.vector
        def _(dve):
            v = nc.vector
            stt = v.scalar_tensor_tensor
            ts = v.tensor_scalar
            tt = v.tensor_tensor
            credit(dve, "pool_done", "pool_done", "y_ev", "g_st", "st_done", "st_done", "corr_add", "conv_done", "take_done", "scans_done", "gcorr_add", "up_ready")
            dve.sem_inc(s["added"], 4)
            dve.sem_inc(s["ew_done"], 1)
            dve.wait_ge(s["stores_set"], 1)
            st = Steps(dve, "ve_setup", 0)
            dve.wait_ge(s["consts_in"], 16 * 13)
            w32, r1 = S[0:GK, 768:784], S[0:GK, 816:832]
            st.done(v.tensor_copy(wgain[0], w32)); st.wait()
            st.done(tt(r1, w32, wgain[0], ALU.subtract)); st.wait()
            st.done(v.tensor_copy(wgain[1], r1)); st.wait()
            st.done(tt(r1, r1, wgain[1], ALU.subtract)); st.wait()
            st.done(v.tensor_copy(wgain[2], r1))
            st.done(v.memset(ones[:, :], 1.0))
            st.done(v.tensor_copy(S[:, 3328:3840].rearrange("p (t n) -> p t n", t=2), wpool[:, :, :]))
            st.wait()
            for h in range(2):
                ins = ts(wpool[:, h, :], wpool[:, h, :], gnw[:, h:h + 1], 0.25, ALU.mult, ALU.mult)
            st.done(ins)
            for w in range(2):
                v.tensor_scalar(nbd[w], bd[w], -1.0, None, ALU.mult)
            for k, tap in enumerate(TE_TAPS):
                ts(taps[:, k, :], S[:, 640:768], dw[:, tap:tap + 1], None, ALU.mult)
            ts(wup[:, :], wup[:, :], 1.0 / 64, None, ALU.mult)
            R = 6 * CM
            w32, p16, acc = S[0:R, 256:512], [S[0:R, 3840 + 128 * j:3968 + 128 * j].bitcast(BF16) for j in range(3)], S[0:R, 4224:4480]
            r1 = S[0:R, 4480:4736]
            st.done(v.tensor_copy(p16[0], w32)); st.wait()
            st.done(tt(r1, w32, p16[0], ALU.subtract)); st.wait()
            st.done(v.tensor_copy(p16[1], r1)); st.wait()
            st.done(tt(r1, r1, p16[1], ALU.subtract)); st.wait()
            st.done(v.tensor_copy(p16[2], r1)); st.wait()
            st.done(ts(acc, p16[0], cols[0:R, 4:5], None, ALU.mult)); st.wait()
            st.done(stt(acc, p16[1], cols[0:R, 5:6], acc, ALU.mult, ALU.add)); st.wait()
            st.done(stt(wstack[:, :], p16[2], cols[0:R, 6:7], acc, ALU.mult, ALU.add))
            dve.wait_ge(s["gain_t"], NSLOT // 16 + 1)
            dve.wait_ge(s["rowb_in"], 16)
            rowb = S[0:1, 1024:1024 + P * CM].rearrange("o (m l) -> o m l", l=P)
            st.done(tt(gains[0:1, :, P:2 * P], gains[0:1, :, P:2 * P], rowb, ALU.add)); st.wait()
            st.done(ts(gains[0:1, :, P:2 * P], gains[0:1, :, P:2 * P], 0.5, None, ALU.mult)); st.wait()
            for j, slot in enumerate((0, None, P, None)):
                if slot is None:
                    st.done(tt(corner[:, :, j], gains[:, :, GA1 + j // 2], gains[:, :, GA1B + j // 2], ALU.add)); st.wait()
                    st.done(ts(corner[:, :, j], corner[:, :, j], 0.25, 1.0, ALU.mult, ALU.add))
                elif slot == 0:
                    st.done(ts(corner[:, :, j], gains[:, :, 0], 0.5, 1.0, ALU.mult, ALU.add))
                else:
                    st.done(ts(corner[:, :, j], gains[:, :, P], 0.5, 1.0, ALU.mult, ALU.add))
            st.wait()
            st.done(ts(gains[:, :, 0:2 * P], gains[:, :, 0:2 * P], quart_h, half_h, ALU.mult, ALU.add))
            dve.wait_ge(s["te_setup"], 1)
            v.tensor_copy(vec[:, 19:23], bank[:, 2, 0:4])
            v.tensor_copy(wsum, bank[:, 3, 0:1])
            tt(gram[:, :], S[:, 512:640], bank[:, 4, 0:P], ALU.mult)
            for band in range(8):
                ts(cmix[:, band, :], bank[:, 5, 0:SIDE], cols[:, 16 + band:17 + band], None, ALU.mult)
            dve.drain().then_inc(s["mv_setup"], 1)

            with dve.Fori(0, B) as b:
                def pool(i, p):
                    n, q = b * 32 + 4 * i + p, p % 2
                    for e in range(2):
                        c = 2 * p + e
                        dve.wait_ge(s[f"x_in{c}"], x_loads(b, i))
                        xr = xslot[c].rearrange("p h (r a w) -> p (h r) a w", a=2, w=SIDE)
                        vr = vert[e].rearrange("p (r w) -> p r w", w=SIDE)
                        tt(vr, xr[:, :, 0, :], xr[:, :, 1, :], ALU.add).then_inc(s["ve_pool"], 1)
                        if e == 0:
                            dve.wait_ge(s["lowp_ps"], freed(n))
                        dve.wait_ge(s["ve_pool"], 2 * n + e + 1)
                        vp = vert[e].rearrange("p (h n a) -> p h n a", h=2, a=2)
                        stt(pooled[q][:, :, e * 256:(e + 1) * 256], vp[:, :, :, 0], 1.0, vp[:, :, :, 1], ALU.mult, ALU.add,
                            accum_out=sum_x[:, bass.ds(8 * i + c, 1)]).then_inc(s["pool_done"], 1)

                def copy_low(i, p):
                    n, q = b * 32 + 4 * i + p, p % 2
                    dve.wait_ge(s["lowp_ps"], ready(n))
                    v.tensor_copy(Y[:, bass.ds(16 * i + 4 * p + 2, 4), 1:1 + LOW],
                                  bank[:, 2 + q, :].rearrange("p (r w) -> p r w", w=LOW)).then_inc(s["y_ev"], 1)
                    dve.wait_ge(s[f"gate_out{q}"], 16 * (b * 16 + 2 * i + p // 2) + 16)
                    v.tensor_copy(gstage[q], bank[:, 4 + q, :]).then_inc(s["g_st"], 1)
                pool(0, 0)
                with dve.Fori(0, 7) as i:
                    for p in range(4):
                        pool(i + (p + 1) // 4, (p + 1) % 4)
                        copy_low(i, p)
                for p in range(4):
                    if p < 3:
                        pool(7, p + 1)
                    copy_low(7, p)
                leave(dve, "end_project", b)
                with dve.Fori(0, 2) as gp:
                    for gi in range(2):
                        grp = b * 4 + gp * 2 + gi
                        step = Steps(dve, "ve_ew", grp * EW)
                        dve.wait_ge(s["ew_done"], grp + 1)
                        dve.wait_ge(s["f_st"], ready(b * 16 + gp * 8 + 4 * gi + 3))
                        ch = bass.ds(8 * gp + 4 * gi, 4)
                        cc, cs, sc, ss = (freq[:, ch, k * P:(k + 1) * P] for k in range(4))
                        edge = freq.rearrange("p m (k l) -> p m k l", l=P)[:, ch, :, 0]
                        u, w_, p_, q_ = (tmp[k].rearrange("p (m l) -> p m l", m=4) for k in range(4))
                        z4, sq4, m4, sw4 = (small[k].rearrange("p (m k) -> p m k", m=4) for k in range(4))
                        hold(dve)
                        step.done(v.tensor_copy(z4, edge))
                        stt(u, ss, negk, cc, ALU.mult, ALU.add)
                        stt(w_, cc, kappa, ss, ALU.mult, ALU.add)
                        stt(p_, sc, kappa, cs, ALU.mult, ALU.add)
                        stt(q_, cs, negk, sc, ALU.mult, ALU.add).then_inc(s["uv_ready"], 1)
                        step.wait()
                        step.done(tt(sq4, z4, z4, ALU.mult))
                        step.wait()
                        v.tensor_copy(sw4[:, :, 0:2], sq4[:, :, 2:4])
                        step.done(v.tensor_copy(sw4[:, :, 2:4], sq4[:, :, 0:2]))
                        step.done(ts(small[2], small[1], TINY, None, ALU.max))
                        step.wait()
                        step.done(stt(small[2], small[3], kappa, small[2], ALU.mult, ALU.add))
                        step.wait()
                        step.done(ts(small[4], small[2], TINY, DELTA, ALU.is_le, ALU.mult))
                        dve.wait_ge(s["sq_ready"], grp + 1)
                        step.done(stt(tmp[4], tmp[4], TINY, tmp[6], ALU.max, ALU.add))
                        step.done(stt(tmp[5], tmp[5], TINY, tmp[7], ALU.max, ALU.add))
                        step.wait()
                        step.done(ts(tmp[6], tmp[4], TINY, DELTA, ALU.is_le, ALU.mult))
                        ts(tmp[7], tmp[5], TINY, DELTA, ALU.is_le, ALU.mult).then_inc(s["m_ready"], 1)
                        dve.wait_ge(s["m_ready"], grp + 1)
                        zmask = cols[:, 8:12]
                        for k in range(4):
                            ins = tt(small[5][:, 4 * k:4 * k + 4], small[4][:, 4 * k:4 * k + 4], zmask, ALU.mult)
                        step.done(ins)
                        step.done(tt(tmp[0], tmp[0], tmp[6], ALU.add))
                        step.done(stt(tmp[1], tmp[7], kappa, tmp[1], ALU.mult, ALU.add))
                        step.done(tt(tmp[3][0:1, :], tmp[3][0:1, :], tmp[7][0:1, :], ALU.add))
                        step.wait()
                        step.done(tt(small[0], small[0], small[5], ALU.add))
                        dve.wait_ge(s["root_ready"], grp + 1)
                        ts(tmp[4], tmp[4], FEPS, 1.0, ALU.mult, ALU.add)
                        ts(tmp[5], tmp[5], FEPS, 1.0, ALU.mult, ALU.add)
                        step.done(ts(small[2], small[2], FEPS, 1.0, ALU.mult, ALU.add))
                        step.wait()
                        gp4, gm4 = (tmp[4 + k].rearrange("p (m l) -> p m l", m=4) for k in range(2))
                        tt(gp4, gp4, gains[:, ch, 0:P], ALU.mult)
                        tt(gm4, gm4, gains[:, ch, P:2 * P], ALU.mult)
                        step.done(tt(m4, m4, corner[:, ch, :], ALU.mult))
                        step.wait()
                        tt(tmp[0], tmp[0], tmp[4], ALU.mult)
                        tt(tmp[2], tmp[2], tmp[4], ALU.mult)
                        tt(tmp[1], tmp[1], tmp[5], ALU.mult)
                        tt(tmp[3], tmp[3], tmp[5], ALU.mult)
                        step.done(tt(small[0], small[0], small[2], ALU.mult))
                        step.wait()
                        stt(cc, w_, kappa, u, ALU.mult, ALU.add)
                        stt(ss, u, negk, w_, ALU.mult, ALU.add)
                        stt(cs, q_, negk, p_, ALU.mult, ALU.add)
                        step.done(stt(sc, p_, kappa, q_, ALU.mult, ALU.add))
                        step.wait()
                        hold(dve)
                        v.tensor_copy(edge, z4).then_inc(s["ew_done"], 1)
                        assert step.n == EW
                leave(dve, "end_fourier", b)
                with dve.Fori(0, 2) as i:
                    for j in range(2):
                        base = (b * 4 + 2 * i + j) * 6
                        for q in range(2):
                            c = 2 * j + q
                            dve.wait_ge(s[f"st_in{c}"], 64 * b + 32 * i + 32)
                            dve.wait_ge(s["st_done"], b * 8 + 4 * i + c + 3)
                            xr = xe_t[c].rearrange("p (r a w) -> p r a w", a=2, w=SIDE)
                            tt(vsum[q].rearrange("p (r w) -> p r w", w=SIDE), xr[:, :, 0, :], xr[:, :, 1, :], ALU.add).then_inc(s["ve_stat"], 1)
                        for q in range(2):
                            c = 2 * j + q
                            dve.wait_ge(s["ve_stat"], base + q + 1)
                            vp = vsum[q].rearrange("p (n a) -> p n a", a=2)
                            stt(pe_t[:, bass.ds(i * 1024 + c * 256, 256)], vp[:, :, 0], 1.0, vp[:, :, 1], ALU.mult, ALU.add,
                                accum_out=sum_xe[:, bass.ds(4 * i + c, 1)]).then_inc(s["ve_stat"], 1)
                        for q in range(2):
                            c = 2 * j + q
                            dve.wait_ge(s["gram_ps"], b * 8 + 4 * i + c + 1)
                            stt(mix[q], xq_t[c], 2.0, bank[:, 2 * c:2 * c + 2, :].rearrange("p k n -> p (k n)"), ALU.mult, ALU.add)\
                                .then_inc(s["ve_stat"], 1)
                        for q in range(2):
                            c = 2 * j + q
                            dve.wait_ge(s["ve_stat"], base + 4 + q + 1)
                            stt(mix[q], mix[q], 1.0, xe_t[c], ALU.mult, ALU.mult, accum_out=cross[:, bass.ds(4 * i + c, 1)]).then_inc(s["st_done"], 1)
                dve.wait_ge(s["st_done"], 4 + b * 8 + 8)
                v.reduce_sum(stat[:, 0:1], sum_x, AX.X)
                v.reduce_sum(stat[:, 1:2], sum_xx, AX.X)
                v.reduce_sum(stat[:, 2:3], cross, AX.X)
                v.reduce_sum(stat[:, 3:4], sum_xe, AX.X)
                dve.drain()
                tt(stat[:, 1:2], stat[:, 1:2], stat[:, 2:3], ALU.add)
                stt(stat[:, 0:1], stat[:, 3:4], wsum, stat[:, 0:1], ALU.mult, ALU.add)
                dve.drain().then_inc(s["tot_in"], 1)
                dve.wait_ge(s["tot_ps"], b + 1)
                total = 1.0 / (SIDE * PIX)
                ts(stat[:, 2:4], bank[:, 4, 0:2], total, None, ALU.mult)
                dve.drain()
                tt(stat[:, 6:7], stat[:, 2:3], stat[:, 2:3], ALU.mult)
                dve.drain()
                tt(stat[:, 4:5], stat[:, 3:4], stat[:, 6:7], ALU.subtract)
                dve.drain()
                ts(stat[:, 4:5], stat[:, 4:5], 0.0, GN_EPS, ALU.max, ALU.add)
                dve.drain().then_inc(s["norm_set"], 1)
                dve.wait_ge(s["var_root"], b + 1)
                v.reciprocal(stat[:, 5:6], stat[:, 5:6])
                dve.drain()
                tt(stat[:, 6:7], stat[:, 5:6], stat[:, 5:6], ALU.mult)
                dve.drain()
                tt(stat[:, 6:7], stat[:, 6:7], stat[:, 4:5], ALU.mult)
                dve.drain()
                ts(stat[:, 6:7], stat[:, 6:7], -0.5, 1.5, ALU.mult, ALU.add)
                dve.drain()
                tt(rs, stat[:, 5:6], stat[:, 6:7], ALU.mult)
                dve.drain()
                stt(stat[:, 7:8], stat[:, 2:3], -1.0, rs, ALU.mult, ALU.mult)
                dve.drain()
                stt(cshift, cw, stat[:, 7:8], cb, ALU.mult, ALU.add)
                leave(dve, "end_stats", b)
                with dve.Fori(0, 16) as i:
                    for q in range(2):
                        n = b * 32 + 2 * i + q
                        dve.wait_ge(s["corr_ps"], ready(n))
                        yv = Y[:, bass.ds(8 * i + 4 * q + 2, 4), 1:1 + LOW]
                        tt(yv, yv, bank[:, 6 + q, :].rearrange("p (r w) -> p r w", w=LOW), ALU.add).then_inc(s["corr_add"], 1)

                def scans(w, q, n):
                    dve.wait_ge(s["gates_done"], ready(n))
                    tk = lines(take[q], 1)
                    stt(tk, bank[:, 4 + q, :].rearrange("p (r w) -> p r w", w=LOW), bv[w], tk, ALU.add, ALU.mult).then_inc(s["take_done"], 1)
                    dve.wait_ge(s["take_done"], ready(n))
                    dve.wait_ge(s["merged"], freed(n))
                    v.tensor_tensor_scan(out=fsc[q][:, 0:SCAN], data0=keep[q][:, 0:SCAN], data1=take[q][:, 0:SCAN],
                                         initial=0.0, op0=ALU.mult, op1=ALU.add)
                    v.tensor_tensor_scan(out=bsc[q][:, 1:SCAN + 1][:, ::-1], data0=keep[q][:, 1:SCAN + 1][:, ::-1],
                                         data1=take[q][:, 1:SCAN + 1][:, ::-1], initial=0.0, op0=ALU.mult, op1=ALU.add)\
                     .then_inc(s["scans_done"], 1)
                NV = 2 * (len(VE_TAPS) - 1)
                dve.wait_ge(s["pads_done"], 4 * b + 4)
                hold(dve)

                def convolve(i):
                    base = (b * 16 + i) * NV
                    for q in range(2):
                        dve.wait_ge(s["norm_done"], b * 33 + 2 * i + q + 2)
                        dve.wait_ge(s["conv_ps"], ready(b * 32 + 2 * i + q))
                        dve.wait_ge(s["s_ready"], freed(b * 32 + 2 * i + q))
                    for k, tap in enumerate(VE_TAPS):
                        for q in range(2):
                            if k:
                                dve.wait_ge(s["ve_l1"], base + 2 * (k - 1) + q + 1)
                            src = Y[:, bass.ds(8 * i + 4 * q + 1 + tap // 3, 4), tap % 3:tap % 3 + LOW]
                            acc = (conv[q] if k else bank[:, q, :]).rearrange("p (r w) -> p r w", w=LOW)
                            stt(conv[q].rearrange("p (r w) -> p r w", w=LOW), src, dw[:, tap:tap + 1], acc, ALU.mult, ALU.add)\
                                .then_inc(s["ve_l1" if k < len(VE_TAPS) - 1 else "conv_done"], 1)

                def row_scans(i):
                    for q in range(2):
                        scans(0, q, b * 64 + 2 * i + q)
                convolve(0)
                with dve.Fori(1, 16) as i:
                    convolve(i)
                    row_scans(i - 1)
                row_scans(15)
                with dve.Fori(0, 16) as i:
                    for q in range(2):
                        scans(1, q, b * 64 + 32 + 2 * i + q)
                    dve.wait_ge(s["scans_done"], ready(b * 64 + 32 + 2 * i + 1))
                    tt(lines(fsc[1], 1), lines(fsc[1], 1), lines(bsc[1], 1), ALU.add).then_inc(s["both_ways"], 1)
                def apply_gate(n):
                    dve.wait_ge(s["gsig_done"], ready(b * 32 + n))
                    yv = Y[:, 4 * n + 1:4 * n + 5, 1:1 + LOW]
                    tt(yv, yv, gsig[1].rearrange("p (r w) -> p r w", w=LOW), ALU.mult).then_inc(s["gated1"], 1)
                dve.wait_ge(s["merged"], ready(b * 64 + 63))
                for n in range(32):
                    if n % 4 == 0:
                        dve.wait_ge(s[f"gate_in{n // 4 % 2}"], 64 * b + 16 * (n // 8) + 16)
                    dve.wait_ge(s["gcorr_ps"], ready(b * 32 + n))
                    dve.wait_ge(s["gsig_done"], freed(b * 32 + n))
                    tt(gsum[n % 2], gload[n // 4 % 2][:, (n % 4) * 512:(n % 4 + 1) * 512], bank[:, 6 + n % 2, :], ALU.add).then_inc(s["gcorr_add"], 1)
                    if n % 2 and n >= 3:
                        apply_gate(n - 2)
                apply_gate(31)
                for q in range(2):
                    dve.wait_ge(s[f"gated{q}"], 16 * b + 16)
                hold(dve)
                v.tensor_copy(Y[:, 1:1 + LOW, 0:1], Y[:, 1:1 + LOW, 1:2])
                v.tensor_copy(Y[:, 1:1 + LOW, LW - 1:LW], Y[:, 1:1 + LOW, LW - 2:LW - 1]).then_inc(s["edge_done"], 1)
                dve.wait_ge(s["edge_done"], b + 1)
                v.tensor_copy(Y[:, 0, :], Y[:, 1, :])
                v.tensor_copy(Y[:, LOW + 1, :], Y[:, LOW, :])
                leave(dve, "end_layer", b)
                def interpolate(i, p):
                    n, q = b * 32 + 4 * i + p, p % 2
                    r0 = 16 * i + 4 * p + 1
                    mid, above, below = (Y[:, bass.ds(r0 + d, 4), :] for d in (0, -1, 1))
                    stt(vup[q][:, :, 0, :], mid, 3.0, above, ALU.mult, ALU.add)
                    stt(vup[q][:, :, 1, :], mid, 3.0, below, ALU.mult, ALU.add).then_inc(s["up_rows"], 1)
                    dve.wait_ge(s["up_rows"], n + 1)
                    dve.wait_ge(s["up_ps"], freed(n))
                    vv = vup[q].rearrange("p i a w -> p (i a) w")
                    uu = up[q].rearrange("p (r w a) -> p r w a", w=LOW, a=2)
                    stt(uu[:, :, :, 0], vv[:, :, 1:1 + LOW], 3.0, vv[:, :, 0:LOW], ALU.mult, ALU.add)
                    stt(uu[:, :, :, 1], vv[:, :, 1:1 + LOW], 3.0, vv[:, :, 2:2 + LOW], ALU.mult, ALU.add).then_inc(s["up_ready"], 1)

                def add_x(i, p):
                    n = b * 32 + 4 * i + p
                    for k in range(4):
                        e, h = k // 2, k % 2
                        if k < 3:
                            dve.wait_ge(s["ve_up"], 3 * n + k + 1)
                        else:
                            dve.wait_ge(s["up_ps"], ready(n))
                        if h == 0:
                            dve.wait_ge(s[f"x_in{2 * p + e}"], x_loads(b, 8 + i))
                        xv = xslot[2 * p + e][:, h, :]
                        tt(xv, xv, bank[:, 2 * k:2 * k + 2, :].rearrange("p k n -> p (k n)"), ALU.add).then_inc(s["added"], 1)
                interpolate(0, 0)
                with dve.Fori(0, 7) as i:
                    for p in range(4):
                        interpolate(i + (p + 1) // 4, (p + 1) % 4)
                        add_x(i, p)
                for p in range(4):
                    if p < 3:
                        interpolate(7, p + 1)
                    add_x(7, p)
                leave(dve, "end_out", b)


def kernel(**inputs):
    import numpy as _np
    import concourse.bacc as _bacc
    from concourse import mybir as _mybir
    from concourse.bass_utils import run_bass_kernel_spmd as _run

    a = {k: _np.asarray(v) for k, v in inputs.items()}
    x = a["x"]
    B = x.shape[0]
    w_in0, w_out0, wts = a["L0_conv_w_in"], a["L0_conv_w_out"], a["L0_conv_weights"]
    fwd, inv = fourier_bases()
    block = (_np.arange(P)[:, None] // CM == _np.arange(P)[None, :] // CM).astype(_np.float32)
    arrays = {
        "x": x.reshape(B, 256, PIX),
        "fwd": fwd, "inv": inv, "basis": gain_basis(), "cols": columns(), "block": block, "ident": _np.eye(P, dtype=_np.float32),
        "wproj": _np.concatenate([w_in0.T, w_out0], axis=1),
        "wtile": _np.tile(w_out0, (1, 8)),
        "wrep": _np.tile(w_out0.T, (6, 1)),
        "wgain": _np.tile(wts[:, :, R0:R0 + NR].reshape(CM, NA * NR).T, (3, 1)),
        "w_in1": a["L1_conv_w_in"].T,
        "wscan": _np.concatenate([a["L1_conv_row_wd"].T, a["L1_conv_row_wv"].T, a["L1_conv_col_wd"].T, a["L1_conv_col_wv"].T], axis=0),
        "w_out1": a["L1_conv_w_out"].T,
        "vec": _np.concatenate([a["L1_conv_gn_w"].reshape(2, P).T, a["L1_conv_gn_b"].reshape(2, P).T]
                               + [a[f"L1_conv_{n}"][:, None] for n in ("row_bd", "row_bv", "col_bd", "col_bv")]
                               + [a["L1_conv_row_bd"][:, None], a["L1_conv_col_bd"][:, None]]
                               + [a["L1_conv_w_dw"].reshape(P, 9)], axis=1),
    }
    nc = _bacc.Bacc("TRN2", target_bir_lowering=False, num_devices=1)
    feed, t = {}, {}
    for name, arr in arrays.items():
        arr = _np.ascontiguousarray(arr)
        feed[f"in_{name}"] = arr
        t[name] = nc.dram_tensor(f"in_{name}", arr.shape, _mybir.dt.from_np(arr.dtype), kind="ExternalInput").ap()
    out = nc.dram_tensor("out", [B, 256, PIX], F32, kind="ExternalOutput").ap()
    build(nc, B, t["x"], out, t)
    r = _run(nc, [feed], core_ids=[0])
    return r.results[0]["out"].reshape(B, 256, SIDE, SIDE)
```
